# Optimizing a Trainium2 kernel written in Bass

```python
import numpy as np
import jax
import jax.numpy as jnp

def _softmax(x, axis=-1):
    return jax.nn.softmax(x, axis=axis)

def _gelu(x):
    return jax.nn.gelu(x, approximate=True)

def _silu(x):
    return jax.nn.silu(x)

def _sigmoid(x):
    return jax.nn.sigmoid(x)

def _layernorm(x, axis=-1, eps=1e-05):
    m = jnp.mean(x, axis=axis, keepdims=True)
    v = jnp.var(x, axis=axis, keepdims=True)
    return (x - m) / jnp.sqrt(v + eps)

def _scatter_add(tgt, idx, src, axis=0):
    return tgt.at[idx].add(src)

def _segment_sum(src, seg, n):
    return jax.ops.segment_sum(src, seg, n)
kernel_name = 'mk_gnn_preln_d4_gnn_r8_034a32'

def setup_inputs(seed: int=0):
    np.random.seed(seed)
    _w = jnp.asarray

    def _rec_inputs():
        import jax
        import jax.numpy as jnp
        _gk = jax.random.key(seed)
        x = -0.0003713 + 1 * jax.random.normal(jax.random.fold_in(_gk, 1), (6250, 128), jnp.float32)
        src = jax.random.randint(jax.random.fold_in(_gk, 2), (100000,), 0, 6250, jnp.int32)
        dst = jax.random.randint(jax.random.fold_in(_gk, 3), (100000,), 0, 6250, jnp.int32)
        _o = jnp.argsort(dst, stable=True)
        src = src[_o]
        dst = dst[_o]
        edge_attr_64 = 0.000167468 + 1.0002 * jax.random.normal(jax.random.fold_in(_gk, 11), (100000, 64), jnp.float32)
        edge_weight = jax.random.uniform(jax.random.fold_in(_gk, 13), (100000,), jnp.float32, 0.0, 8)
        edge_weight1 = jax.random.uniform(jax.random.fold_in(_gk, 14), (100000, 1), jnp.float32, 0.0, 1)
        return (x, src, dst, edge_attr_64, edge_weight, edge_weight1)
    x, src, dst, edge_attr_64, edge_weight, edge_weight1 = _rec_inputs()

    def _L0_gnn_setup():
        import jax, jax.numpy as jnp
        import numpy as np
        N_NODES = 12500
        N_EDGES = 200000
        HIDDEN = 128
        N_FILTERS = 64
        CUTOFF = 8.0
        BN_EPS = 0.001
        key = jax.random.key(seed)
        ks = jax.random.split(key, 12)
        x = jax.random.normal(ks[0], (N_NODES, HIDDEN), dtype=jnp.float32)
        edge_index = jax.random.randint(ks[1], (2, N_EDGES), 0, N_NODES, dtype=jnp.int32)
        edge_weight = jax.random.uniform(ks[2], (N_EDGES,), dtype=jnp.float32) * CUTOFF
        edge_attr = jax.random.uniform(ks[3], (N_EDGES, 1), dtype=jnp.float32)
        s = 0.05
        Wf1 = jax.random.normal(ks[4], (1, N_FILTERS), dtype=jnp.float32) * s
        bf1 = jnp.zeros((N_FILTERS,), jnp.float32)
        Wf2 = jax.random.normal(ks[5], (N_FILTERS, N_FILTERS), dtype=jnp.float32) * s
        bf2 = jnp.zeros((N_FILTERS,), jnp.float32)
        Wi1 = jax.random.normal(ks[6], (HIDDEN, HIDDEN), dtype=jnp.float32) * s
        bi1 = jnp.zeros((HIDDEN,), jnp.float32)
        Wi2 = jax.random.normal(ks[7], (HIDDEN, HIDDEN), dtype=jnp.float32) * s
        bi2 = jnp.zeros((HIDDEN,), jnp.float32)
        gamma = jnp.ones((HIDDEN,), jnp.float32)
        beta = jnp.zeros((HIDDEN,), jnp.float32)
        mov_mean = jax.random.normal(ks[8], (HIDDEN,), dtype=jnp.float32) * 0.01
        mov_var = jnp.ones((HIDDEN,), jnp.float32)
        return {'x': x, 'edge_index': edge_index, 'edge_weight': edge_weight, 'edge_attr': edge_attr, 'Wf1': Wf1, 'bf1': bf1, 'Wf2': Wf2, 'bf2': bf2, 'Wi1': Wi1, 'bi1': bi1, 'Wi2': Wi2, 'bi2': bi2, 'gamma': gamma, 'beta': beta, 'mov_mean': mov_mean, 'mov_var': mov_var}
    _L0_gnn_all = _L0_gnn_setup()
    _L0_gnn_in = {k: v for k, v in _L0_gnn_all.items() if k in ('Wf1', 'bf1', 'Wf2', 'bf2', 'Wi1', 'bi1', 'Wi2', 'bi2', 'gamma', 'beta', 'mov_mean', 'mov_var')}
    del _L0_gnn_all

    def _L1_gnn_setup():
        import jax, jax.numpy as jnp
        import numpy as np
        N, E, D, L = (6250, 100000, 128, 2)
        NEG_SLOPE = 0.2
        LN_EPS = 1e-05
        key = jax.random.key(seed)
        ks = jax.random.split(key, 6)
        scale = 1.0 / np.sqrt(D)
        x = jax.random.normal(ks[0], (N, D), dtype=jnp.float32)
        edge_index = jax.random.randint(ks[1], (2, E), 0, N, dtype=jnp.int64)
        W = jax.random.normal(ks[2], (L, D, D), dtype=jnp.float32) * scale
        att_src = jax.random.normal(ks[3], (L, D), dtype=jnp.float32) * scale
        att_dst = jax.random.normal(ks[4], (L, D), dtype=jnp.float32) * scale
        bias = jnp.zeros((L, D), dtype=jnp.float32)
        gamma = jnp.ones((L, D), dtype=jnp.float32)
        beta = jnp.zeros((L, D), dtype=jnp.float32)
        return {'x': x, 'edge_index': edge_index, 'W': W, 'att_src': att_src, 'att_dst': att_dst, 'bias': bias, 'gamma': gamma, 'beta': beta}
    _L1_gnn_all = _L1_gnn_setup()
    _L1_gnn_in = {k: v for k, v in _L1_gnn_all.items() if k in ('W', 'att_src', 'att_dst', 'bias', 'gamma', 'beta')}
    del _L1_gnn_all

    def _L2_gnn_setup():
        import jax, jax.numpy as jnp
        import numpy as np
        N_NODES = 12500
        N_EDGES = 80000
        HID = 128
        EDGE_D = 64
        GLOB_D = 64
        LN_EPS = 1e-05

        def _linear(x, W, b):
            return x @ W.T + b
        key = jax.random.key(seed)
        ks = jax.random.split(key, 16)
        s = lambda d: 1.0 / np.sqrt(d)
        inp = {'node_state': jax.random.normal(ks[0], (N_NODES, HID), jnp.float32), 'edge_index': jax.random.randint(ks[1], (2, N_EDGES), 0, N_NODES, jnp.int64), 'edge_state': jax.random.normal(ks[2], (N_EDGES, EDGE_D), jnp.float32), 'global_state': jax.random.normal(ks[3], (GLOB_D,), jnp.float32), 'Wm1': jax.random.uniform(ks[4], (HID, HID + EDGE_D + GLOB_D), jnp.float32, -s(HID + EDGE_D + GLOB_D), s(HID + EDGE_D + GLOB_D)), 'bm1': jnp.zeros((HID,), jnp.float32), 'Wm2': jax.random.uniform(ks[5], (HID, HID), jnp.float32, -s(HID), s(HID)), 'bm2': jnp.zeros((HID,), jnp.float32), 'Wu1': jax.random.uniform(ks[6], (HID, HID + HID + GLOB_D), jnp.float32, -s(HID + HID + GLOB_D), s(HID + HID + GLOB_D)), 'bu1': jnp.zeros((HID,), jnp.float32), 'Wu2': jax.random.uniform(ks[7], (HID, HID), jnp.float32, -s(HID), s(HID)), 'bu2': jnp.zeros((HID,), jnp.float32), 'ln_g': jnp.ones((HID,), jnp.float32), 'ln_b': jnp.zeros((HID,), jnp.float32)}
        return inp
    _L2_gnn_all = _L2_gnn_setup()
    _L2_gnn_in = {k: v for k, v in _L2_gnn_all.items() if k in ('global_state', 'Wm1', 'bm1', 'Wm2', 'bm2', 'Wu1', 'bu1', 'Wu2', 'bu2', 'ln_g', 'ln_b')}
    del _L2_gnn_all

    def _L3_gnn_setup():
        import jax, jax.numpy as jnp
        import numpy as np
        N = 12500
        E = 400000
        IN = 128
        H = 8
        C = 16
        NEG_SLOPE = 0.2
        key = jax.random.key(seed)
        k1, k2, k3, k4, k5, k6 = jax.random.split(key, 6)
        x = jax.random.normal(k1, (N, IN), dtype=jnp.float32)
        edge_index = jax.random.randint(k2, (2, E), 0, N, dtype=jnp.int32)
        W = jax.random.normal(k3, (IN, H * C), dtype=jnp.float32) / np.float32(np.sqrt(IN))
        att_src = jax.random.normal(k4, (H, C), dtype=jnp.float32) / np.float32(np.sqrt(C))
        att_dst = jax.random.normal(k5, (H, C), dtype=jnp.float32) / np.float32(np.sqrt(C))
        bias = jax.random.normal(k6, (H * C,), dtype=jnp.float32) * 0.01
        return {'x': x, 'edge_index': edge_index, 'W': W, 'att_src': att_src, 'att_dst': att_dst, 'bias': bias}
    _L3_gnn_all = _L3_gnn_setup()
    _L3_gnn_in = {k: v for k, v in _L3_gnn_all.items() if k in ('W', 'att_src', 'att_dst', 'bias')}
    del _L3_gnn_all
    return {'x': x, 'src': src, 'dst': dst, 'edge_attr_64': edge_attr_64, 'edge_weight': edge_weight, 'edge_weight1': edge_weight1, 'L0_gnn_Wf1': _L0_gnn_in['Wf1'], 'L0_gnn_bf1': _L0_gnn_in['bf1'], 'L0_gnn_Wf2': _L0_gnn_in['Wf2'], 'L0_gnn_bf2': _L0_gnn_in['bf2'], 'L0_gnn_Wi1': _L0_gnn_in['Wi1'], 'L0_gnn_bi1': _L0_gnn_in['bi1'], 'L0_gnn_Wi2': _L0_gnn_in['Wi2'], 'L0_gnn_bi2': _L0_gnn_in['bi2'], 'L0_gnn_gamma': _L0_gnn_in['gamma'], 'L0_gnn_beta': _L0_gnn_in['beta'], 'L0_gnn_mov_mean': _L0_gnn_in['mov_mean'], 'L0_gnn_mov_var': _L0_gnn_in['mov_var'], 'L1_gnn_W': _L1_gnn_in['W'], 'L1_gnn_att_src': _L1_gnn_in['att_src'], 'L1_gnn_att_dst': _L1_gnn_in['att_dst'], 'L1_gnn_bias': _L1_gnn_in['bias'], 'L1_gnn_gamma': _L1_gnn_in['gamma'], 'L1_gnn_beta': _L1_gnn_in['beta'], 'L2_gnn_global_state': _L2_gnn_in['global_state'], 'L2_gnn_Wm1': _L2_gnn_in['Wm1'], 'L2_gnn_bm1': _L2_gnn_in['bm1'], 'L2_gnn_Wm2': _L2_gnn_in['Wm2'], 'L2_gnn_bm2': _L2_gnn_in['bm2'], 'L2_gnn_Wu1': _L2_gnn_in['Wu1'], 'L2_gnn_bu1': _L2_gnn_in['bu1'], 'L2_gnn_Wu2': _L2_gnn_in['Wu2'], 'L2_gnn_bu2': _L2_gnn_in['bu2'], 'L2_gnn_ln_g': _L2_gnn_in['ln_g'], 'L2_gnn_ln_b': _L2_gnn_in['ln_b'], 'L3_gnn_W': _L3_gnn_in['W'], 'L3_gnn_att_src': _L3_gnn_in['att_src'], 'L3_gnn_att_dst': _L3_gnn_in['att_dst'], 'L3_gnn_bias': _L3_gnn_in['bias']}

def reference(x, src, dst, edge_attr_64, edge_weight, edge_weight1, L0_gnn_Wf1, L0_gnn_bf1, L0_gnn_Wf2, L0_gnn_bf2, L0_gnn_Wi1, L0_gnn_bi1, L0_gnn_Wi2, L0_gnn_bi2, L0_gnn_gamma, L0_gnn_beta, L0_gnn_mov_mean, L0_gnn_mov_var, L1_gnn_W, L1_gnn_att_src, L1_gnn_att_dst, L1_gnn_bias, L1_gnn_gamma, L1_gnn_beta, L2_gnn_global_state, L2_gnn_Wm1, L2_gnn_bm1, L2_gnn_Wm2, L2_gnn_bm2, L2_gnn_Wu1, L2_gnn_bu1, L2_gnn_Wu2, L2_gnn_bu2, L2_gnn_ln_g, L2_gnn_ln_b, L3_gnn_W, L3_gnn_att_src, L3_gnn_att_dst, L3_gnn_bias):
    import jax
    import jax.numpy as jnp

    def _L0_gnn_ref(x, edge_index, edge_weight, edge_attr, Wf1, bf1, Wf2, bf2, Wi1, bi1, Wi2, bi2, gamma, beta, mov_mean, mov_var):
        import jax, jax.numpy as jnp
        import numpy as np
        N_NODES = 12500
        N_EDGES = 200000
        HIDDEN = 128
        N_FILTERS = 64
        CUTOFF = 8.0
        BN_EPS = 0.001
        row, col = (edge_index[0], edge_index[1])
        scaled = edge_weight * (2.0 / CUTOFF) - 1.0
        h = jnp.tanh(scaled[:, None] @ Wf1 + bf1)
        filters = h @ Wf2 + bf2
        cut = 0.5 * (jnp.cos(edge_weight * jnp.pi / CUTOFF) + 1.0)
        cut = jnp.where(edge_weight <= CUTOFF, cut, 0.0)
        filters = filters * cut[:, None]
        fsum = jnp.sum(filters, axis=-1, keepdims=True)
        messages = x[col] * fsum
        agg = jax.ops.segment_sum(messages, row, num_segments=x.shape[0])
        out = jax.nn.softplus(agg @ Wi1 + bi1) @ Wi2 + bi2
        out = gamma * (out - mov_mean) * jax.lax.rsqrt(mov_var + BN_EPS) + beta
        return out

    def _L1_gnn_ref(x, edge_index, W, att_src, att_dst, bias, gamma, beta):
        import jax, jax.numpy as jnp
        import numpy as np
        N, E, D, L = (6250, 100000, 128, 2)
        NEG_SLOPE = 0.2
        LN_EPS = 1e-05
        n = x.shape[0]
        loops = jnp.arange(n, dtype=edge_index.dtype)
        ei = jnp.concatenate([edge_index, jnp.stack([loops, loops])], axis=1)
        src, dst = (ei[0], ei[1])
        for l in range(W.shape[0]):
            h = x @ W[l]
            a_src = h @ att_src[l]
            a_dst = h @ att_dst[l]
            logit = jax.nn.leaky_relu(a_src[src] + a_dst[dst], NEG_SLOPE)
            m = jax.ops.segment_max(logit, dst, num_segments=n)
            e = jnp.exp(logit - m[dst])
            s = jax.ops.segment_sum(e, dst, num_segments=n)
            alpha = e / s[dst]
            msg = h[src] * alpha[:, None]
            x_att = jax.ops.segment_sum(msg, dst, num_segments=n) + bias[l]
            y = x + x_att
            mu = jnp.mean(y, axis=-1, keepdims=True)
            var = jnp.var(y, axis=-1, keepdims=True)
            x = (y - mu) * jax.lax.rsqrt(var + LN_EPS) * gamma[l] + beta[l]
        return x

    def _L2_gnn_ref(node_state, edge_index, edge_state, global_state, Wm1, bm1, Wm2, bm2, Wu1, bu1, Wu2, bu2, ln_g, ln_b):
        import jax, jax.numpy as jnp
        import numpy as np
        N_NODES = 12500
        N_EDGES = 80000
        HID = 128
        EDGE_D = 64
        GLOB_D = 64
        LN_EPS = 1e-05

        def _linear(x, W, b):
            return x @ W.T + b
        src, dst = (edge_index[0], edge_index[1])
        num_nodes = node_state.shape[0]
        num_edges = edge_state.shape[0]
        g_edges = jnp.broadcast_to(global_state[None, :], (num_edges, GLOB_D))
        msg_in = jnp.concatenate([node_state[src], edge_state, g_edges], axis=-1)
        messages = _linear(jax.nn.relu(_linear(msg_in, Wm1, bm1)), Wm2, bm2)
        aggregated = jax.ops.segment_sum(messages, dst, num_segments=num_nodes)
        degree = jax.ops.segment_sum(jnp.ones((num_edges,), node_state.dtype), dst, num_segments=num_nodes)
        aggregated = aggregated / jnp.maximum(degree, 1.0)[:, None]
        g_nodes = jnp.broadcast_to(global_state[None, :], (num_nodes, GLOB_D))
        upd_in = jnp.concatenate([node_state, aggregated, g_nodes], axis=-1)
        delta = _linear(jax.nn.relu(_linear(upd_in, Wu1, bu1)), Wu2, bu2)
        h = node_state + delta
        mu = jnp.mean(h, axis=-1, keepdims=True)
        var = jnp.mean(jnp.square(h - mu), axis=-1, keepdims=True)
        return (h - mu) * jax.lax.rsqrt(var + LN_EPS) * ln_g + ln_b

    def _L3_gnn_ref(x, edge_index, W, att_src, att_dst, bias):
        import jax, jax.numpy as jnp
        import numpy as np
        N = 12500
        E = 400000
        IN = 128
        H = 8
        C = 16
        NEG_SLOPE = 0.2
        n = x.shape[0]
        h = (x @ W).reshape(n, H, C)
        loop = jnp.arange(n, dtype=edge_index.dtype)
        src = jnp.concatenate([edge_index[0], loop])
        dst = jnp.concatenate([edge_index[1], loop])
        a_src = jnp.einsum('nhc,hc->nh', h, att_src)
        a_dst = jnp.einsum('nhc,hc->nh', h, att_dst)
        alpha = jax.nn.leaky_relu(a_src[src] + a_dst[dst], NEG_SLOPE)
        amax = jax.lax.stop_gradient(jax.ops.segment_max(alpha, dst, num_segments=n))
        ex = jnp.exp(alpha - amax[dst])
        denom = jax.ops.segment_sum(ex, dst, num_segments=n)
        w = ex / (denom[dst] + 1e-16)
        msg = h[src] * w[:, :, None]
        out = jax.ops.segment_sum(msg, dst, num_segments=n)
        return out.reshape(n, H * C) + bias
    edge_index = jnp.stack([src, dst])
    h = jnp.maximum(_layernorm(x, axis=-1), 0.0)
    x = x + _L0_gnn_ref(h, edge_index, edge_weight, edge_weight1, L0_gnn_Wf1, L0_gnn_bf1, L0_gnn_Wf2, L0_gnn_bf2, L0_gnn_Wi1, L0_gnn_bi1, L0_gnn_Wi2, L0_gnn_bi2, L0_gnn_gamma, L0_gnn_beta, L0_gnn_mov_mean, L0_gnn_mov_var)
    h = jnp.maximum(_layernorm(x, axis=-1), 0.0)
    x = x + _L1_gnn_ref(h, edge_index, L1_gnn_W, L1_gnn_att_src, L1_gnn_att_dst, L1_gnn_bias, L1_gnn_gamma, L1_gnn_beta)
    h = jnp.maximum(_layernorm(x, axis=-1), 0.0)
    x = x + _L2_gnn_ref(h, edge_index, edge_attr_64, L2_gnn_global_state, L2_gnn_Wm1, L2_gnn_bm1, L2_gnn_Wm2, L2_gnn_bm2, L2_gnn_Wu1, L2_gnn_bu1, L2_gnn_Wu2, L2_gnn_bu2, L2_gnn_ln_g, L2_gnn_ln_b)
    h = jnp.maximum(_layernorm(x, axis=-1), 0.0)
    x = x + _L3_gnn_ref(h, edge_index, L3_gnn_W, L3_gnn_att_src, L3_gnn_att_dst, L3_gnn_bias)
    return x

_drawn_inputs = setup_inputs


def setup_inputs(seed=0):
    import zlib

    import numpy as np

    out = dict(_drawn_inputs(seed))
    spreads = {'L0_gnn_bf1': (0.0, 0.1),
     'L0_gnn_bf2': (0.0, 0.1),
     'L0_gnn_bi1': (0.0, 0.1),
     'L0_gnn_bi2': (0.0, 0.1),
     'L0_gnn_gamma': (1.0, 0.2),
     'L0_gnn_beta': (0.0, 0.1),
     'L0_gnn_mov_var': (1.0, 0.2),
     'L1_gnn_bias': (0.0, 0.1),
     'L1_gnn_gamma': (1.0, 0.2),
     'L1_gnn_beta': (0.0, 0.1),
     'L2_gnn_bm1': (0.0, 2.0),
     'L2_gnn_bm2': (0.0, 2.0),
     'L2_gnn_bu1': (0.0, 1.118),
     'L2_gnn_bu2': (0.0, 0.374),
     'L2_gnn_ln_g': (1.0, 0.2),
     'L2_gnn_ln_b': (0.0, 0.1)}
    factors = {'edge_attr_64': 8.0,
     'L0_gnn_Wf1': 3.082,
     'L0_gnn_mov_mean': 6.001,
     'L1_gnn_att_dst': 20.063,
     'L2_gnn_Wm1': 5.091,
     'L2_gnn_Wm2': 4.212,
     'L3_gnn_att_dst': 131.228,
     'L3_gnn_bias': 8.0}
    for name, (base, spread) in spreads.items():
        noise = np.random.default_rng([zlib.crc32(name.encode()), seed]).standard_normal(out[name].shape)
        drawn = base * np.exp(spread * noise) if base else spread * noise
        out[name] = jnp.asarray(drawn.astype(out[name].dtype))
    for name, factor in factors.items():
        out[name] = (out[name] * factor).astype(out[name].dtype)
    return out
```

```python
from contextlib import ExitStack, contextmanager

import concourse.bass as bass
from concourse import mybir

F32 = mybir.dt.float32
I32 = mybir.dt.int32
ALU = mybir.AluOpType
ACT = mybir.ActivationFunctionType
AX = mybir.AxisListType

P = 128
N = 6250
E = 100000
D = 128
EA = 64
NF = 64
NODE_TILES = -(-N // P)
GN = 4
NG = -(-NODE_TILES // GN)
NBP = GN * NG
FULL = N // P
REST = N - FULL * P
EP, EC = 125, 800
G = 8
MAX_TILES = (E + NODE_TILES * (P - 1)) // P
NT = -(-MAX_TILES // (2 * G)) * 2 * G
ITERS = NT // (2 * G)
SLOTS = NT * P
SC = 16
RW = 72
R_DLOC, R_SRC, R_POS, R_W, R_SLOC = 64, 65, 66, 67, 68
MW = 132
SKIP = 1 << 20
LN_EPS = 1e-5
BN_EPS = 1e-3
CUTOFF = 8.0
SLOPE = 0.2
PI = 3.141592653589793


class Steps:

    def __init__(self, eng, sem, start=0):
        self.eng, self.sem, self.start, self.n = eng, sem, start, 0

    def then(self, ins):
        ins.then_inc(self.sem, 1)
        self.n += 1
        self.eng.wait_ge(self.sem, self.start + self.n)


def looped(eng, n, body):
    body(0, True)
    with eng.Fori(1, n) as i:
        body(i, False)


def gnn(nc, a, out, stop=4):
    ctx = ExitStack()
    names = [0]

    def sem(name):
        names[0] += 1
        return nc.alloc_semaphore(name=f"{name}_{names[0]}")

    @contextmanager
    def stage_of_work():
        before = nc.snapshot_sems()
        yield
        nc.clear_and_free_semaphores(nc.allocated_since(before))
        nc.all_engine_barrier()

    def dram(name, shape, dt=F32):
        return nc.dram_tensor(name, shape, dt, kind="Internal").ap()

    def sbuf(stack, name, shape, dt=F32):
        names[0] += 1
        return stack.enter_context(nc.sbuf_tensor(f"{name}_{names[0]}", shape, dt))

    rec_d = dram("edge_records", [SLOTS, RW])
    msg_d = dram("layer0_messages", [SLOTS, MW])
    tab_d = [dram(f"node_table{i}", [NBP * P, w]) for i, w in enumerate((D + 1, D + 1, D, D + 8))]

    with ctx:
        def sb(name, shape, dt=F32):
            return sbuf(ctx, name, shape, dt)

        bank = [ctx.enter_context(nc.psum_tensor(f"bank{i}", [P, 512], F32)) for i in range(8)]

        iota_row = sb("iota_row", [P, P])
        ident = sb("ident", [P, P])
        zero1 = sb("zero1", [P, 1])
        dloc = sb("dloc", [P, NT])
        src_ix = sb("src_ix", [P, NT], I32)
        tile_of_d = sb("tile_of_d", [1, NT], I32)
        tile_of_s = sb("tile_of_s", [1, NT], I32)
        X = sb("X", [P, NBP, D])
        ACC = sb("ACC", [P, NBP, D + 8])
        vec = {}
        for v in ("L0_gnn_bi2", "L0_gnn_gamma", "L0_gnn_beta", "L0_gnn_mov_mean", "L0_gnn_mov_var",
                  "L2_gnn_bm1", "L2_gnn_bm2", "L2_gnn_bu2", "L2_gnn_ln_g", "L2_gnn_ln_b", "L3_gnn_bias"):
            vec[v] = (sb(v, [P, D]), a[v])
        for v in ("L1_gnn_att_src", "L1_gnn_att_dst", "L1_gnn_bias", "L1_gnn_gamma", "L1_gnn_beta"):
            for l in range(2):
                vec[v, l] = (sb(f"{v}{l}", [P, D]), a[v][l, :])
        for v in ("L3_gnn_att_src", "L3_gnn_att_dst"):
            vec[v] = (sb(v, [P, D]), a[v].rearrange("h c -> (h c)"))
        mat = {"Wi1": (sb("Wi1", [P, D]), a["L0_gnn_Wi1"]), "Wi2": (sb("Wi2", [P, D]), a["L0_gnn_Wi2"]),
               "W1_0": (sb("W1_0", [P, D]), a["L1_gnn_W"][0]), "W1_1": (sb("W1_1", [P, D]), a["L1_gnn_W"][1]),
               "W3": (sb("W3", [P, D]), a["L3_gnn_W"])}
        bi1_col = sb("bi1_col", [P, 1])
        bu1_col = sb("bu1_col", [P, 1])
        gs_col = sb("gs_col", [64, 1])
        wmaT, wmbT, wmcT = sb("wmaT", [P, D]), sb("wmbT", [64, D]), sb("wmcT", [64, D])
        wm2T, wuaT, wubT, wucT = sb("wm2T", [P, D]), sb("wuaT", [P, D]), sb("wubT", [P, D]), sb("wucT", [64, D])
        wu2T = sb("wu2T", [P, D])
        cm_row = sb("cm_row", [P, D])
        cu_col = sb("cu_col", [P, 1])
        bn_scale = sb("bn_scale", [P, D])
        bn_shift = sb("bn_shift", [P, D])

        with ExitStack() as tmp:
            def tb(name, shape, dt=F32):
                return sbuf(tmp, name, shape, dt)

            tri = tb("tri", [P, P])
            ones = tb("ones", [P, P])
            iota_t = tb("iota_t", [1, NT])
            pad_rec = tb("pad_rec", [P, G * RW])
            pad_msg = tb("pad_msg", [P, G * MW])
            node = [tb("dst_i", [EP, EC], I32), tb("src_i", [EP, EC], I32)]
            key = [tb("key_d", [EP, EC]), tb("key_s", [EP, EC])]
            pos = [tb("pos_d", [EP, EC]), tb("pos_s", [EP, EC])]
            row = [tb("row_d", [EP, EC], I32), tb("row_s", [EP, EC], I32)]
            eq = [tb("eq_d", [EP, EC]), tb("eq_s", [EP, EC])]
            cum = [tb("cum_d", [EP, EC]), tb("cum_s", [EP, EC])]
            meta = tb("meta", [EP, EC, 5])
            meta_i = meta[:, :, :].bitcast(I32)
            count = [tb("count_d", [EP, NODE_TILES]), tb("count_s", [EP, NODE_TILES])]
            ntile = [tb("ntile_d", [P, NODE_TILES]), tb("ntile_s", [P, NODE_TILES])]
            ntile_i = [tb("ntile_di", [P, NODE_TILES], I32), tb("ntile_si", [P, NODE_TILES], I32)]
            upto = [tb("upto_d", [P, NODE_TILES]), tb("upto_s", [P, NODE_TILES])]
            off = [tb("off_d", [P, NODE_TILES]), tb("off_s", [P, NODE_TILES])]
            tile_f = [tb("tile_fd", [1, NT]), tb("tile_fs", [1, NT])]
            tile_i = [tile_of_d, tile_of_s]
            wt = tb("edge_w", [EP, EC])
            fsum = tb("fsum", [EP, EC])
            th = [tb("tanh0", [EP, EC]), tb("tanh1", [EP, EC])]
            wf1, bf1 = tb("wf1", [P, NF]), tb("bf1", [P, NF])
            fscale, fbias = tb("fscale", [P, NF]), tb("fbias", [P, NF])
            wf2, bf2 = tb("wf2", [P, NF, NF]), tb("bf2", [P, NF])
            wf2_sum, bf2_sum = tb("wf2_sum", [P, NF]), tb("bf2_sum", [P, 1])
            wm1, wm2, wu1, wu2 = tb("wm1", [P, 256]), tb("wm2", [P, D]), tb("wu1", [P, 320]), tb("wu2", [P, D])
            half_pi = tb("half_pi", [P, 1])
            gs_b = tb("gs_b", [64, D])

            with stage_of_work():
                consts, pads, edges_in, weights_in, filled, steps_v, steps_p = (
                    sem("consts"), sem("pads"), sem("edges_in"), sem("weights_in"), sem("filled"),
                    sem("steps_v"), sem("steps_p"))
                loop_a, loop_b, counts_ready, offs_in_psum = sem("loop_a"), sem("loop_b"), sem("counts_ready"), sem("offs_in_psum")
                filt_ready, tanh_ready, tanh_used, cos_ready = sem("filt_ready"), sem("tanh_ready"), sem("tanh_used"), sem("cos_ready")
                wT_ready, wT_copied, cvec_ready, steps_a = sem("wT_ready"), sem("wT_copied"), sem("cvec_ready"), sem("steps_a")
                x_zero, bnv, bns = sem("x_zero"), sem("bnv"), sem("bns")
                NW = len(vec) + len(mat) + 7
                with nc.Block() as block:
                    @block.sync
                    def _(sp):
                        sp.dma_start(node[0][:, :], a["dst"].rearrange("(p c) -> p c", c=EC)).then_inc(edges_in, 16)
                        sp.dma_start(node[1][:, :], a["src"].rearrange("(p c) -> p c", c=EC)).then_inc(edges_in, 16)
                        sp.dma_start(wt[:, :], a["edge_weight"].rearrange("(p c) -> p c", c=EC)).then_inc(edges_in, 16)
                        sp.dma_start(wf1[:, :], a["L0_gnn_Wf1"].to_broadcast([P, NF])).then_inc(edges_in, 16)
                        sp.dma_start(bf1[:, :], a["L0_gnn_bf1"].unsqueeze(0).to_broadcast([P, NF])).then_inc(edges_in, 16)
                        sp.dma_start(bf2[:, :], a["L0_gnn_bf2"].unsqueeze(0).to_broadcast([P, NF])).then_inc(edges_in, 16)
                        sp.dma_start(wf2[:, :, :], a["L0_gnn_Wf2"].unsqueeze(0).to_broadcast([P, NF, NF])).then_inc(edges_in, 16)
                        for t, v in vec.values():
                            sp.dma_start(t[:, :], v.unsqueeze(0).to_broadcast([P, D])).then_inc(weights_in, 16)
                        for t, v in mat.values():
                            sp.dma_start(t[:, :], v).then_inc(weights_in, 16)
                        for t, v in ((bi1_col, a["L0_gnn_bi1"]), (bu1_col, a["L2_gnn_bu1"]), (gs_col, a["L2_gnn_global_state"])):
                            sp.dma_start(t[:, :], v.rearrange("(p a) -> p a", a=1)).then_inc(weights_in, 16)
                        for t, v in ((wm1, "L2_gnn_Wm1"), (wm2, "L2_gnn_Wm2"), (wu1, "L2_gnn_Wu1"), (wu2, "L2_gnn_Wu2")):
                            sp.dma_start(t[:, :], a[v]).then_inc(weights_in, 16)
                        sp.wait_ge(x_zero, 1)
                        sp.dma_start(X[:, 0:FULL, :], a["x"][0:FULL * P, :].rearrange("(b p) f -> p b f", p=P)).then_inc(filled, 16)
                        sp.dma_start(X[0:REST, FULL, :], a["x"][FULL * P:N, :]).then_inc(filled, 16)
                        sp.wait_ge(pads, 1)
                        sp.dma_start(rec_d.rearrange("(k p j) w -> p k (j w)", p=P, j=G),
                                     pad_rec[:, :].unsqueeze(1).to_broadcast([P, NT // G, G * RW])).then_inc(filled, 16)
                        sp.dma_start(msg_d.rearrange("(k p j) w -> p k (j w)", p=P, j=G),
                                     pad_msg[:, :].unsqueeze(1).to_broadcast([P, NT // G, G * MW])).then_inc(filled, 16)
                        sp.wait_ge(filled, 64)

                    @block.gpsimd
                    def _(pool):
                        st = Steps(pool, steps_p)
                        st.then(pool.memset(ident[:, :], 0.0))
                        st.then(pool.affine_select(out=ident[:, :], in_=ident[:, :], compare_op=ALU.not_equal, fill=1.0,
                                                   base=0, pattern=[[-1, P]], channel_multiplier=1))
                        st.then(pool.memset(tri[:, :], 1.0))
                        st.then(pool.affine_select(out=tri[:, :], in_=tri[:, :], compare_op=ALU.is_gt, fill=0.0,
                                                   base=0, pattern=[[1, P]], channel_multiplier=-1))
                        st.then(pool.memset(ones[:, :], 1.0))
                        st.then(pool.iota(iota_row[:, :], [[1, P]], base=0, channel_multiplier=0,
                                          allow_small_or_imprecise_dtypes=True))
                        st.then(pool.iota(iota_t[:, :], [[1, NT]], base=0, channel_multiplier=0,
                                          allow_small_or_imprecise_dtypes=True))
                        st.then(pool.memset(zero1[:, :], 0.0))
                        pool.sem_inc(consts, 1)
                        pr = pad_rec[:, :].rearrange("p (j w) -> p j w", w=RW)
                        pm = pad_msg[:, :].rearrange("p (j w) -> p j w", w=MW)
                        st.then(pool.memset(pad_rec[:, :], 0.0))
                        st.then(pool.memset(pad_msg[:, :], 0.0))
                        st.then(pool.memset(pr[:, :, R_DLOC:R_DLOC + 1], -1.0))
                        st.then(pool.memset(pr[:, :, R_SLOC:R_SLOC + 1], -1.0))
                        st.then(pool.memset(pr[:, :, R_POS:R_POS + 1].bitcast(I32), SKIP))
                        st.then(pool.memset(pm[:, :, D:D + 1], -1.0))
                        pool.sem_inc(pads, 1)
                        st.then(pool.memset(X[:, :, :], 0.0))
                        pool.sem_inc(x_zero, 1)
                        st.then(pool.memset(ACC[:, :, :], 0.0))

                    @block.tensor
                    def _(pe):
                        pe.wait_ge(consts, 1)
                        pe.wait_ge(counts_ready, 1)
                        for q in range(2):
                            nc.tensor.matmul(bank[q][:, 0:NODE_TILES], tri[0:EP, :], count[q][:, :], start=True, stop=True)
                            nc.tensor.matmul(bank[2 + q][:, 0:NODE_TILES], ones[0:EP, :], count[q][:, :], start=True,
                                             stop=True).then_inc(offs_in_psum, 1)
                        pe.wait_ge(weights_in, 16 * NW)
                        for n, (w, lo, hi) in enumerate(((wm1, 0, 128), (wm1, 128, 192), (wm1, 192, 256), (wm2, 0, 128))):
                            nc.tensor.transpose(bank[4][0:hi - lo, n * P:n * P + P], w[:, lo:hi], ident[:, :]).then_inc(wT_ready, 1)
                        for n, (w, lo, hi) in enumerate(((wu1, 0, 128), (wu1, 128, 256), (wu1, 256, 320), (wu2, 0, 128))):
                            nc.tensor.transpose(bank[5][0:hi - lo, n * P:n * P + P], w[:, lo:hi], ident[:, :]).then_inc(wT_ready, 1)
                        pe.wait_ge(wT_copied, 1)
                        nc.tensor.matmul(bank[6][:, 0:P], gs_b[:, :], wmcT[:, :], start=True, stop=True)
                        nc.tensor.matmul(bank[7][:, 0:1], wucT[:, :], gs_col[:, :], start=True, stop=True).then_inc(cvec_ready, 1)

                    @block.scalar
                    def _(act):
                        st = Steps(act, steps_a)
                        act.wait_ge(filt_ready, 1)
                        for f in range(NF):
                            if f >= 2:
                                act.wait_ge(tanh_used, f - 1)
                            nc.scalar.activation(th[f % 2][:, :], wt[:, :], ACT.Tanh, bias=fbias[0:EP, f:f + 1],
                                                 scale=fscale[0:EP, f:f + 1]).then_inc(tanh_ready, 1)
                        act.wait_ge(tanh_used, NF)
                        act.wait_ge(cos_ready, 1)
                        st.then(nc.scalar.activation(th[0][:, :], th[1][:, :], ACT.Sin, bias=half_pi[0:EP, :],
                                                     scale=-PI / CUTOFF))
                        act.sem_inc(cos_ready, 1)
                        act.wait_ge(wT_ready, 8)
                        for n, (t, r) in enumerate(((wmaT, P), (wmbT, 64), (wmcT, 64), (wm2T, P))):
                            st.then(nc.scalar.copy(t[:, :], bank[4][0:r, n * P:n * P + P]))
                        for n, (t, r) in enumerate(((wuaT, P), (wubT, P), (wucT, 64), (wu2T, P))):
                            st.then(nc.scalar.copy(t[:, :], bank[5][0:r, n * P:n * P + P]))
                        st.then(nc.scalar.copy(gs_b[:, :], gs_col[:, 0:1].to_broadcast([64, D])))
                        act.sem_inc(wT_copied, 1)
                        act.wait_ge(bnv, 1)
                        st.then(nc.scalar.activation(bn_scale[:, :], bn_scale[:, :], ACT.Sqrt, bias=zero1[:, :]))
                        act.sem_inc(bns, 1)

                    @block.vector
                    def _(dve):
                        v = nc.vector
                        st = Steps(dve, steps_v)
                        dve.wait_ge(edges_in, 16 * 7)
                        dve.wait_ge(consts, 1)
                        st.then(v.tensor_scalar(fscale[:, :], wf1[:, :], 2.0 / CUTOFF, None, ALU.mult))
                        st.then(v.tensor_tensor(fbias[:, :], bf1[:, :], wf1[:, :], ALU.subtract))
                        st.then(v.tensor_reduce(wf2_sum[:, :], wf2[:, :, :], AX.X, ALU.add))
                        st.then(v.tensor_reduce(bf2_sum[:, :], bf2[:, :], AX.X, ALU.add))
                        st.then(v.memset(half_pi[:, :], PI / 2))
                        dve.sem_inc(filt_ready, 1)
                        for q in range(2):
                            st.then(v.tensor_single_scalar(row[q][:, :], node[q][:, :], 7, ALU.logical_shift_right))
                            st.then(v.tensor_copy(key[q][:, :], row[q][:, :]))
                            st.then(v.tensor_single_scalar(row[q][:, :], node[q][:, :], P - 1, ALU.bitwise_and))
                            st.then(v.tensor_copy(meta[:, :, 4 * q:4 * q + 1], row[q][:, :].unsqueeze(2)))
                            st.then(v.memset(pos[q][:, :], 0.0))
                            st.then(v.memset(tile_f[q][:, :], 0.0))
                        st.then(v.tensor_copy(meta_i[:, :, 1:2], node[1][:, :].unsqueeze(2)))
                        with dve.Fori(0, NODE_TILES) as b:
                            ls = Steps(dve, loop_a, b * 4)
                            for q in range(2):
                                ls.then(v.tensor_scalar(eq[q][:, :], key[q][:, :], iota_row[0:EP, bass.ds(b, 1)], None,
                                                        ALU.is_equal))
                                ls.then(v.tensor_reduce(count[q][:, bass.ds(b, 1)], eq[q][:, :], AX.X, ALU.add))
                        dve.sem_inc(counts_ready, 1)
                        dve.wait_ge(offs_in_psum, 2)
                        for q in range(2):
                            st.then(v.tensor_scalar(ntile_i[q][:, :], bank[2 + q][:, 0:NODE_TILES], float(P - 1), None, ALU.add))
                            st.then(v.tensor_single_scalar(ntile_i[q][:, :], ntile_i[q][:, :], 7, ALU.logical_shift_right))
                            st.then(v.tensor_copy(ntile[q][:, :], ntile_i[q][:, :]))
                            st.then(v.tensor_tensor_scan(upto[q][:, :], ntile[q][:, :], ntile[q][:, :], 0.0, ALU.add, ALU.bypass))
                            st.then(v.tensor_tensor(ntile[q][:, :], upto[q][:, :], ntile[q][:, :], ALU.subtract))
                            st.then(v.tensor_scalar(ntile[q][:, :], ntile[q][:, :], float(P), -1.0, ALU.mult, ALU.add))
                            st.then(v.tensor_tensor(off[q][:, :], ntile[q][:, :], bank[q][:, 0:NODE_TILES], ALU.add))
                        with dve.Fori(0, NODE_TILES) as b:
                            ls = Steps(dve, loop_b, b * 10)
                            for q in range(2):
                                col = iota_row[0:EP, bass.ds(b, 1)]
                                ls.then(v.tensor_scalar(eq[q][:, :], key[q][:, :], col, None, ALU.is_equal))
                                ls.then(v.tensor_tensor_scan(cum[q][:, :], eq[q][:, :], eq[q][:, :], off[q][0:EP, bass.ds(b, 1)],
                                                             ALU.add, ALU.bypass))
                                ls.then(v.tensor_tensor(cum[q][:, :], cum[q][:, :], eq[q][:, :], ALU.mult))
                                ls.then(v.tensor_tensor(pos[q][:, :], pos[q][:, :], cum[q][:, :], ALU.add))
                                ls.then(v.scalar_tensor_tensor(tile_f[q][:, :], iota_t[:, :], upto[q][0:1, bass.ds(b, 1)],
                                                               tile_f[q][:, :], ALU.is_ge, ALU.add))
                        for q in range(2):
                            st.then(v.tensor_scalar(tile_i[q][:, :], tile_f[q][:, :], float(NODE_TILES - 1), None, ALU.min))
                            ci, ei = cum[q][:, :].bitcast(I32), eq[q][:, :].bitcast(I32)
                            st.then(v.tensor_copy(ci, pos[q][:, :]))
                            st.then(v.tensor_scalar(row[q][:, :], ci, -P * G, None, ALU.bitwise_and))
                            st.then(v.tensor_scalar(ei, ci, P - 1, 3, ALU.bitwise_and, ALU.logical_shift_left))
                            st.then(v.tensor_tensor(row[q][:, :], row[q][:, :], ei, ALU.bitwise_or))
                            st.then(v.tensor_scalar(ei, ci, 7, G - 1, ALU.logical_shift_right, ALU.bitwise_and))
                            st.then(v.tensor_tensor(row[q][:, :], row[q][:, :], ei, ALU.bitwise_or))
                        st.then(v.tensor_copy(meta_i[:, :, 2:3], row[1][:, :].unsqueeze(2)))
                        for f in range(NF):
                            dve.wait_ge(tanh_ready, f + 1)
                            if f == 0:
                                v.tensor_scalar(fsum[:, :], th[0][:, :], wf2_sum[0:EP, 0:1], bf2_sum[0:EP, 0:1],
                                                ALU.mult, ALU.add).then_inc(tanh_used, 1)
                            else:
                                dve.wait_ge(tanh_used, f)
                                v.scalar_tensor_tensor(fsum[:, :], th[f % 2][:, :], wf2_sum[0:EP, f:f + 1], fsum[:, :],
                                                       ALU.mult, ALU.add).then_inc(tanh_used, 1)
                        dve.wait_ge(tanh_used, NF)
                        st.then(v.tensor_scalar(th[1][:, :], wt[:, :], CUTOFF, None, ALU.min))
                        dve.sem_inc(cos_ready, 1)
                        dve.wait_ge(cos_ready, 2)
                        st.then(v.tensor_scalar(th[0][:, :], th[0][:, :], 0.5, 0.5, ALU.mult, ALU.add))
                        st.then(v.scalar_tensor_tensor(th[1][:, :], wt[:, :], CUTOFF, th[0][:, :], ALU.is_le, ALU.mult))
                        st.then(v.tensor_tensor(meta[:, :, 3:4], fsum[:, :].unsqueeze(2), th[1][:, :].unsqueeze(2), ALU.mult))
                        dve.wait_ge(weights_in, 16 * NW)
                        st.then(v.tensor_scalar(bn_scale[:, :], vec["L0_gnn_mov_var"][0][:, :], BN_EPS, None, ALU.add))
                        dve.sem_inc(bnv, 1)
                        dve.wait_ge(bns, 1)
                        st.then(v.reciprocal(bn_scale[:, :], bn_scale[:, :]))
                        st.then(v.tensor_tensor(bn_scale[:, :], bn_scale[:, :], vec["L0_gnn_gamma"][0][:, :], ALU.mult))
                        st.then(v.tensor_tensor(bn_shift[:, :], vec["L0_gnn_bi2"][0][:, :], vec["L0_gnn_mov_mean"][0][:, :], ALU.subtract))
                        st.then(v.tensor_tensor(bn_shift[:, :], bn_shift[:, :], bn_scale[:, :], ALU.mult))
                        st.then(v.tensor_tensor(bn_shift[:, :], bn_shift[:, :], vec["L0_gnn_beta"][0][:, :], ALU.add))
                        dve.wait_ge(cvec_ready, 1)
                        st.then(v.tensor_tensor(cm_row[:, :], bank[6][:, 0:P], vec["L2_gnn_bm1"][0][:, :], ALU.add))
                        st.then(v.tensor_tensor(cu_col[:, :], bank[7][:, 0:1], bu1_col[:, :], ALU.add))

            rec = [tb(f"rec_out{h}", [EP, SC, RW]) for h in range(2)]
            ixs = [tb(f"ixs_out{h}", [EP, SC], I32) for h in range(2)]
            with stage_of_work():
                attr_in = [sem("attr_in0"), sem("attr_in1")]
                meta_in = [sem("meta_in0"), sem("meta_in1")]
                scattered = [sem("scattered0"), sem("scattered1")]
                tick, cleared = sem("tick"), sem("cleared")
                attr_v = a["edge_attr_64"].rearrange("(p c) w -> p c w", c=EC)
                with nc.Block() as block:
                    @block.sync
                    def _(sp):
                        def body(i, first):
                            for h in range(2):
                                if first:
                                    sp.wait_ge(cleared, h + 1)
                                else:
                                    sp.wait_ge(scattered[h], i * (16 * SC))
                                sp.dma_start(rec[h][:, :, 0:EA],
                                             attr_v[:, bass.ds((2 * i + h) * SC, SC), :]).then_inc(attr_in[h], 16)
                        looped(sp, EC // (2 * SC), body)

                    @block.vector
                    def _(dve):
                        def body(i, first):
                            for h in range(2):
                                if first:
                                    nc.vector.memset(rec[h][:, :, EA:RW], 0.0).then_inc(cleared, 1)
                                    dve.wait_ge(cleared, h + 1)
                                else:
                                    dve.wait_ge(scattered[h], i * (16 * SC))
                                nc.vector.tensor_copy(rec[h][:, :, EA:EA + 5], meta[:, bass.ds((2 * i + h) * SC, SC), :]) \
                                    .then_inc(meta_in[h], 1)
                                nc.vector.tensor_copy(ixs[h][:, :], row[0][:, bass.ds((2 * i + h) * SC, SC)]) \
                                    .then_inc(meta_in[h], 1)
                        looped(dve, EC // (2 * SC), body)

                    @block.gpsimd
                    def _(pool):
                        with pool.Fori(0, EC // (2 * SC)) as i:
                            for h in range(2):
                                pool.wait_ge(attr_in[h], i * 16 + 16)
                                pool.sem_inc(tick, 1)
                                pool.wait_ge(meta_in[h], i * 2 + 2)
                                pool.sem_inc(tick, 1)
                                for j in range(SC):
                                    pool.indirect_dma_start(rec_d, bass.IndirectOffsetOnAxis(ap=ixs[h][:, j:j + 1], axis=0),
                                                            rec[h][:, j, :], None).then_inc(scattered[h], 16)
                        for h in range(2):
                            pool.wait_ge(scattered[h], 16 * SC * (EC // (2 * SC)))

        H = sb("H", [P, NBP, D])
        Y = sb("Y", [P, NBP, D])

        def per_tile(t, w=D):
            return t.unsqueeze(2).to_broadcast([P, NBP, w])

        def per_col(t):
            return t[:, :].unsqueeze(1).to_broadcast([P, NBP, D])

        mean, var = sb("mean", [P, NBP]), sb("var", [P, NBP])

        class Dense:

            def __init__(self, work):
                self.jobs = []
                steps, asked, done = sem("dense_steps"), sem("dense_asked"), sem("dense_done")
                with nc.Block() as block:
                    @block.vector
                    def _(dve):
                        self.dve, self.st, self.asked, self.done = dve, Steps(dve, steps), asked, done
                        work(self, nc.vector, self.st.then)

                    @block.scalar
                    def _(act):
                        for n, (o, i, f) in enumerate(self.jobs):
                            act.wait_ge(asked, n + 1)
                            nc.scalar.activation(o, i, f, bias=zero1[0:P, :]).then_inc(done, 1)

            def act(self, o, i, f):
                self.jobs.append((o, i, f))
                self.dve.sem_inc(self.asked, 1)
                self.dve.wait_ge(self.done, len(self.jobs))

            def norm(self, v, then, o, i):
                then(v.tensor_reduce(mean[:, :], i, AX.X, ALU.add))
                then(v.tensor_scalar(mean[:, :], mean[:, :], 1.0 / D, None, ALU.mult))
                then(v.tensor_tensor(o, i, per_tile(mean[:, :]), ALU.subtract))
                sq = ACC[:, :, 0:D]
                then(v.tensor_tensor(sq, o, o, ALU.mult))
                then(v.tensor_reduce(var[:, :], sq, AX.X, ALU.add))
                then(v.tensor_scalar(var[:, :], var[:, :], 1.0 / D, LN_EPS, ALU.mult, ALU.add))
                self.act(var[:, :], var[:, :], ACT.Sqrt)
                then(v.reciprocal(var[:, :], var[:, :]))
                then(v.tensor_tensor(o, o, per_tile(var[:, :]), ALU.mult))

        stage = [sb("stage0", [P, GN, D]), sb("stage1", [P, GN, D])]
        stT = [sb("stT0", [P, GN * P]), sb("stT1", [P, GN * P])]
        hid = sb("hid", [P, GN * P])
        tmp_e = sb("tmp_e", [P, GN * P])

        def node_product(dst, srcs, ws, w2=None, hidden=None, bias=None):
            k = len(srcs)
            staged, turned, turned_sb, in_hid, hid_ready, prod, steps, hsteps = (
                sem("staged"), sem("turned"), sem("turned_sb"), sem("in_hid"), sem("hid_ready"), sem("prod"),
                sem("np_steps"), sem("np_hsteps"))
            with nc.Block() as block:
                @block.vector
                def _(dve):
                    with dve.Fori(0, NG) as g:
                        for n, s in enumerate(srcs):
                            nc.vector.tensor_copy(stage[n][:, :, :], s[:, bass.ds(g * GN, GN), 0:D]).then_inc(staged, 1)
                        if w2 is not None and hidden == "softplus":
                            dve.wait_ge(in_hid, g * 3 + 1)
                            nc.vector.tensor_scalar(hid[:, :], bank[2][:, :], bias[:, 0:1], None, ALU.add).then_inc(steps, 1)
                            dve.wait_ge(steps, g * 4 + 1)
                            nc.vector.tensor_scalar(tmp_e[:, :], hid[:, :], -1.0, None, ALU.mult).then_inc(steps, 1)
                            dve.wait_ge(steps, g * 4 + 2)
                            nc.vector.tensor_tensor(tmp_e[:, :], tmp_e[:, :], hid[:, :], ALU.min).then_inc(steps, 1)
                            dve.wait_ge(steps, g * 4 + 3)
                            dve.sem_inc(in_hid, 1)
                            dve.wait_ge(in_hid, g * 3 + 3)
                            nc.vector.scalar_tensor_tensor(hid[:, :], hid[:, :], 0.0, tmp_e[:, :], ALU.max, ALU.add) \
                                .then_inc(steps, 1)
                            dve.wait_ge(steps, g * 4 + 4)
                            dve.sem_inc(hid_ready, 1)
                        dve.wait_ge(prod, g + 1)
                        nc.vector.tensor_copy(dst[:, bass.ds(g * GN, GN), 0:D],
                                              bank[3][:, :].rearrange("p (j f) -> p j f", f=D)).then_inc(hsteps, 1)
                        dve.wait_ge(hsteps, g + 1)

                @block.tensor
                def _(pe):
                    with pe.Fori(0, NG) as g:
                        for n in range(k):
                            pe.wait_ge(staged, g * k + n + 1)
                            for j in range(GN):
                                ins = nc.tensor.transpose(bank[n][:, j * P:j * P + P], stage[n][:, j, :], ident[:, :])
                            ins.then_inc(turned, 1)
                        pe.wait_ge(turned_sb, g * k + k)
                        if w2 is None:
                            for j in range(GN):
                                for n in range(k):
                                    ins = nc.tensor.matmul(bank[3][:, j * P:j * P + P], stT[n][:, j * P:j * P + P],
                                                           ws[n][:, :], start=(n == 0), stop=(n == k - 1))
                        else:
                            for n in range(k):
                                ins = nc.tensor.matmul(bank[2][:, :], ws[n][:, :], stT[n][:, :], start=(n == 0), stop=(n == k - 1))
                            ins.then_inc(in_hid, 1)
                            pe.wait_ge(hid_ready, g + 1)
                            for j in range(GN):
                                ins = nc.tensor.matmul(bank[3][:, j * P:j * P + P], hid[:, j * P:j * P + P], w2[:, :],
                                                       start=True, stop=True)
                        ins.then_inc(prod, 1)

                @block.scalar
                def _(act):
                    with act.Fori(0, NG) as g:
                        for n in range(k):
                            act.wait_ge(turned, g * k + n + 1)
                            nc.scalar.copy(stT[n][:, :], bank[n][:, :]).then_inc(turned_sb, 1)
                        if w2 is not None and hidden == "relu":
                            act.wait_ge(in_hid, g + 1)
                            nc.scalar.activation(hid[:, :], bank[2][:, :], ACT.Relu, bias=bias[:, 0:1]).then_inc(hid_ready, 1)
                        if w2 is not None and hidden == "softplus":
                            act.wait_ge(in_hid, g * 3 + 2)
                            nc.scalar.activation(tmp_e[:, :], tmp_e[:, :], ACT.Exp, bias=zero1[:, :]).then_inc(turned_sp, 1)
                            act.wait_ge(turned_sp, g + 1)
                            nc.scalar.activation(tmp_e[:, :], tmp_e[:, :], ACT.Ln, bias=one1[:, :]).then_inc(in_hid, 1)

        one1 = sb("one1", [P, 1])
        turned_sp = sem("exp_done")

        Yflat = Y[:, :, :].rearrange("p b f -> p (b f)")
        oh = [Yflat[:, h * G * P:(h + 1) * G * P].rearrange("p (j n) -> p j n", j=G) for h in range(2)]
        ohT = [Yflat[:, (2 + h) * G * P:(3 + h) * G * P] for h in range(2)]
        rows = [sb(f"rows{h}", [P, G, D + 8]) for h in range(2)]
        recs = [sb(f"recs{h}", [P, G, RW]) for h in range(2)]
        ixr = [sb(f"ixr{h}", [P, G], I32) for h in range(2)]
        z = [sb(f"z{h}", [P, G, 8]) for h in range(2)]
        adc = sb("adc", [P, NBP * 16])

        def onehot(dve, h, loc):
            return nc.vector.tensor_tensor(oh[h][:, :, :], iota_row[:, :].unsqueeze(1).to_broadcast([P, G, P]),
                                           loc.to_broadcast([P, G, P]), ALU.is_equal)

        def sum_slot(j):
            return bank[4 + j // 3][:, (j % 3) * 136:(j % 3) * 136 + 136]

        def add_sums(dve, i, h, tiles, w, summed, added):
            for j in range(G):
                t = i * 2 * G + h * G + j
                b = dve.value_load(tiles[0:1, bass.ds(t, 1)], min_val=0, max_val=NODE_TILES - 1)
                if j == 0:
                    dve.wait_ge(summed, i * 2 + h + 1)
                acc = ACC[:, bass.ds(b, 1), 0:w]
                nc.vector.tensor_tensor(acc, acc, sum_slot(j)[:, 0:w].unsqueeze(1), ALU.add).then_inc(added, 1)
                dve.wait_ge(added, t + 1)

        def turn_onehot(pe, i, h, first, oh_ready, turned, ohT_ready):
            pe.wait_ge(oh_ready[h], i + 1)
            if not (first and h == 0):
                pe.wait_ge(ohT_ready, i * 4 + 2 * h)
            for j in range(G):
                ins = nc.tensor.transpose(bank[j // 4][:, (j % 4) * P:(j % 4) * P + P], oh[h][:, j, :], ident[:, :])
                if j % 4 == 3:
                    ins.then_inc(turned, 1)

        def copy_turned(act, i, h, first, turned, ohT_ready, ohT_used):
            if not first:
                act.wait_ge(ohT_used[h], i)
            for n in range(2):
                act.wait_ge(turned, i * 4 + 2 * h + n + 1)
                nc.scalar.copy(ohT[h][:, n * 512:n * 512 + 512], bank[n][:, :]).then_inc(ohT_ready, 1)

        def layer0_dst_pass():
            rec_in, oh_ready, ohT_used, scaled, sent = ([sem(f"{n}{h}") for h in range(2)] for n in
                                                        ("rec_in", "oh_ready", "ohT_used", "scaled", "sent"))
            turned, ohT_ready, picked, tick, psum_free = sem("turned"), sem("ohT_ready"), sem("picked"), sem("tick"), sem("psum_free")
            rec_v = rec_d.rearrange("(k p j) w -> k p (j w)", p=P, j=G)
            with nc.Block() as block:
                @block.sync
                def _(sp):
                    def body(i, first):
                        for h in range(2):
                            if not first:
                                sp.wait_ge(sent[h], i * (16 * G))
                            sp.dma_start(recs[h][:, :, :].rearrange("p j w -> p (j w)"),
                                         rec_v[bass.ds(2 * i + h, 1)].rearrange("k p w -> (k p) w")).then_inc(rec_in[h], 16)
                    looped(sp, ITERS, body)

                @block.vector
                def _(dve):
                    def body(i, first):
                        for h in range(2):
                            dve.wait_ge(rec_in[h], i * 16 + 16)
                            t = i * 2 * G + h * G
                            nc.vector.tensor_copy(dloc[:, bass.ds(t, G)].unsqueeze(2), recs[h][:, :, R_DLOC:R_DLOC + 1])
                            nc.vector.tensor_copy(src_ix[:, bass.ds(t, G)].unsqueeze(2),
                                                  recs[h][:, :, R_SRC:R_SRC + 1].bitcast(I32))
                            if not first:
                                dve.wait_ge(ohT_used[h], i)
                            onehot(dve, h, recs[h][:, :, R_DLOC:R_DLOC + 1]).then_inc(oh_ready[h], 1)
                            if not first:
                                dve.wait_ge(sent[h], i * (16 * G))
                            nc.vector.tensor_copy(rows[h][:, :, D:D + 1], recs[h][:, :, R_SLOC:R_SLOC + 1]).then_inc(scaled[h], 1)
                            for n in range(2):
                                dve.wait_ge(picked, i * 4 + 2 * h + n + 1)
                                nc.vector.tensor_tensor(rows[h][:, 4 * n:4 * n + 4, 0:D],
                                                        bank[2 + n][:, :].rearrange("p (j f) -> p j f", f=D),
                                                        recs[h][:, 4 * n:4 * n + 4, R_W:R_W + 1].to_broadcast([P, 4, D]),
                                                        ALU.mult).then_inc(scaled[h], 1)
                            dve.wait_ge(scaled[h], i * 3 + 3)
                            dve.sem_inc(psum_free, 1)
                    for h in range(2):
                        nc.vector.memset(rows[h][:, :, D:D + 8], 0.0).then_inc(tick, 1)
                    dve.wait_ge(tick, 2)
                    looped(dve, ITERS, body)

                @block.tensor
                def _(pe):
                    def body(i, first):
                        for h in range(2):
                            turn_onehot(pe, i, h, first, oh_ready, turned, ohT_ready)
                            if not (first and h == 0):
                                pe.wait_ge(psum_free, i * 2 + h)
                            for j in range(G):
                                b = pe.value_load(tile_of_d[0:1, bass.ds(i * 2 * G + h * G + j, 1)], min_val=0,
                                                  max_val=NODE_TILES - 1)
                                if j % 4 == 0:
                                    pe.wait_ge(ohT_ready, i * 4 + 2 * h + j // 4 + 1)
                                ins = nc.tensor.matmul(bank[2 + j // 4][:, (j % 4) * P:(j % 4) * P + P],
                                                       ohT[h][:, j * P:j * P + P], Hflat[:, bass.ds(b * D, D)],
                                                       start=True, stop=True)
                                if j % 4 == 3:
                                    ins.then_inc(picked, 1)
                            pe.wait_ge(picked, i * 4 + 2 * h + 2)
                            pe.sem_inc(ohT_used[h], 1)
                    looped(pe, ITERS, body)

                @block.scalar
                def _(act):
                    looped(act, ITERS, lambda i, first: [copy_turned(act, i, h, first, turned, ohT_ready, ohT_used)
                                                         for h in range(2)])

                @block.gpsimd
                def _(pool):
                    with pool.Fori(0, ITERS) as i:
                        for h in range(2):
                            pool.wait_ge(scaled[h], i * 3 + 3)
                            pool.sem_inc(poolt, 1)
                            for j in range(G):
                                pool.indirect_dma_start(
                                    msg_d, bass.IndirectOffsetOnAxis(ap=recs[h][:, j, R_POS:R_POS + 1].bitcast(I32), axis=0),
                                    rows[h][:, j, 0:MW], None, bounds_check=SLOTS - 1, oob_is_err=False).then_inc(sent[h], 16)
                    for h in range(2):
                        pool.wait_ge(sent[h], 16 * G * ITERS)

        poolt = sem("pool_tick")
        Hflat = H[:, :, :].rearrange("p b f -> p (b f)")

        def layer0_src_pass():
            msg_in, oh_ready, used = ([sem(f"{n}{h}") for h in range(2)] for n in ("msg_in", "oh_ready", "used"))
            summed, added = sem("summed"), sem("added")
            msg_v = msg_d.rearrange("(k p j) w -> k p (j w)", p=P, j=G)
            with nc.Block() as block:
                @block.sync
                def _(sp):
                    def body(i, first):
                        for h in range(2):
                            if not first:
                                sp.wait_ge(used[h], i)
                            sp.dma_start(rows[h][:, :, :].rearrange("p j w -> p (j w)")[:, 0:G * MW],
                                         msg_v[bass.ds(2 * i + h, 1)].rearrange("k p w -> (k p) w")).then_inc(msg_in[h], 16)
                    looped(sp, ITERS, body)

                msgs = [rows[h][:, :, :].rearrange("p j w -> p (j w)")[:, 0:G * MW].rearrange("p (j w) -> p j w", w=MW)
                        for h in range(2)]

                @block.vector
                def _(dve):
                    def body(i, first):
                        for h in range(2):
                            dve.wait_ge(msg_in[h], i * 16 + 16)
                            if not first:
                                dve.wait_ge(used[h], i)
                            onehot(dve, h, msgs[h][:, :, D:D + 1]).then_inc(oh_ready[h], 1)
                            add_sums(dve, i, h, tile_of_s, D, summed, added)
                    looped(dve, ITERS, body)

                @block.tensor
                def _(pe):
                    def body(i, first):
                        for h in range(2):
                            pe.wait_ge(oh_ready[h], i + 1)
                            if not (first and h == 0):
                                pe.wait_ge(added, i * 2 * G + h * G)
                            for j in range(G):
                                ins = nc.tensor.matmul(sum_slot(j)[:, 0:D], oh[h][:, j, :], msgs[h][:, j, 0:D],
                                                       start=True, stop=True)
                            ins.then_inc(summed, 1)
                            pe.wait_ge(summed, i * 2 + h + 1)
                            pe.sem_inc(used[h], 1)
                    looped(pe, ITERS, body)

        def gather_rows(pool, i, h, first, table, w, used, ix_ready, rows_in):
            if not first:
                pool.wait_ge(used[h], i)
                pool.sem_inc(poolt, 1)
            nc.gpsimd.tensor_copy(ixr[h][:, :], src_ix[:, bass.ds(i * 2 * G + h * G, G)]).then_inc(ix_ready, 1)
            pool.wait_ge(ix_ready, i * 2 + h + 1)
            pool.sem_inc(poolt, 1)
            for j in range(G):
                pool.indirect_dma_start(rows[h][:, j, 0:w], None, table,
                                        bass.IndirectOffsetOnAxis(ap=ixr[h][:, j:j + 1], axis=0)).then_inc(rows_in[h], 16)

        def gat_pass(table, heads):
            w, c = D + heads, D // heads
            rows_in, oh_ready, ohT_used, used, msg_ready = ([sem(f"{n}{h}") for h in range(2)] for n in
                                                            ("rows_in", "oh_ready", "ohT_used", "used", "msg_ready"))
            ix_ready, turned, ohT_ready, picked, logits, probs, zst, summed, added = (
                sem(n) for n in ("ix_ready", "turned", "ohT_ready", "picked", "logits", "probs", "zst", "summed", "added"))
            with nc.Block() as block:
                @block.gpsimd
                def _(pool):
                    looped(pool, ITERS, lambda i, first: [gather_rows(pool, i, h, first, table, w, used, ix_ready, rows_in)
                                                          for h in range(2)])

                @block.vector
                def _(dve):
                    def body(i, first):
                        for h in range(2):
                            t = i * 2 * G + h * G
                            if not first:
                                dve.wait_ge(used[h], i)
                            onehot(dve, h, dloc[:, bass.ds(t, G)].unsqueeze(2)).then_inc(oh_ready[h], 1)
                            dve.wait_ge(rows_in[h], i * (16 * G) + 16 * G)
                            dve.wait_ge(picked, i * 2 + h + 1)
                            zz = z[h][:, :, 0:heads]
                            ps = bank[2 + h][:, 0:G * 2 * heads].rearrange("p (j k) -> p j k", j=G)
                            st = Steps(dve, zst, i * 6 + h * 3)
                            st.then(nc.vector.tensor_tensor(zz, rows[h][:, :, D:w], ps[:, :, 0:heads], ALU.add))
                            st.then(nc.vector.scalar_tensor_tensor(zz, zz, SLOPE, zz, ALU.mult, ALU.max))
                            st.then(nc.vector.tensor_tensor(zz, zz, ps[:, :, heads:2 * heads], ALU.subtract))
                            nc.vector.tensor_scalar(zz, zz, 0.0, None, ALU.min).then_inc(logits, 1)
                            dve.wait_ge(probs, i * 2 + h + 1)
                            hv = rows[h][:, :, 0:D].rearrange("p j (k c) -> p j k c", c=c)
                            nc.vector.tensor_tensor(hv, hv, rows[h][:, :, D:w].unsqueeze(3).to_broadcast([P, G, heads, c]),
                                                    ALU.mult).then_inc(msg_ready[h], 1)
                            add_sums(dve, i, h, tile_of_d, w, summed, added)
                    looped(dve, ITERS, body)

                @block.scalar
                def _(act):
                    def body(i, first):
                        for h in range(2):
                            copy_turned(act, i, h, first, turned, ohT_ready, ohT_used)
                            act.wait_ge(logits, i * 2 + h + 1)
                            nc.scalar.activation(rows[h][:, :, D:w], z[h][:, :, 0:heads], ACT.Exp, bias=zero1[:, :]) \
                                .then_inc(probs, 1)
                    looped(act, ITERS, body)

                @block.tensor
                def _(pe):
                    def body(i, first):
                        for h in range(2):
                            turn_onehot(pe, i, h, first, oh_ready, turned, ohT_ready)
                            if not first:
                                pe.wait_ge(msg_ready[h], i)
                            for j in range(G):
                                b = pe.value_load(tile_of_d[0:1, bass.ds(i * 2 * G + h * G + j, 1)], min_val=0,
                                                  max_val=NODE_TILES - 1)
                                if j % 4 == 0:
                                    pe.wait_ge(ohT_ready, i * 4 + 2 * h + j // 4 + 1)
                                ins = nc.tensor.matmul(bank[2 + h][:, j * 2 * heads:(j + 1) * 2 * heads],
                                                       ohT[h][:, j * P:j * P + P], adc[:, bass.ds(b * (2 * heads), 2 * heads)],
                                                       start=True, stop=True)
                            ins.then_inc(picked, 1)
                            pe.wait_ge(picked, i * 2 + h + 1)
                            pe.sem_inc(ohT_used[h], 1)
                            pe.wait_ge(msg_ready[h], i + 1)
                            if not (first and h == 0):
                                pe.wait_ge(added, i * 2 * G + h * G)
                            for j in range(G):
                                ins = nc.tensor.matmul(sum_slot(j)[:, 0:w], oh[h][:, j, :], rows[h][:, j, 0:w],
                                                       start=True, stop=True)
                            ins.then_inc(summed, 1)
                            pe.wait_ge(summed, i * 2 + h + 1)
                            pe.sem_inc(used[h], 1)
                    looped(pe, ITERS, body)

        def mlp_pass(table):
            w = D + 1
            rec_in, rows_in, oh_ready, used, ones_in, hid_ready = ([sem(f"{n}{h}") for h in range(2)] for n in
                                                          ("rec_in", "rows_in", "oh_ready", "used", "ones_in", "hid_ready"))
            pe_tick = sem("pe_tick")
            ix_ready, turned, at_ready, prod, added_rows, summed, added = (
                sem(n) for n in ("ix_ready", "turned", "at_ready", "prod", "added_rows", "summed", "added"))
            rec_v = rec_d.rearrange("(k p j) w -> k p (j w)", p=P, j=G)
            with nc.Block() as block:
                @block.gpsimd
                def _(pool):
                    looped(pool, ITERS, lambda i, first: [gather_rows(pool, i, h, first, table, D, used, ix_ready, rows_in)
                                                          for h in range(2)])

                @block.sync
                def _(sp):
                    def body(i, first):
                        for h in range(2):
                            if not first:
                                sp.wait_ge(used[h], i)
                            sp.dma_start(recs[h][:, :, :].rearrange("p j w -> p (j w)"),
                                         rec_v[bass.ds(2 * i + h, 1)].rearrange("k p w -> (k p) w")).then_inc(rec_in[h], 16)
                    looped(sp, ITERS, body)

                @block.vector
                def _(dve):
                    def body(i, first):
                        for h in range(2):
                            t = i * 2 * G + h * G
                            if not first:
                                dve.wait_ge(used[h], i)
                            onehot(dve, h, dloc[:, bass.ds(t, G)].unsqueeze(2)).then_inc(oh_ready[h], 1)
                            dve.wait_ge(rows_in[h], i * (16 * G) + 16 * G)
                            for n in range(2):
                                dve.wait_ge(prod, i * 4 + 2 * h + n + 1)
                                hv = rows[h][:, 4 * n:4 * n + 4, 0:D]
                                nc.vector.tensor_tensor(hv, hv, bank[2 + n][:, :].rearrange("p (j f) -> p j f", f=D),
                                                        ALU.add).then_inc(added_rows, 1)
                            add_sums(dve, i, h, tile_of_d, w, summed, added)
                    for h in range(2):
                        nc.vector.memset(rows[h][:, :, D:D + 8], 1.0).then_inc(ones_in[h], 1)
                        dve.wait_ge(ones_in[h], 1)
                    looped(dve, ITERS, body)

                @block.scalar
                def _(act):
                    def body(i, first):
                        for h in range(2):
                            if not (first and h == 0):
                                act.wait_ge(prod, i * 4 + 2 * h)
                            for n in range(2):
                                act.wait_ge(turned, i * 4 + 2 * h + n + 1)
                                nc.scalar.copy(ohT[0][0:EA, n * 512:n * 512 + 512], bank[n][0:EA, :]).then_inc(at_ready, 1)
                            act.wait_ge(added_rows, i * 4 + 2 * h + 2)
                            nc.scalar.activation(rows[h][:, :, 0:D], rows[h][:, :, 0:D], ACT.Relu, bias=zero1[:, :]) \
                                .then_inc(hid_ready[h], 1)
                    looped(act, ITERS, body)

                @block.tensor
                def _(pe):
                    for h in range(2):
                        pe.wait_ge(ones_in[h], 1)

                    def body(i, first):
                        for h in range(2):
                            pe.wait_ge(rec_in[h], i * 16 + 16)
                            if not (first and h == 0):
                                pe.wait_ge(at_ready, i * 4 + 2 * h)
                            pe.sem_inc(pe_tick, 1)
                            for j in range(G):
                                ins = nc.tensor.transpose(bank[j // 4][0:EA, (j % 4) * P:(j % 4) * P + P],
                                                          recs[h][:, j, 0:EA], ident[:, :])
                                if j % 4 == 3:
                                    ins.then_inc(turned, 1)
                            for j in range(G):
                                if j % 4 == 0:
                                    pe.wait_ge(at_ready, i * 4 + 2 * h + j // 4 + 1)
                                ins = nc.tensor.matmul(bank[2 + j // 4][:, (j % 4) * P:(j % 4) * P + P],
                                                       ohT[0][0:EA, j * P:j * P + P], wmbT[:, :], start=True, stop=True)
                                if j % 4 == 3:
                                    ins.then_inc(prod, 1)
                            pe.wait_ge(oh_ready[h], i + 1)
                            pe.wait_ge(hid_ready[h], i + 1)
                            if not (first and h == 0):
                                pe.wait_ge(added, i * 2 * G + h * G)
                            for j in range(G):
                                ins = nc.tensor.matmul(sum_slot(j)[:, 0:w], oh[h][:, j, :], rows[h][:, j, 0:w],
                                                       start=True, stop=True)
                            ins.then_inc(summed, 1)
                            pe.wait_ge(summed, i * 2 + h + 1)
                            pe.sem_inc(used[h], 1)
                    looped(pe, ITERS, body)

        def store_table(table, src, w):
            stored = sem("stored")
            with nc.Block() as block:
                @block.sync
                def _(sp):
                    sp.dma_start(table.rearrange("(b p) w -> p b w", p=P), src[:, :, 0:w]).then_inc(stored, 16)
                    sp.wait_ge(stored, 16)

        small = {n: sb(n, [P, NBP, 8]) for n in ("a_src", "a_dst", "p_self")}
        gmax, gmax_all = sb("gmax", [P, 8]), sb("gmax_all", [P, 8])

        def gat_prepare(att_s, att_d, heads, table):
            c = D // heads
            a_s, a_d, p_s = (small[n][:, :, 0:heads] for n in ("a_src", "a_dst", "p_self"))
            H4 = H[:, :, :].rearrange("p b (k c) -> p (b k) c", c=c)
            Y4 = Y[:, :, :].rearrange("p b (k c) -> p (b k) c", c=c)
            flat = {n: sb_small(n, heads) for n in ("a_src", "a_dst")}

            def work(d, v, then):
                for name, att in (("a_src", att_s), ("a_dst", att_d)):
                    then(v.tensor_tensor(Y[:, :, :], H[:, :, :], per_col(att), ALU.mult))
                    then(v.tensor_reduce(flat[name], Y4, AX.X, ALU.add))
                then(v.tensor_copy(ACC[:, :, 0:D], H[:, :, :]))
                then(v.tensor_copy(ACC[:, :, D:D + heads], flat3("a_src", heads)))
                then(v.tensor_reduce(gmax[:, 0:heads], flat3("a_src", heads).rearrange("p b k -> p k b"), AX.X, ALU.max))
            Dense(work)
            store_table(table, ACC, D + heads)
            reduced = sem("reduced")
            with nc.Block() as block:
                @block.gpsimd
                def _(pool):
                    pool.partition_all_reduce(gmax_all[:, 0:heads], gmax[:, 0:heads], P, bass.bass_isa.ReduceOp.max) \
                        .then_inc(reduced, 1)
                    pool.wait_ge(reduced, 1)
            as3, ad3, ps3 = flat3("a_src", heads), flat3("a_dst", heads), flat3("p_self", heads)
            adc3 = adc[:, 0:NBP * 2 * heads].rearrange("p (b k) -> p b k", k=2 * heads)
            bound = adc3[:, :, heads:2 * heads]

            def work2(d, v, then):
                then(v.tensor_copy(adc3[:, :, 0:heads], ad3))
                then(v.tensor_tensor(bound, ad3, gmax_all[:, 0:heads].unsqueeze(1).to_broadcast([P, NBP, heads]), ALU.add))
                then(v.scalar_tensor_tensor(bound, bound, SLOPE, bound, ALU.mult, ALU.max))
                then(v.tensor_tensor(ps3, as3, ad3, ALU.add))
                then(v.scalar_tensor_tensor(ps3, ps3, SLOPE, ps3, ALU.mult, ALU.max))
                then(v.tensor_tensor(ps3, ps3, bound, ALU.subtract))
                d.act(ps3, ps3, ACT.Exp)
                A4 = ACC[:, :, 0:D].rearrange("p b (k c) -> p b k c", c=c)
                then(v.tensor_tensor(A4, H[:, :, :].rearrange("p b (k c) -> p b k c", c=c),
                                     ps3.unsqueeze(3).to_broadcast([P, NBP, heads, c]), ALU.mult))
                then(v.tensor_copy(ACC[:, :, D:D + heads], ps3))
            Dense(work2)

        def sb_small(n, heads):
            return small[n][:, :, :].rearrange("p b k -> p (b k)")[:, 0:NBP * heads]

        def flat3(n, heads):
            return sb_small(n, heads).rearrange("p (b k) -> p b k", k=heads)

        def gat_finish(v, then, heads, bias, o):
            c = D // heads
            then(v.tensor_copy(flat3("p_self", heads), ACC[:, :, D:D + heads]))
            if heads == 8:
                then(v.tensor_scalar(flat3("p_self", heads), flat3("p_self", heads), 1e-16, None, ALU.add))
            then(v.reciprocal(flat3("p_self", heads), flat3("p_self", heads)))
            then(v.tensor_tensor(o.rearrange("p b (k c) -> p b k c", c=c), ACC[:, :, 0:D].rearrange("p b (k c) -> p b k c", c=c),
                                 flat3("p_self", heads).unsqueeze(3).to_broadcast([P, NBP, heads, c]), ALU.mult))
            then(v.tensor_tensor(o, o, per_col(bias), ALU.add))

        def relu(v, then, t):
            then(v.tensor_scalar(t, t, 0.0, None, ALU.max))

        Xa, Ha, Ya = X[:, :, :], H[:, :, :], Y[:, :, :]
        XI = sb("XI", [P, NBP, D])
        XIa = XI[:, :, :]

        def start0(d, v, then):
            then(v.memset(one1[:, :], 1.0))
            d.norm(v, then, Ha, Xa)
            relu(v, then, Ha)
            then(v.memset(ACC[:, :, :], 0.0))
        with stage_of_work():
            Dense(start0)
            layer0_dst_pass()
            layer0_src_pass()
            node_product(Y, [ACC], [mat["Wi1"][0]], mat["Wi2"][0], "softplus", bi1_col)

            def end0(d, v, then):
                then(v.tensor_tensor(Ya, Ya, per_col(bn_scale), ALU.mult))
                then(v.tensor_tensor(Ya, Ya, per_col(bn_shift), ALU.add))
                then(v.tensor_tensor(Xa, Xa, Ya, ALU.add))
                if stop > 0:
                    d.norm(v, then, XIa, Xa)
                    relu(v, then, XIa)
            Dense(end0)

        if stop > 0:
            for l in range(2):
                with stage_of_work():
                    node_product(H, [XI], [mat[f"W1_{l}"][0]])
                    gat_prepare(vec["L1_gnn_att_src", l][0], vec["L1_gnn_att_dst", l][0], 1, tab_d[l])
                    gat_pass(tab_d[l], 1)

                    def end1(d, v, then):
                        gat_finish(v, then, 1, vec["L1_gnn_bias", l][0], Ya)
                        then(v.tensor_tensor(Ya, Ya, XIa, ALU.add))
                        d.norm(v, then, XIa, Ya)
                        then(v.tensor_tensor(XIa, XIa, per_col(vec["L1_gnn_gamma", l][0]), ALU.mult))
                        then(v.tensor_tensor(XIa, XIa, per_col(vec["L1_gnn_beta", l][0]), ALU.add))
                        if l == 1:
                            then(v.tensor_tensor(Xa, Xa, XIa, ALU.add))
                            d.norm(v, then, XIa, Xa)
                            relu(v, then, XIa)
                    Dense(end1)

        if stop > 1:
            with stage_of_work():
                node_product(H, [XI], [wmaT])

                def start2(d, v, then):
                    then(v.tensor_tensor(Ha, Ha, per_col(cm_row), ALU.add))
                    then(v.memset(ACC[:, :, :], 0.0))
                Dense(start2)
                store_table(tab_d[2], H, D)
                mlp_pass(tab_d[2])

                def mean2(d, v, then):
                    deg = ACC[:, :, D:D + 1]
                    then(v.tensor_scalar(mean[:, :].unsqueeze(2), deg, 1.0, None, ALU.max))
                    then(v.reciprocal(mean[:, :], mean[:, :]))
                    then(v.tensor_tensor(ACC[:, :, 0:D], ACC[:, :, 0:D], per_tile(mean[:, :]), ALU.mult))
                    then(v.tensor_tensor(var[:, :].unsqueeze(2), deg, mean[:, :].unsqueeze(2), ALU.mult))
                Dense(mean2)
                node_product(Y, [ACC], [wm2T])

                def bias2(d, v, then):
                    then(v.tensor_tensor(Ha, per_col(vec["L2_gnn_bm2"][0]), per_tile(var[:, :]), ALU.mult))
                    then(v.tensor_tensor(Ya, Ya, Ha, ALU.add))
                Dense(bias2)
                node_product(H, [XI, Y], [wuaT, wubT], wu2T, "relu", cu_col)

                def end2(d, v, then):
                    then(v.tensor_tensor(Ha, Ha, per_col(vec["L2_gnn_bu2"][0]), ALU.add))
                    then(v.tensor_tensor(Ha, Ha, XIa, ALU.add))
                    d.norm(v, then, Ya, Ha)
                    then(v.tensor_tensor(Ya, Ya, per_col(vec["L2_gnn_ln_g"][0]), ALU.mult))
                    then(v.tensor_tensor(Ya, Ya, per_col(vec["L2_gnn_ln_b"][0]), ALU.add))
                    then(v.tensor_tensor(Xa, Xa, Ya, ALU.add))
                    d.norm(v, then, XIa, Xa)
                    relu(v, then, XIa)
                Dense(end2)

        if stop > 2:
            with stage_of_work():
                node_product(H, [XI], [mat["W3"][0]])
                gat_prepare(vec["L3_gnn_att_src"][0], vec["L3_gnn_att_dst"][0], 8, tab_d[3])
                gat_pass(tab_d[3], 8)

                def end3(d, v, then):
                    gat_finish(v, then, 8, vec["L3_gnn_bias"][0], Ya)
                    then(v.tensor_tensor(Xa, Xa, Ya, ALU.add))
                Dense(end3)

        written = sem("written")
        with nc.Block() as block:
            @block.sync
            def _(sp):
                sp.dma_start(out[0:FULL * P, :].rearrange("(b p) f -> p b f", p=P), X[:, 0:FULL, :]).then_inc(written, 16)
                sp.dma_start(out[FULL * P:N, :], X[0:REST, FULL, :]).then_inc(written, 16)
                sp.wait_ge(written, 32)


STOP = 4


def kernel(**inputs):
    import numpy as _np
    import concourse.bacc as _bacc
    from concourse import mybir as _mybir
    from concourse.bass_utils import run_bass_kernel_spmd as _run

    nc = _bacc.Bacc("TRN2", target_bir_lowering=False, num_devices=1)
    arrays, args = {}, {}
    for name, value in inputs.items():
        if name == "edge_weight1":
            continue
        v = _np.ascontiguousarray(value)
        arrays[f"in_{name}_dram"] = v
        args[name] = nc.dram_tensor(f"in_{name}_dram", v.shape, _mybir.dt.from_np(v.dtype), kind="ExternalInput").ap()
    out = nc.dram_tensor("out_0_dram", (N, D), F32, kind="ExternalOutput").ap()
    gnn(nc, args, out, STOP)
    r = _run(nc, [arrays], core_ids=[0])
    return r.results[0]["out_0_dram"]
```

```python
from contextlib import ExitStack, contextmanager

import concourse.bass as bass
from concourse import mybir

F32 = mybir.dt.float32
I32 = mybir.dt.int32
BF16 = mybir.dt.bfloat16
ALU = mybir.AluOpType
ACT = mybir.ActivationFunctionType
AX = mybir.AxisListType

P = 128
N = 6250
E = 100000
D = 128
EA = 64
NF = 64
NODE_TILES = -(-N // P)
GN = 4
NG = -(-NODE_TILES // GN)
NBP = GN * NG
FULL = N // P
REST = N - FULL * P
EP, EC = 125, 800
G = 8
MAX_TILES = (E + NODE_TILES * (P - 1)) // P
NT = -(-MAX_TILES // (2 * G)) * 2 * G
ITERS = NT // (2 * G)
SLOTS = NT * P
NTP = NT + G
SC = 16
RW = 72
R_DLOC, R_SRC, R_POS, R_W, R_SLOC = 64, 65, 66, 67, 68
AW = D + 8
MW = 132
SKIP = 1 << 20
LN_EPS = 1e-5
BN_EPS = 1e-3
CUTOFF = 8.0
SLOPE = 0.2
PI = 3.141592653589793


class Steps:

    def __init__(self, eng, sem, start=0):
        self.eng, self.sem, self.start, self.n = eng, sem, start, 0

    def then(self, ins):
        ins.then_inc(self.sem, 1)
        self.n += 1
        self.eng.wait_ge(self.sem, self.start + self.n)


def later(i):
    return not (isinstance(i, int) and i == 0)


def looped(eng, n, body):
    body(0, True)
    with eng.Fori(1, n) as i:
        body(i, False)


def gnn(nc, a, out, stop=4):
    ctx = ExitStack()
    names = [0]

    def sem(name):
        names[0] += 1
        return nc.alloc_semaphore(name=f"{name}_{names[0]}")

    @contextmanager
    def stage_of_work():
        before = nc.snapshot_sems()
        yield
        nc.clear_and_free_semaphores(nc.allocated_since(before))
        nc.all_engine_barrier()

    def dram(name, shape, dt=F32):
        return nc.dram_tensor(name, shape, dt, kind="Internal").ap()

    def sbuf(stack, name, shape, dt=F32):
        names[0] += 1
        return stack.enter_context(nc.sbuf_tensor(f"{name}_{names[0]}", shape, dt))

    rec_d = dram("edge_records", [SLOTS, RW])
    msg_d = dram("layer0_messages", [SLOTS, MW])
    tab_d = [dram(f"node_table{i}", [NBP * P, w]) for i, w in enumerate((D + 1, D + 1, D, D + 8))]

    with ctx:
        def sb(name, shape, dt=F32):
            return sbuf(ctx, name, shape, dt)

        bank = [ctx.enter_context(nc.psum_tensor(f"bank{i}", [P, 512], F32)) for i in range(8)]

        iota_row = sb("iota_row", [P, P])
        ident = sb("ident", [P, P])
        ident_b = sb("ident_b", [P, P], BF16)
        zero1 = sb("zero1", [P, 1])
        dloc = sb("dloc", [P, NTP])
        src_ix = sb("src_ix", [P, NT], I32)
        tile_of_d = sb("tile_of_d", [1, NTP], I32)
        acc_of_d = sb("acc_of_d", [1, NTP], I32)
        acc_of_s = sb("acc_of_s", [1, NTP], I32)
        X = sb("X", [P, NBP, D])
        ACC = sb("ACC", [P, NBP, AW])
        vec = {}
        for v in ("L0_gnn_bi2", "L0_gnn_gamma", "L0_gnn_beta", "L0_gnn_mov_mean", "L0_gnn_mov_var",
                  "L2_gnn_bm1", "L2_gnn_bm2", "L2_gnn_bu2", "L2_gnn_ln_g", "L2_gnn_ln_b", "L3_gnn_bias"):
            vec[v] = (sb(v, [P, D]), a[v])
        for v in ("L1_gnn_att_src", "L1_gnn_att_dst", "L1_gnn_bias", "L1_gnn_gamma", "L1_gnn_beta"):
            for l in range(2):
                vec[v, l] = (sb(f"{v}{l}", [P, D]), a[v][l, :])
        for v in ("L3_gnn_att_src", "L3_gnn_att_dst"):
            vec[v] = (sb(v, [P, D]), a[v].rearrange("h c -> (h c)"))
        mat = {"Wi1": (sb("Wi1", [P, D]), a["L0_gnn_Wi1"]), "Wi2": (sb("Wi2", [P, D]), a["L0_gnn_Wi2"]),
               "W1_0": (sb("W1_0", [P, D]), a["L1_gnn_W"][0]), "W1_1": (sb("W1_1", [P, D]), a["L1_gnn_W"][1]),
               "W3": (sb("W3", [P, D]), a["L3_gnn_W"])}
        bi1_col = sb("bi1_col", [P, 1])
        bu1_col = sb("bu1_col", [P, 1])
        gs_col = sb("gs_col", [64, 1])
        wmaT, wmbT, wmcT = sb("wmaT", [P, D]), sb("wmbT", [64, D]), sb("wmcT", [64, D])
        wm2T, wuaT, wubT, wucT = sb("wm2T", [P, D]), sb("wuaT", [P, D]), sb("wubT", [P, D]), sb("wucT", [64, D])
        wu2T = sb("wu2T", [P, D])
        cm_row = sb("cm_row", [P, D])
        cu_col = sb("cu_col", [P, 1])
        bn_scale = sb("bn_scale", [P, D])
        bn_shift = sb("bn_shift", [P, D])

        with ExitStack() as tmp:
            def tb(name, shape, dt=F32):
                return sbuf(tmp, name, shape, dt)

            tri = tb("tri", [P, P])
            ones = tb("ones", [P, P])
            iota_t = tb("iota_t", [1, NTP])
            pad_rec = tb("pad_rec", [P, G * RW])
            pad_msg = tb("pad_msg", [P, G * MW])
            node = [tb("dst_i", [EP, EC], I32), tb("src_i", [EP, EC], I32)]
            key = [tb("key_d", [EP, EC]), tb("key_s", [EP, EC])]
            pos = [tb("pos_d", [EP, EC]), tb("pos_s", [EP, EC])]
            row = [tb("row_d", [EP, EC], I32), tb("row_s", [EP, EC], I32)]
            eq = [tb("eq_d", [EP, EC]), tb("eq_s", [EP, EC])]
            cum = [tb("cum_d", [EP, EC]), tb("cum_s", [EP, EC])]
            meta = tb("meta", [EP, EC, 5])
            count = [tb("count_d", [EP, NODE_TILES]), tb("count_s", [EP, NODE_TILES])]
            ntile = [tb("ntile_d", [P, NODE_TILES]), tb("ntile_s", [P, NODE_TILES])]
            ntile_i = [tb("ntile_di", [P, NODE_TILES], I32), tb("ntile_si", [P, NODE_TILES], I32)]
            upto = [tb("upto_d", [P, NODE_TILES]), tb("upto_s", [P, NODE_TILES])]
            off = [tb("off_d", [P, NODE_TILES]), tb("off_s", [P, NODE_TILES])]
            tile_f = [tb("tile_fd", [1, NTP]), tb("tile_fs", [1, NTP])]
            acc_i = [acc_of_d, acc_of_s]
            wt = tb("edge_w", [EP, EC])
            fsum = tb("fsum", [EP, EC])
            th = [tb("tanh0", [EP, EC]), tb("tanh1", [EP, EC])]
            wf1, bf1 = tb("wf1", [P, NF]), tb("bf1", [P, NF])
            fscale, fbias = tb("fscale", [P, NF]), tb("fbias", [P, NF])
            wf2, bf2 = tb("wf2", [P, NF, NF]), tb("bf2", [P, NF])
            wf2_sum, bf2_sum = tb("wf2_sum", [P, NF]), tb("bf2_sum", [P, 1])
            wm1, wm2, wu1, wu2 = tb("wm1", [P, 256]), tb("wm2", [P, D]), tb("wu1", [P, 320]), tb("wu2", [P, D])
            half_pi = tb("half_pi", [P, 1])
            gs_b = tb("gs_b", [64, D])

            with stage_of_work():
                consts, pads, edges_in, weights_in, filled, steps_v, steps_p = (
                    sem("consts"), sem("pads"), sem("edges_in"), sem("weights_in"), sem("filled"),
                    sem("steps_v"), sem("steps_p"))
                loop_a, loop_b, counts_ready, offs_in_psum = sem("loop_a"), sem("loop_b"), sem("counts_ready"), sem("offs_in_psum")
                filt_ready, tanh_ready, tanh_used, cos_ready = sem("filt_ready"), sem("tanh_ready"), sem("tanh_used"), sem("cos_ready")
                wT_ready, wT_copied, cvec_ready, steps_a = sem("wT_ready"), sem("wT_copied"), sem("cvec_ready"), sem("steps_a")
                x_zero, bnv, bns = sem("x_zero"), sem("bnv"), sem("bns")
                NW = len(vec) + len(mat) + 7
                with nc.Block() as block:
                    @block.sync
                    def _(sp):
                        sp.dma_start(node[0][:, :], a["dst"].rearrange("(p c) -> p c", c=EC)).then_inc(edges_in, 16)
                        sp.dma_start(node[1][:, :], a["src"].rearrange("(p c) -> p c", c=EC)).then_inc(edges_in, 16)
                        sp.dma_start(wt[:, :], a["edge_weight"].rearrange("(p c) -> p c", c=EC)).then_inc(edges_in, 16)
                        sp.dma_start(wf1[:, :], a["L0_gnn_Wf1"].to_broadcast([P, NF])).then_inc(edges_in, 16)
                        sp.dma_start(bf1[:, :], a["L0_gnn_bf1"].unsqueeze(0).to_broadcast([P, NF])).then_inc(edges_in, 16)
                        sp.dma_start(bf2[:, :], a["L0_gnn_bf2"].unsqueeze(0).to_broadcast([P, NF])).then_inc(edges_in, 16)
                        sp.dma_start(wf2[:, :, :], a["L0_gnn_Wf2"].unsqueeze(0).to_broadcast([P, NF, NF])).then_inc(edges_in, 16)
                        for t, v in vec.values():
                            sp.dma_start(t[:, :], v.unsqueeze(0).to_broadcast([P, D])).then_inc(weights_in, 16)
                        for t, v in mat.values():
                            sp.dma_start(t[:, :], v).then_inc(weights_in, 16)
                        for t, v in ((bi1_col, a["L0_gnn_bi1"]), (bu1_col, a["L2_gnn_bu1"]), (gs_col, a["L2_gnn_global_state"])):
                            sp.dma_start(t[:, :], v.rearrange("(p a) -> p a", a=1)).then_inc(weights_in, 16)
                        for t, v in ((wm1, "L2_gnn_Wm1"), (wm2, "L2_gnn_Wm2"), (wu1, "L2_gnn_Wu1"), (wu2, "L2_gnn_Wu2")):
                            sp.dma_start(t[:, :], a[v]).then_inc(weights_in, 16)
                        sp.wait_ge(x_zero, 1)
                        sp.dma_start(X[:, 0:FULL, :], a["x"][0:FULL * P, :].rearrange("(b p) f -> p b f", p=P)).then_inc(filled, 16)
                        sp.dma_start(X[0:REST, FULL, :], a["x"][FULL * P:N, :]).then_inc(filled, 16)
                        sp.wait_ge(pads, 1)
                        sp.dma_start(rec_d.rearrange("(k p j) w -> p k (j w)", p=P, j=G),
                                     pad_rec[:, :].unsqueeze(1).to_broadcast([P, NT // G, G * RW])).then_inc(filled, 16)
                        sp.dma_start(msg_d.rearrange("(k p j) w -> p k (j w)", p=P, j=G),
                                     pad_msg[:, :].unsqueeze(1).to_broadcast([P, NT // G, G * MW])).then_inc(filled, 16)
                        sp.wait_ge(filled, 64)

                    @block.gpsimd
                    def _(pool):
                        st = Steps(pool, steps_p)
                        st.then(pool.memset(ident[:, :], 0.0))
                        st.then(pool.affine_select(out=ident[:, :], in_=ident[:, :], compare_op=ALU.not_equal, fill=1.0,
                                                   base=0, pattern=[[-1, P]], channel_multiplier=1))
                        st.then(pool.tensor_copy(ident_b[:, :], ident[:, :]))
                        st.then(pool.memset(tri[:, :], 1.0))
                        st.then(pool.affine_select(out=tri[:, :], in_=tri[:, :], compare_op=ALU.is_gt, fill=0.0,
                                                   base=0, pattern=[[1, P]], channel_multiplier=-1))
                        st.then(pool.memset(ones[:, :], 1.0))
                        st.then(pool.memset(dloc[:, NT:NTP], -1.0))
                        st.then(pool.iota(iota_row[:, :], [[1, P]], base=0, channel_multiplier=0,
                                          allow_small_or_imprecise_dtypes=True))
                        st.then(pool.iota(iota_t[:, :], [[1, NTP]], base=0, channel_multiplier=0,
                                          allow_small_or_imprecise_dtypes=True))
                        st.then(pool.memset(zero1[:, :], 0.0))
                        pool.sem_inc(consts, 1)
                        pr = pad_rec[:, :].rearrange("p (j w) -> p j w", w=RW)
                        pm = pad_msg[:, :].rearrange("p (j w) -> p j w", w=MW)
                        st.then(pool.memset(pad_rec[:, :], 0.0))
                        st.then(pool.memset(pad_msg[:, :], 0.0))
                        st.then(pool.memset(pr[:, :, R_DLOC:R_DLOC + 1], -1.0))
                        st.then(pool.memset(pr[:, :, R_SLOC:R_SLOC + 1], -1.0))
                        st.then(pool.memset(pr[:, :, R_POS:R_POS + 1], float(SKIP)))
                        st.then(pool.memset(pm[:, :, D:D + 1], -1.0))
                        pool.sem_inc(pads, 1)
                        st.then(pool.memset(X[:, :, :], 0.0))
                        pool.sem_inc(x_zero, 1)
                        st.then(pool.memset(ACC[:, :, :], 0.0))

                    @block.tensor
                    def _(pe):
                        pe.wait_ge(consts, 1)
                        pe.wait_ge(counts_ready, 1)
                        for q in range(2):
                            nc.tensor.matmul(bank[q][:, 0:NODE_TILES], tri[0:EP, :], count[q][:, :], start=True, stop=True)
                            nc.tensor.matmul(bank[2 + q][:, 0:NODE_TILES], ones[0:EP, :], count[q][:, :], start=True,
                                             stop=True).then_inc(offs_in_psum, 1)
                        pe.wait_ge(weights_in, 16 * NW)
                        for n, (w, lo, hi) in enumerate(((wm1, 0, 128), (wm1, 128, 192), (wm1, 192, 256), (wm2, 0, 128))):
                            nc.tensor.transpose(bank[4][0:hi - lo, n * P:n * P + P], w[:, lo:hi], ident[:, :]).then_inc(wT_ready, 1)
                        for n, (w, lo, hi) in enumerate(((wu1, 0, 128), (wu1, 128, 256), (wu1, 256, 320), (wu2, 0, 128))):
                            nc.tensor.transpose(bank[5][0:hi - lo, n * P:n * P + P], w[:, lo:hi], ident[:, :]).then_inc(wT_ready, 1)
                        pe.wait_ge(wT_copied, 1)
                        nc.tensor.matmul(bank[6][:, 0:P], gs_b[:, :], wmcT[:, :], start=True, stop=True)
                        nc.tensor.matmul(bank[7][:, 0:1], wucT[:, :], gs_col[:, :], start=True, stop=True).then_inc(cvec_ready, 1)

                    @block.scalar
                    def _(act):
                        st = Steps(act, steps_a)
                        act.wait_ge(filt_ready, 1)
                        for f in range(NF):
                            if f >= 2:
                                act.wait_ge(tanh_used, f - 1)
                            nc.scalar.activation(th[f % 2][:, :], wt[:, :], ACT.Tanh, bias=fbias[0:EP, f:f + 1],
                                                 scale=fscale[0:EP, f:f + 1]).then_inc(tanh_ready, 1)
                        act.wait_ge(tanh_used, NF)
                        act.wait_ge(cos_ready, 1)
                        st.then(nc.scalar.activation(th[0][:, :], th[1][:, :], ACT.Sin, bias=half_pi[0:EP, :],
                                                     scale=-PI / CUTOFF))
                        act.sem_inc(cos_ready, 1)
                        act.wait_ge(wT_ready, 8)
                        for n, (t, r) in enumerate(((wmaT, P), (wmbT, 64), (wmcT, 64), (wm2T, P))):
                            st.then(nc.scalar.copy(t[:, :], bank[4][0:r, n * P:n * P + P]))
                        for n, (t, r) in enumerate(((wuaT, P), (wubT, P), (wucT, 64), (wu2T, P))):
                            st.then(nc.scalar.copy(t[:, :], bank[5][0:r, n * P:n * P + P]))
                        st.then(nc.scalar.copy(gs_b[:, :], gs_col[:, 0:1].to_broadcast([64, D])))
                        act.sem_inc(wT_copied, 1)
                        act.wait_ge(bnv, 1)
                        st.then(nc.scalar.activation(bn_scale[:, :], bn_scale[:, :], ACT.Sqrt, bias=zero1[:, :]))
                        act.sem_inc(bns, 1)

                    @block.vector
                    def _(dve):
                        v = nc.vector
                        st = Steps(dve, steps_v)
                        dve.wait_ge(edges_in, 16 * 7)
                        dve.wait_ge(consts, 1)
                        st.then(v.tensor_scalar(fscale[:, :], wf1[:, :], 2.0 / CUTOFF, None, ALU.mult))
                        st.then(v.tensor_tensor(fbias[:, :], bf1[:, :], wf1[:, :], ALU.subtract))
                        st.then(v.tensor_reduce(wf2_sum[:, :], wf2[:, :, :], AX.X, ALU.add))
                        st.then(v.tensor_reduce(bf2_sum[:, :], bf2[:, :], AX.X, ALU.add))
                        st.then(v.memset(half_pi[:, :], PI / 2))
                        dve.sem_inc(filt_ready, 1)
                        for q in range(2):
                            st.then(v.tensor_single_scalar(row[q][:, :], node[q][:, :], 7, ALU.logical_shift_right))
                            st.then(v.tensor_copy(key[q][:, :], row[q][:, :]))
                            st.then(v.tensor_single_scalar(row[q][:, :], node[q][:, :], P - 1, ALU.bitwise_and))
                            st.then(v.tensor_copy(meta[:, :, 4 * q:4 * q + 1], row[q][:, :].unsqueeze(2)))
                            st.then(v.memset(pos[q][:, :], 0.0))
                            st.then(v.memset(tile_f[q][:, :], 0.0))
                        st.then(v.tensor_copy(meta[:, :, 1:2], node[1][:, :].unsqueeze(2)))
                        with dve.Fori(0, NODE_TILES) as b:
                            ls = Steps(dve, loop_a, b * 4)
                            for q in range(2):
                                ls.then(v.tensor_scalar(eq[q][:, :], key[q][:, :], iota_row[0:EP, bass.ds(b, 1)], None,
                                                        ALU.is_equal))
                                ls.then(v.tensor_reduce(count[q][:, bass.ds(b, 1)], eq[q][:, :], AX.X, ALU.add))
                        dve.sem_inc(counts_ready, 1)
                        dve.wait_ge(offs_in_psum, 2)
                        for q in range(2):
                            st.then(v.tensor_scalar(ntile_i[q][:, :], bank[2 + q][:, 0:NODE_TILES], float(P - 1), None, ALU.add))
                            st.then(v.tensor_single_scalar(ntile_i[q][:, :], ntile_i[q][:, :], 7, ALU.logical_shift_right))
                            st.then(v.tensor_copy(ntile[q][:, :], ntile_i[q][:, :]))
                            st.then(v.tensor_tensor_scan(upto[q][:, :], ntile[q][:, :], ntile[q][:, :], 0.0, ALU.add, ALU.bypass))
                            st.then(v.tensor_tensor(ntile[q][:, :], upto[q][:, :], ntile[q][:, :], ALU.subtract))
                            st.then(v.tensor_scalar(ntile[q][:, :], ntile[q][:, :], float(P), -1.0, ALU.mult, ALU.add))
                            st.then(v.tensor_tensor(off[q][:, :], ntile[q][:, :], bank[q][:, 0:NODE_TILES], ALU.add))
                        with dve.Fori(0, NODE_TILES) as b:
                            ls = Steps(dve, loop_b, b * 10)
                            for q in range(2):
                                col = iota_row[0:EP, bass.ds(b, 1)]
                                ls.then(v.tensor_scalar(eq[q][:, :], key[q][:, :], col, None, ALU.is_equal))
                                ls.then(v.tensor_tensor_scan(cum[q][:, :], eq[q][:, :], eq[q][:, :], off[q][0:EP, bass.ds(b, 1)],
                                                             ALU.add, ALU.bypass))
                                ls.then(v.tensor_tensor(cum[q][:, :], cum[q][:, :], eq[q][:, :], ALU.mult))
                                ls.then(v.tensor_tensor(pos[q][:, :], pos[q][:, :], cum[q][:, :], ALU.add))
                                ls.then(v.scalar_tensor_tensor(tile_f[q][:, :], iota_t[:, :], upto[q][0:1, bass.ds(b, 1)],
                                                               tile_f[q][:, :], ALU.is_ge, ALU.add))
                        for q in range(2):
                            if q == 0:
                                st.then(v.tensor_scalar(tile_of_d[:, :], tile_f[q][:, :], float(NODE_TILES - 1), None, ALU.min))
                            st.then(v.tensor_scalar(acc_i[q][:, :], tile_f[q][:, :], float(NODE_TILES - 1), float(AW),
                                                    ALU.min, ALU.mult))
                            ci, ei = cum[q][:, :].bitcast(I32), eq[q][:, :].bitcast(I32)
                            st.then(v.tensor_copy(ci, pos[q][:, :]))
                            st.then(v.tensor_scalar(row[q][:, :], ci, -P * G, None, ALU.bitwise_and))
                            st.then(v.tensor_scalar(ei, ci, P - 1, 3, ALU.bitwise_and, ALU.logical_shift_left))
                            st.then(v.tensor_tensor(row[q][:, :], row[q][:, :], ei, ALU.bitwise_or))
                            st.then(v.tensor_scalar(ei, ci, 7, G - 1, ALU.logical_shift_right, ALU.bitwise_and))
                            st.then(v.tensor_tensor(row[q][:, :], row[q][:, :], ei, ALU.bitwise_or))
                        st.then(v.tensor_copy(meta[:, :, 2:3], row[1][:, :].unsqueeze(2)))
                        for f in range(NF):
                            dve.wait_ge(tanh_ready, f + 1)
                            if f == 0:
                                v.tensor_scalar(fsum[:, :], th[0][:, :], wf2_sum[0:EP, 0:1], bf2_sum[0:EP, 0:1],
                                                ALU.mult, ALU.add).then_inc(tanh_used, 1)
                            else:
                                dve.wait_ge(tanh_used, f)
                                v.scalar_tensor_tensor(fsum[:, :], th[f % 2][:, :], wf2_sum[0:EP, f:f + 1], fsum[:, :],
                                                       ALU.mult, ALU.add).then_inc(tanh_used, 1)
                        dve.wait_ge(tanh_used, NF)
                        st.then(v.tensor_scalar(th[1][:, :], wt[:, :], CUTOFF, None, ALU.min))
                        dve.sem_inc(cos_ready, 1)
                        dve.wait_ge(cos_ready, 2)
                        st.then(v.tensor_scalar(th[0][:, :], th[0][:, :], 0.5, 0.5, ALU.mult, ALU.add))
                        st.then(v.scalar_tensor_tensor(th[1][:, :], wt[:, :], CUTOFF, th[0][:, :], ALU.is_le, ALU.mult))
                        st.then(v.tensor_tensor(meta[:, :, 3:4], fsum[:, :].unsqueeze(2), th[1][:, :].unsqueeze(2), ALU.mult))
                        dve.wait_ge(weights_in, 16 * NW)
                        st.then(v.tensor_scalar(bn_scale[:, :], vec["L0_gnn_mov_var"][0][:, :], BN_EPS, None, ALU.add))
                        dve.sem_inc(bnv, 1)
                        dve.wait_ge(bns, 1)
                        st.then(v.reciprocal(bn_scale[:, :], bn_scale[:, :]))
                        st.then(v.tensor_tensor(bn_scale[:, :], bn_scale[:, :], vec["L0_gnn_gamma"][0][:, :], ALU.mult))
                        st.then(v.tensor_tensor(bn_shift[:, :], vec["L0_gnn_bi2"][0][:, :], vec["L0_gnn_mov_mean"][0][:, :], ALU.subtract))
                        st.then(v.tensor_tensor(bn_shift[:, :], bn_shift[:, :], bn_scale[:, :], ALU.mult))
                        st.then(v.tensor_tensor(bn_shift[:, :], bn_shift[:, :], vec["L0_gnn_beta"][0][:, :], ALU.add))
                        dve.wait_ge(cvec_ready, 1)
                        st.then(v.tensor_tensor(cm_row[:, :], bank[6][:, 0:P], vec["L2_gnn_bm1"][0][:, :], ALU.add))
                        st.then(v.tensor_tensor(cu_col[:, :], bank[7][:, 0:1], bu1_col[:, :], ALU.add))

            rec = [tb(f"rec_out{h}", [EP, SC, RW]) for h in range(2)]
            ixs = [tb(f"ixs_out{h}", [EP, SC], I32) for h in range(2)]
            with stage_of_work():
                attr_in = [sem("attr_in0"), sem("attr_in1")]
                meta_in = [sem("meta_in0"), sem("meta_in1")]
                scattered = [sem("scattered0"), sem("scattered1")]
                tick, cleared = sem("tick"), sem("cleared")
                attr_v = a["edge_attr_64"].rearrange("(p c) w -> p c w", c=EC)
                with nc.Block() as block:
                    @block.sync
                    def _(sp):
                        def body(i, first):
                            for h in range(2):
                                if first:
                                    sp.wait_ge(cleared, h + 1)
                                else:
                                    sp.wait_ge(scattered[h], i * (16 * SC))
                                sp.dma_start(rec[h][:, :, 0:EA],
                                             attr_v[:, bass.ds((2 * i + h) * SC, SC), :]).then_inc(attr_in[h], 16)
                        looped(sp, EC // (2 * SC), body)

                    @block.vector
                    def _(dve):
                        def body(i, first):
                            for h in range(2):
                                if first:
                                    nc.vector.memset(rec[h][:, :, EA:RW], 0.0).then_inc(cleared, 1)
                                    dve.wait_ge(cleared, h + 1)
                                else:
                                    dve.wait_ge(scattered[h], i * (16 * SC))
                                nc.vector.tensor_copy(rec[h][:, :, EA:EA + 5], meta[:, bass.ds((2 * i + h) * SC, SC), :]) \
                                    .then_inc(meta_in[h], 1)
                                nc.vector.tensor_copy(ixs[h][:, :], row[0][:, bass.ds((2 * i + h) * SC, SC)]) \
                                    .then_inc(meta_in[h], 1)
                        looped(dve, EC // (2 * SC), body)

                    @block.gpsimd
                    def _(pool):
                        with pool.Fori(0, EC // (2 * SC)) as i:
                            for h in range(2):
                                pool.wait_ge(attr_in[h], i * 16 + 16)
                                pool.sem_inc(tick, 1)
                                pool.wait_ge(meta_in[h], i * 2 + 2)
                                pool.sem_inc(tick, 1)
                                for j in range(SC):
                                    pool.indirect_dma_start(rec_d, bass.IndirectOffsetOnAxis(ap=ixs[h][:, j:j + 1], axis=0),
                                                            rec[h][:, j, :], None).then_inc(scattered[h], 16)
                        for h in range(2):
                            pool.wait_ge(scattered[h], 16 * SC * (EC // (2 * SC)))

        H = sb("H", [P, NBP, AW])
        XI = sb("XI", [P, NBP, D])
        Y = sb("Y", [P, NBP, D])

        def per_tile(t, w=D):
            return t.unsqueeze(2).to_broadcast([P, NBP, w])

        def per_col(t):
            return t[:, :].unsqueeze(1).to_broadcast([P, NBP, D])

        mean, var = sb("mean", [P, NBP]), sb("var", [P, NBP])
        stats = sb("stats", [P, NBP, 6])

        class Dense:

            def __init__(self, work):
                self.jobs = []
                steps, asked, done = sem("dense_steps"), sem("dense_asked"), sem("dense_done")
                with nc.Block() as block:
                    @block.vector
                    def _(dve):
                        self.dve, self.st, self.asked, self.done = dve, Steps(dve, steps), asked, done
                        work(self, nc.vector, self.st.then)

                    @block.scalar
                    def _(act):
                        for n, (o, i, f) in enumerate(self.jobs):
                            act.wait_ge(asked, n + 1)
                            nc.scalar.activation(o, i, f, bias=zero1[0:P, :]).then_inc(done, 1)

            def act(self, o, i, f):
                self.jobs.append((o, i, f))
                self.dve.sem_inc(self.asked, 1)
                self.dve.wait_ge(self.done, len(self.jobs))

            def norm(self, v, then, o, i):
                for b in range(NBP):
                    ins = v.bn_stats(stats[:, b, :], i[:, b, :])
                then(ins)
                mean_e, mean_o = stats[:, :, 1], stats[:, :, 4]
                then(v.tensor_tensor(var[:, :], mean_e, mean_o, ALU.subtract))
                then(v.tensor_tensor(var[:, :], var[:, :], var[:, :], ALU.mult))
                then(v.scalar_tensor_tensor(var[:, :], var[:, :], D / 4.0, stats[:, :, 2], ALU.mult, ALU.add))
                then(v.tensor_tensor(var[:, :], var[:, :], stats[:, :, 5], ALU.add))
                then(v.tensor_scalar(var[:, :], var[:, :], 1.0 / D, LN_EPS, ALU.mult, ALU.add))
                then(v.tensor_tensor(mean[:, :], mean_e, mean_o, ALU.add))
                then(v.tensor_scalar(mean[:, :], mean[:, :], 0.5, None, ALU.mult))
                self.act(var[:, :], var[:, :], ACT.Sqrt)
                then(v.reciprocal(var[:, :], var[:, :]))
                for b in range(NBP):
                    ins = v.tensor_scalar(o[:, b, :], i[:, b, :], mean[:, b:b + 1], var[:, b:b + 1], ALU.subtract, ALU.mult)
                then(ins)

        rows = [sb(f"rows{h}", [P, G, AW]) for h in range(2)]
        recs = [sb(f"recs{h}", [P, G, RW]) for h in range(2)]
        rows_w = [t[:, :, :].rearrange("p j w -> p (j w)") for t in rows]
        stage = [rows_w[0][:, n * GN * D:(n + 1) * GN * D].rearrange("p (j f) -> p j f", f=D) for n in range(2)]
        hid, tmp_e = (rows_w[1][:, n * GN * P:(n + 1) * GN * P] for n in range(2))
        stT = [t[:, :, :].rearrange("p j w -> p (j w)")[:, 0:GN * P] for t in recs]

        def node_product(dst, srcs, ws, w2=None, hidden=None, bias=None, extra=None):
            k = len(srcs)
            cols = D + (extra[1] if extra else 0)
            staged, turned, turned_sb, in_hid, hid_ready, prod, taken, minus, exps = (
                sem(n) for n in ("staged", "turned", "turned_sb", "in_hid", "hid_ready", "prod", "taken", "minus", "exps"))
            turns = 2 if k == 1 else 1

            with nc.Block() as block:
                @block.vector
                def _(dve):
                    def put(g):
                        for n, src in enumerate(srcs):
                            if g >= turns:
                                dve.wait_ge(turned, (g - turns) * k + n + 1)
                            nc.vector.tensor_copy(stage[n if k > 1 else g % 2][:, :, :], src[:, g * GN:(g + 1) * GN, 0:D]) \
                                .then_inc(staged, 1)

                    def take(g):
                        dve.wait_ge(prod, 2 * g + 2)
                        for q in range(2):
                            ps = bank[4 + 2 * (g % 2) + q][:, 0:2 * cols].rearrange("p (j f) -> p j f", f=cols)
                            at = slice(g * GN + 2 * q, g * GN + 2 * q + 2)
                            half = extra[1] // 2 if extra else 0
                            ins = nc.vector.tensor_copy(dst[:, at, 0:D + half], ps[:, :, 0:D + half])
                            if extra:
                                ins = nc.vector.tensor_copy(extra[0][:, at, :], ps[:, :, D + half:cols])
                        ins.then_inc(taken, 1)

                    put(0)
                    for g in range(NG):
                        if g + 1 < NG:
                            put(g + 1)
                        if hidden == "softplus":
                            dve.wait_ge(in_hid, g + 1)
                            if g:
                                dve.wait_ge(prod, 2 * g)
                            nc.vector.tensor_scalar(hid[:, :], bank[2][:, :], bias[:, 0:1], None, ALU.add).then_inc(minus, 1)
                            dve.wait_ge(minus, 3 * g + 1)
                            nc.vector.tensor_scalar(tmp_e[:, :], hid[:, :], -1.0, None, ALU.mult).then_inc(minus, 1)
                            dve.wait_ge(minus, 3 * g + 2)
                            nc.vector.tensor_tensor(tmp_e[:, :], tmp_e[:, :], hid[:, :], ALU.min).then_inc(minus, 1)
                            dve.wait_ge(exps, 2 * g + 2)
                            nc.vector.scalar_tensor_tensor(hid[:, :], hid[:, :], 0.0, tmp_e[:, :], ALU.max, ALU.add) \
                                .then_inc(hid_ready, 1)
                        if g >= 1 or w2 is None:
                            take(g if w2 is None else g - 1)
                    if w2 is not None:
                        take(NG - 1)
                    dve.wait_ge(taken, NG)

                @block.tensor
                def _(pe):
                    def turn(g):
                        for n in range(k):
                            pe.wait_ge(staged, g * k + n + 1)
                            if g >= turns:
                                pe.wait_ge(turned_sb, (g - turns) * k + n + 1)
                            buf = n if k > 1 else g % 2
                            for j in range(GN):
                                ins = nc.tensor.transpose(bank[buf][:, j * P:j * P + P], stage[buf][:, j, :], ident[:, :])
                            ins.then_inc(turned, 1)

                    def first(g):
                        pe.wait_ge(turned_sb, g * k + k)
                        if g:
                            pe.wait_ge(hid_ready, g)
                        for n in range(k):
                            ins = nc.tensor.matmul(bank[2][:, :], ws[n][:, :], stT[n if k > 1 else g % 2],
                                                   start=(n == 0), stop=(n == k - 1))
                        ins.then_inc(in_hid, 1)

                    def last(g):
                        if w2 is None:
                            pe.wait_ge(turned_sb, g * k + k)
                        else:
                            pe.wait_ge(hid_ready, g + 1)
                        if g >= 2:
                            pe.wait_ge(taken, g - 1)
                        for j in range(GN):
                            o = bank[4 + 2 * (g % 2) + j // 2][:, (j % 2) * cols:(j % 2 + 1) * cols]
                            if w2 is not None:
                                ins = nc.tensor.matmul(o, hid[:, j * P:j * P + P], w2[:, :], start=True, stop=True)
                            for n in range(k if w2 is None else 0):
                                ins = nc.tensor.matmul(o, stT[n if k > 1 else g % 2][:, j * P:j * P + P], ws[n][:, 0:cols],
                                                       start=(n == 0), stop=(n == k - 1))
                            if j % 2:
                                ins.then_inc(prod, 1)

                    turn(0)
                    for g in range(NG):
                        if w2 is not None:
                            first(g)
                        if g + 1 < NG:
                            turn(g + 1)
                        last(g)

                @block.scalar
                def _(act):
                    def copy(g):
                        for n in range(k):
                            act.wait_ge(turned, g * k + n + 1)
                            if g >= turns:
                                if w2 is None:
                                    act.wait_ge(prod, 2 * (g - turns) + 2)
                                else:
                                    act.wait_ge(in_hid, g - turns + 1)
                            buf = n if k > 1 else g % 2
                            nc.scalar.copy(stT[buf][:, :], bank[buf][:, :]).then_inc(turned_sb, 1)

                    copy(0)
                    for g in range(NG):
                        if w2 is None:
                            if g + 1 < NG:
                                copy(g + 1)
                            continue
                        if hidden == "relu":
                            act.wait_ge(in_hid, g + 1)
                            if g:
                                act.wait_ge(prod, 2 * g)
                            nc.scalar.activation(hid[:, :], bank[2][:, :], ACT.Relu, bias=bias[:, 0:1]).then_inc(hid_ready, 1)
                        else:
                            act.wait_ge(minus, 3 * g + 3)
                            nc.scalar.activation(tmp_e[:, :], tmp_e[:, :], ACT.Exp, bias=zero1[:, :]).then_inc(exps, 1)
                            act.wait_ge(exps, 2 * g + 1)
                            nc.scalar.activation(tmp_e[:, :], tmp_e[:, :], ACT.Ln, bias=one1[:, :]).then_inc(exps, 1)
                        if g + 1 < NG:
                            copy(g + 1)

        one1 = sb("one1", [P, 1])

        Yflat = Y[:, :, :].rearrange("p b f -> p (b f)")
        oh = [Yflat[:, h * G * P:(h + 1) * G * P].rearrange("p (j n) -> p j n", j=G) for h in range(2)]
        ohT = [Yflat[:, (2 + h) * G * P:(3 + h) * G * P] for h in range(2)]
        msgs = [Yflat[:, 4 * G * P + h * G * AW:4 * G * P + (h + 1) * G * AW].rearrange("p (j w) -> p j w", j=G)
                for h in range(2)]
        ixr = [sb(f"ixr{h}", [P, G], I32) for h in range(2)]
        z = [sb(f"z{h}", [P, G, 8]) for h in range(2)]
        adc = sb("adc", [P, NBP * 48], BF16)
        ohb = [ohT[h].bitcast(BF16)[:, 0:G * P] for h in range(2)]
        ohbT = [ohT[h].bitcast(BF16)[:, G * P:2 * G * P] for h in range(2)]
        pk = sb("pk", [P, G, 16])

        def onehot(dve, h, loc):
            return nc.vector.tensor_tensor(oh[h][:, :, :], iota_row[:, :].unsqueeze(1).to_broadcast([P, G, P]),
                                           loc.to_broadcast([P, G, P]), ALU.is_equal)

        sums = [ACC[:, :, :].rearrange("p b w -> p (b w)"), H[:, :, :].rearrange("p b w -> p (b w)")]

        def both_sums(v, then, w):
            then(v.tensor_tensor(ACC[:, :, 0:w], ACC[:, :, 0:w], H[:, :, 0:w], ALU.add))

        def node_tiles(engine, tiles, i, h):
            return nc.values_load_multi_w_load_instructions(
                tiles[0:1, bass.ds(i * 2 * G + h * G, G)], engines=[engine], min_val=0,
                max_val=(NODE_TILES - 1) * (AW if tiles is not tile_of_d else 1),
                skip_runtime_bounds_check_because="setup cuts them at NODE_TILES - 1")[1]

        def sum_slot(j):
            return bank[4 + j // 2][:, (j % 2) * AW:(j % 2) * AW + AW]

        def sum_tiles(pe, i, h, onehots, messages, w, summed, added, used):
            for j in range(G):
                if j % 2 == 0 and (later(i) or h):
                    pe.wait_ge(added, i * 2 * G + h * G - G + j + 2)
                ins = nc.tensor.matmul(sum_slot(j)[:, 0:w], onehots[:, j, :], messages[:, j, 0:w], start=True, stop=True)
                if j % 2:
                    ins.then_inc(summed, 1)
            pe.wait_ge(summed, (i * 2 + h + 1) * (G // 2))
            pe.sem_inc(used[h], 1)

        def before(i, h):
            return (i, 0) if h else (i - 1, 1)

        def add_sums(dve, i, h, tiles, w, summed, added):
            at = node_tiles(mybir.EngineType.DVE, tiles, i, h)
            for j in range(G):
                if j % 2 == 0:
                    dve.wait_ge(summed, (i * 2 + h) * (G // 2) + j // 2 + 1)
                t = i * 2 * G + h * G + j
                acc = sums[j % 2][:, bass.ds(at[j], w)]
                if j >= 2 or h or later(i):
                    dve.wait_ge(added, t - 1)
                nc.vector.tensor_tensor(acc, acc, sum_slot(j)[:, 0:w], ALU.add).then_inc(added, 1)

        def ahead(h):
            return (1, 0) if h == 0 else (0, 1)

        def turn_onehot(pe, i, h, oh_ready, turned, ohT_ready):
            pe.wait_ge(oh_ready[h], i + 1)
            if later(i) or h:
                pe.wait_ge(ohT_ready, i * 4 + 2 * h)
            for j in range(G):
                ins = nc.tensor.transpose(bank[j // 4][:, (j % 4) * P:(j % 4) * P + P], oh[h][:, j, :], ident[:, :])
                if j % 4 == 3:
                    ins.then_inc(turned, 1)

        def copy_turned(act, i, h, turned, ohT_ready, ohT_used):
            if later(i):
                act.wait_ge(ohT_used[h], i)
            for n in range(2):
                act.wait_ge(turned, i * 4 + 2 * h + n + 1)
                nc.scalar.copy(ohT[h][:, n * 512:n * 512 + 512], bank[n][:, :]).then_inc(ohT_ready, 1)

        def layer0_dst_pass():
            rec_in, oh_ready, ohT_used, scaled, sent, kept = ([sem(f"{n}{h}") for h in range(2)] for n in
                                                              ("rec_in", "oh_ready", "ohT_used", "scaled", "sent", "kept"))
            turned, ohT_ready, picked, psum_free = sem("turned"), sem("ohT_ready"), sem("picked"), sem("psum_free")
            cleared = sem("cleared")
            fields = XI[:, :, :].rearrange("p b f -> p (b f)")[:, 0:NT * 5].rearrange("p (t k) -> p t k", k=5)
            rec_v = rec_d.rearrange("(k p j) w -> k p (j w)", p=P, j=G)
            with nc.Block() as block:
                @block.sync
                def _(sp):
                    def body(i, first):
                        for h in range(2):
                            if not first:
                                sp.wait_ge(kept[h], i)
                            sp.dma_start(recs[h][:, :, :].rearrange("p j w -> p (j w)"),
                                         rec_v[bass.ds(2 * i + h, 1)].rearrange("k p w -> (k p) w")).then_inc(rec_in[h], 16)
                    looped(sp, ITERS, body)

                @block.vector
                def _(dve):
                    def prepare(i, h):
                        t = i * 2 * G + h * G
                        dve.wait_ge(rec_in[h], i * 16 + 16)
                        nc.vector.tensor_copy(fields[:, bass.ds(t, G), :], recs[h][:, :, EA:EA + 5]).then_inc(kept[h], 1)
                        dve.wait_ge(kept[h], i + 1)
                        if later(i):
                            dve.wait_ge(ohT_used[h], i)
                        onehot(dve, h, fields[:, bass.ds(t, G), 0:1]).then_inc(oh_ready[h], 1)

                    def finish(i, h):
                        t = i * 2 * G + h * G
                        if later(i):
                            dve.wait_ge(sent[h], i * (16 * G))
                        nc.vector.tensor_copy(rows[h][:, :, D:D + 1], fields[:, bass.ds(t, G), R_SLOC - EA:R_SLOC - EA + 1]) \
                            .then_inc(scaled[h], 1)
                        nc.vector.tensor_copy(ixr[h][:, :].unsqueeze(2),
                                              fields[:, bass.ds(t, G), R_POS - EA:R_POS - EA + 1]) \
                            .then_inc(scaled[h], 1)
                        for n in range(2):
                            dve.wait_ge(picked, i * 4 + 2 * h + n + 1)
                            nc.vector.tensor_tensor(rows[h][:, 4 * n:4 * n + 4, 0:D],
                                                    bank[2 + n][:, :].rearrange("p (j f) -> p j f", f=D),
                                                    fields[:, bass.ds(t + 4 * n, 4), R_W - EA:R_W - EA + 1].to_broadcast([P, 4, D]),
                                                    ALU.mult).then_inc(scaled[h], 1)
                        dve.wait_ge(scaled[h], i * 4 + 4)
                        dve.sem_inc(psum_free, 1)

                    for h in range(2):
                        nc.vector.memset(rows[h][:, :, D:D + 8], 0.0).then_inc(cleared, 1)
                    dve.wait_ge(cleared, 2)
                    prepare(0, 0)

                    def body(i, last):
                        finish_after = (0, 1)
                        for h in finish_after:
                            nh, step = ahead(h)
                            if not (last and h == 1):
                                prepare(i + step, nh)
                            finish(i, h)
                    body(0, False)
                    with dve.Fori(1, ITERS - 1) as i:
                        body(i, False)
                    body(ITERS - 1, True)
                    for n in range(2):
                        dve.wait_ge(kept[n], ITERS)
                    nc.vector.tensor_copy(dloc[:, 0:NT].unsqueeze(2), fields[:, :, 0:1])
                    nc.vector.tensor_copy(src_ix[:, :].unsqueeze(2), fields[:, :, 1:2])

                @block.tensor
                def _(pe):
                    def pick(i, h):
                        at = node_tiles(mybir.EngineType.PE, tile_of_d, i, h)
                        if later(i) or h:
                            pe.wait_ge(psum_free, i * 2 + h)
                        for j in range(G):
                            if j % 4 == 0:
                                pe.wait_ge(ohT_ready, i * 4 + 2 * h + j // 4 + 1)
                            ins = nc.tensor.matmul(bank[2 + j // 4][:, (j % 4) * P:(j % 4) * P + P],
                                                   ohT[h][:, j * P:j * P + P], Hflat[:, bass.ds(at[j] * AW, D)],
                                                   start=True, stop=True)
                            if j % 4 == 3:
                                ins.then_inc(picked, 1)
                        pe.wait_ge(picked, i * 4 + 2 * h + 2)
                        pe.sem_inc(ohT_used[h], 1)

                    turn_onehot(pe, 0, 0, oh_ready, turned, ohT_ready)

                    def body(i, last):
                        for h in range(2):
                            nh, step = ahead(h)
                            if not (last and h == 1):
                                turn_onehot(pe, i + step, nh, oh_ready, turned, ohT_ready)
                            pick(i, h)
                    body(0, False)
                    with pe.Fori(1, ITERS - 1) as i:
                        body(i, False)
                    body(ITERS - 1, True)

                @block.scalar
                def _(act):
                    looped(act, ITERS, lambda i, first: [copy_turned(act, i, h, turned, ohT_ready, ohT_used)
                                                         for h in range(2)])

                @block.gpsimd
                def _(pool):
                    with pool.Fori(0, ITERS) as i:
                        for h in range(2):
                            pool.wait_ge(scaled[h], i * 4 + 4)
                            pool.sem_inc(poolt, 1)
                            for j in range(G):
                                pool.indirect_dma_start(
                                    msg_d, bass.IndirectOffsetOnAxis(ap=ixr[h][:, j:j + 1], axis=0),
                                    rows[h][:, j, 0:MW], None, bounds_check=SLOTS - 1, oob_is_err=False).then_inc(sent[h], 16)
                    for h in range(2):
                        pool.wait_ge(sent[h], 16 * G * ITERS)

        poolt = sem("pool_tick")
        Hflat = sums[1]

        def layer0_src_pass():
            msg_in, oh_ready, used = ([sem(f"{n}{h}") for h in range(2)] for n in ("msg_in", "oh_ready", "used"))
            summed, added = sem("summed"), sem("added")
            msg_v = msg_d.rearrange("(k p j) w -> k p (j w)", p=P, j=G)
            with nc.Block() as block:
                @block.sync
                def _(sp):
                    def body(i, first):
                        for h in range(2):
                            if not first:
                                sp.wait_ge(used[h], i)
                            sp.dma_start(rows[h][:, :, :].rearrange("p j w -> p (j w)")[:, 0:G * MW],
                                         msg_v[bass.ds(2 * i + h, 1)].rearrange("k p w -> (k p) w")).then_inc(msg_in[h], 16)
                    looped(sp, ITERS, body)

                sent_msgs = [rows[h][:, :, :].rearrange("p j w -> p (j w)")[:, 0:G * MW].rearrange("p (j w) -> p j w", w=MW)
                        for h in range(2)]

                @block.vector
                def _(dve):
                    def prepare(i, h):
                        dve.wait_ge(msg_in[h], i * 16 + 16)
                        if later(i):
                            dve.wait_ge(used[h], i)
                        onehot(dve, h, sent_msgs[h][:, :, D:D + 1]).then_inc(oh_ready[h], 1)

                    prepare(0, 0)

                    def body(i, last):
                        for h in range(2):
                            nh, step = ahead(h)
                            if not (last and h == 1):
                                prepare(i + step, nh)
                            add_sums(dve, i, h, acc_of_s, D, summed, added)
                    body(0, False)
                    with dve.Fori(1, ITERS - 1) as i:
                        body(i, False)
                    body(ITERS - 1, True)

                @block.tensor
                def _(pe):
                    def body(i, first):
                        for h in range(2):
                            pe.wait_ge(oh_ready[h], i + 1)
                            sum_tiles(pe, i, h, oh[h], sent_msgs[h], D, summed, added, used)
                    looped(pe, ITERS, body)

        def gather_rows(pool, i, h, first, table, w, msg_ready, ix_ready, rows_in):
            if not first:
                pool.wait_ge(msg_ready[h], i)
                pool.sem_inc(poolt, 1)
            nc.gpsimd.tensor_copy(ixr[h][:, :], src_ix[:, bass.ds(i * 2 * G + h * G, G)]).then_inc(ix_ready, 1)
            pool.wait_ge(ix_ready, i * 2 + h + 1)
            pool.sem_inc(poolt, 1)
            for j in range(G):
                pool.indirect_dma_start(rows[h][:, j, 0:w], None, table,
                                        bass.IndirectOffsetOnAxis(ap=ixr[h][:, j:j + 1], axis=0)).then_inc(rows_in[h], 16)

        def gat_pass(table, heads):
            w, c = D + heads, D // heads

            def picks(h):
                return bank[2 + h][:, 0:G * 6 * heads]

            rows_in, oh_ready, used, msg_ready, ohb_ready, turned, ohbT_ready, picked = (
                [sem(f"{n}{h}") for h in range(2)] for n in
                ("rows_in", "oh_ready", "used", "msg_ready", "ohb_ready", "turned", "ohbT_ready", "picked"))
            ix_ready, logits, probs, zst, summed, added = (
                sem(n) for n in ("ix_ready", "logits", "probs", "zst", "summed", "added"))
            with nc.Block() as block:
                @block.gpsimd
                def _(pool):
                    looped(pool, ITERS, lambda i, first: [gather_rows(pool, i, h, first, table, w, msg_ready, ix_ready, rows_in)
                                                          for h in range(2)])

                @block.vector
                def _(dve):
                    def prepare(i, h):
                        if later(i):
                            dve.wait_ge(used[h], i)
                        onehot(dve, h, dloc[:, bass.ds(i * 2 * G + h * G, G)].unsqueeze(2)).then_inc(oh_ready[h], 1)

                    prepare(0, 0)

                    def body(i, first):
                        for h in range(2):
                            nh, step = ahead(h)
                            prepare(i + step, nh)
                            dve.wait_ge(rows_in[h], i * (16 * G) + 16 * G)
                            dve.wait_ge(picked[h], i + 1)
                            zz = z[h][:, :, 0:heads]
                            ps = pk[:, :, 0:2 * heads]
                            st = Steps(dve, zst, i * 8 + h * 4)
                            st.then(nc.vector.tensor_reduce(ps, picks(h).rearrange("p (j t k) -> p j k t", j=G, t=3),
                                                            AX.X, ALU.add))
                            st.then(nc.vector.tensor_tensor(zz, rows[h][:, :, D:w], ps[:, :, 0:heads], ALU.add))
                            st.then(nc.vector.scalar_tensor_tensor(zz, zz, SLOPE, zz, ALU.mult, ALU.max))
                            st.then(nc.vector.tensor_tensor(zz, zz, ps[:, :, heads:2 * heads], ALU.subtract))
                            nc.vector.tensor_scalar(zz, zz, 0.0, None, ALU.min).then_inc(logits, 1)
                            dve.wait_ge(probs, i * 2 + h + 1)
                            split = "p j (k c) -> p j k c"
                            nc.vector.tensor_tensor(msgs[h][:, :, 0:D].rearrange(split, c=c),
                                                    rows[h][:, :, 0:D].rearrange(split, c=c),
                                                    msgs[h][:, :, D:w].unsqueeze(3).to_broadcast([P, G, heads, c]),
                                                    ALU.mult).then_inc(msg_ready[h], 1)
                            if h or not first:
                                add_sums(dve, *before(i, h), acc_of_d, w, summed, added)
                    looped(dve, ITERS, body)
                    add_sums(dve, ITERS - 1, 1, acc_of_d, w, summed, added)

                @block.scalar
                def _(act):
                    def narrow(i, h):
                        act.wait_ge(oh_ready[h], i + 1)
                        if later(i):
                            act.wait_ge(turned[h], i)
                        nc.scalar.copy(ohb[h], oh[h].rearrange("p j n -> p (j n)")).then_inc(ohb_ready[h], 1)

                    def copy_turned_b(i, h):
                        act.wait_ge(turned[h], i + 1)
                        if later(i):
                            act.wait_ge(picked[h], i)
                        nc.scalar.copy(ohbT[h], bank[h][:, :].bitcast(BF16)).then_inc(ohbT_ready[h], 1)

                    narrow(0, 0)
                    copy_turned_b(0, 0)

                    def body(i, first):
                        for h in range(2):
                            nh, step = ahead(h)
                            narrow(i + step, nh)
                            act.wait_ge(logits, i * 2 + h + 1)
                            if not first:
                                act.wait_ge(used[h], i)
                            nc.scalar.activation(msgs[h][:, :, D:w], z[h][:, :, 0:heads], ACT.Exp, bias=zero1[:, :]) \
                                .then_inc(probs, 1)
                            copy_turned_b(i + step, nh)
                    looped(act, ITERS, body)

                @block.tensor
                def _(pe):
                    def turn(i, h):
                        pe.wait_ge(ohb_ready[h], i + 1)
                        if later(i):
                            pe.wait_ge(ohbT_ready[h], i)
                        tb_ = bank[h][:, :].bitcast(BF16)
                        for j in range(G):
                            ins = nc.tensor.transpose(tb_[:, j * P:(j + 1) * P], ohb[h][:, j * P:(j + 1) * P], ident_b[:, :])
                        ins.then_inc(turned[h], 1)

                    def pick(i, h):
                        at = node_tiles(mybir.EngineType.PE, tile_of_d, i, h)
                        if later(i):
                            pe.wait_ge(msg_ready[h], i)
                        pe.wait_ge(ohbT_ready[h], i + 1)
                        for j in range(G):
                            ins = nc.tensor.matmul(picks(h)[:, j * 6 * heads:(j + 1) * 6 * heads],
                                                   ohbT[h][:, j * P:j * P + P], adc[:, bass.ds(at[j] * (6 * heads), 6 * heads)],
                                                   start=True, stop=True)
                        ins.then_inc(picked[h], 1)

                    turn(0, 0)
                    pick(0, 0)

                    def body(i, first):
                        for h in range(2):
                            nh, step = ahead(h)
                            turn(i + step, nh)
                            pe.wait_ge(msg_ready[h], i + 1)
                            sum_tiles(pe, i, h, oh[h], msgs[h], w, summed, added, used)
                            pick(i + step, nh)
                    looped(pe, ITERS, body)

        def mlp_pass(table):
            w = D + 1
            rec_in, rows_in, oh_ready, used, ones_in, hid_ready = ([sem(f"{n}{h}") for h in range(2)] for n in
                                                          ("rec_in", "rows_in", "oh_ready", "used", "ones_in", "hid_ready"))
            pe_tick = sem("pe_tick")
            ix_ready, turned, at_ready, prod, added_rows, summed, added = (
                sem(n) for n in ("ix_ready", "turned", "at_ready", "prod", "added_rows", "summed", "added"))
            rec_v = rec_d.rearrange("(k p j) w -> k p (j w)", p=P, j=G)
            with nc.Block() as block:
                @block.gpsimd
                def _(pool):
                    looped(pool, ITERS, lambda i, first: [gather_rows(pool, i, h, first, table, D, hid_ready, ix_ready, rows_in)
                                                          for h in range(2)])

                @block.sync
                def _(sp):
                    def body(i, first):
                        for h in range(2):
                            if not first:
                                sp.wait_ge(turned, i * 4 + 2 * h - 2)
                            sp.dma_start(recs[h][:, :, :].rearrange("p j w -> p (j w)"),
                                         rec_v[bass.ds(2 * i + h, 1)].rearrange("k p w -> (k p) w")).then_inc(rec_in[h], 16)
                    looped(sp, ITERS, body)

                @block.vector
                def _(dve):
                    def prepare(i, h):
                        if later(i):
                            dve.wait_ge(used[h], i)
                        onehot(dve, h, dloc[:, bass.ds(i * 2 * G + h * G, G)].unsqueeze(2)).then_inc(oh_ready[h], 1)

                    def body(i, first):
                        for h in range(2):
                            dve.wait_ge(rows_in[h], i * (16 * G) + 16 * G)
                            for n in range(2):
                                dve.wait_ge(prod, i * 4 + 2 * h + n + 1)
                                hv = rows[h][:, 4 * n:4 * n + 4, 0:D]
                                nc.vector.tensor_tensor(hv, hv, bank[2 + n][:, :].rearrange("p (j f) -> p j f", f=D),
                                                        ALU.add).then_inc(added_rows, 1)
                            if h or not first:
                                add_sums(dve, *before(i, h), acc_of_d, w, summed, added)
                            nh, step = ahead(h)
                            prepare(i + step, nh)
                    for h in range(2):
                        nc.vector.memset(msgs[h][:, :, D:D + 8], 1.0).then_inc(ones_in[h], 1)
                        dve.wait_ge(ones_in[h], 1)
                    prepare(0, 0)
                    looped(dve, ITERS, body)
                    add_sums(dve, ITERS - 1, 1, acc_of_d, w, summed, added)

                @block.scalar
                def _(act):
                    def copy_attr(i, h):
                        if later(i) or h:
                            act.wait_ge(prod, i * 4 + 2 * h)
                        for n in range(2):
                            act.wait_ge(turned, i * 4 + 2 * h + n + 1)
                            nc.scalar.copy(ohT[0][0:EA, n * 512:n * 512 + 512], bank[n][0:EA, :]).then_inc(at_ready, 1)

                    copy_attr(0, 0)

                    def body(i, last):
                        for h in range(2):
                            nh, step = ahead(h)
                            if not (last and h == 1):
                                copy_attr(i + step, nh)
                            act.wait_ge(added_rows, i * 4 + 2 * h + 2)
                            if later(i):
                                act.wait_ge(used[h], i)
                            nc.scalar.activation(msgs[h][:, :, 0:D], rows[h][:, :, 0:D], ACT.Relu, bias=zero1[:, :]) \
                                .then_inc(hid_ready[h], 1)
                    body(0, False)
                    with act.Fori(1, ITERS - 1) as i:
                        body(i, False)
                    body(ITERS - 1, True)

                @block.tensor
                def _(pe):
                    for h in range(2):
                        pe.wait_ge(ones_in[h], 1)

                    def edge_part(i, h):
                        pe.wait_ge(rec_in[h], i * 16 + 16)
                        if later(i) or h:
                            pe.wait_ge(at_ready, i * 4 + 2 * h)
                        pe.sem_inc(pe_tick, 1)
                        for j in range(G):
                            ins = nc.tensor.transpose(bank[j // 4][0:EA, (j % 4) * P:(j % 4) * P + P],
                                                      recs[h][:, j, 0:EA], ident[:, :])
                            if j % 4 == 3:
                                ins.then_inc(turned, 1)
                        if later(i) or h:
                            pe.wait_ge(added_rows, i * 4 + 2 * h)
                        for j in range(G):
                            if j % 4 == 0:
                                pe.wait_ge(at_ready, i * 4 + 2 * h + j // 4 + 1)
                            ins = nc.tensor.matmul(bank[2 + j // 4][:, (j % 4) * P:(j % 4) * P + P],
                                                   ohT[0][0:EA, j * P:j * P + P], wmbT[:, :], start=True, stop=True)
                            if j % 4 == 3:
                                ins.then_inc(prod, 1)

                    edge_part(0, 0)

                    def body(i, last):
                        for h in range(2):
                            nh, step = ahead(h)
                            if not (last and h == 1):
                                edge_part(i + step, nh)
                            pe.wait_ge(oh_ready[h], i + 1)
                            pe.wait_ge(hid_ready[h], i + 1)
                            sum_tiles(pe, i, h, oh[h], msgs[h], w, summed, added, used)
                    body(0, False)
                    with pe.Fori(1, ITERS - 1) as i:
                        body(i, False)
                    body(ITERS - 1, True)

        def store_table(table, src, w):
            stored = sem("stored")
            with nc.Block() as block:
                @block.sync
                def _(sp):
                    sp.dma_start(table.rearrange("(b p) w -> p b w", p=P), src[:, :, 0:w]).then_inc(stored, 16)
                    sp.wait_ge(stored, 16)

        small = {n: sb(n, [P, NBP, 8]) for n in ("a_src", "a_dst", "p_self")}
        gmax, gmax_all = sb("gmax", [P, 8]), sb("gmax_all", [P, 8])

        def gat_prepare(att_s, att_d, heads, table):
            c = D // heads
            a_s, a_d, p_s = (small[n][:, :, 0:heads] for n in ("a_src", "a_dst", "p_self"))
            Y4 = Y[:, :, :].rearrange("p b (k c) -> p (b k) c", c=c)
            flat = {n: sb_small(n, heads) for n in ("a_src", "a_dst")}

            def work(d, v, then):
                for name, att in (("a_src", att_s), ("a_dst", att_d)):
                    then(v.tensor_tensor(Y[:, :, :], H[:, :, 0:D], per_col(att), ALU.mult))
                    then(v.tensor_reduce(flat[name], Y4, AX.X, ALU.add))
                then(v.tensor_copy(ACC[:, :, 0:D], H[:, :, 0:D]))
                then(v.tensor_copy(ACC[:, :, D:D + heads], flat3("a_src", heads)))
                then(v.tensor_reduce(gmax[:, 0:heads], flat3("a_src", heads).rearrange("p b k -> p k b"), AX.X, ALU.max))
            Dense(work)
            store_table(table, ACC, D + heads)
            reduced = sem("reduced")
            with nc.Block() as block:
                @block.gpsimd
                def _(pool):
                    pool.partition_all_reduce(gmax_all[:, 0:heads], gmax[:, 0:heads], P, bass.bass_isa.ReduceOp.max) \
                        .then_inc(reduced, 1)
                    pool.wait_ge(reduced, 1)
            as3, ad3, ps3 = flat3("a_src", heads), flat3("a_dst", heads), flat3("p_self", heads)
            adc3, rest = (Yflat[:, n * NBP * 16:n * NBP * 16 + NBP * 2 * heads].rearrange("p (b k) -> p b k", k=2 * heads)
                          for n in range(2))
            parts = adc[:, 0:NBP * 6 * heads].rearrange("p (b t k) -> p b t k", t=3, k=2 * heads)
            bound = adc3[:, :, heads:2 * heads]

            def work2(d, v, then):
                then(v.tensor_copy(adc3[:, :, 0:heads], ad3))
                then(v.tensor_tensor(bound, ad3, gmax_all[:, 0:heads].unsqueeze(1).to_broadcast([P, NBP, heads]), ALU.add))
                then(v.scalar_tensor_tensor(bound, bound, SLOPE, bound, ALU.mult, ALU.max))
                then(v.tensor_tensor(ps3, as3, ad3, ALU.add))
                then(v.scalar_tensor_tensor(ps3, ps3, SLOPE, ps3, ALU.mult, ALU.max))
                then(v.tensor_tensor(ps3, ps3, bound, ALU.subtract))
                d.act(ps3, ps3, ACT.Exp)
                A4 = ACC[:, :, 0:D].rearrange("p b (k c) -> p b k c", c=c)
                then(v.tensor_tensor(A4, H[:, :, 0:D].rearrange("p b (k c) -> p b k c", c=c),
                                     ps3.unsqueeze(3).to_broadcast([P, NBP, heads, c]), ALU.mult))
                then(v.tensor_copy(ACC[:, :, D:D + heads], ps3))
                then(v.tensor_copy(parts[:, :, 0, :], adc3))
                then(v.tensor_tensor(rest, adc3, parts[:, :, 0, :], ALU.subtract))
                then(v.tensor_copy(parts[:, :, 1, :], rest))
                then(v.tensor_tensor(rest, rest, parts[:, :, 1, :], ALU.subtract))
                then(v.tensor_copy(parts[:, :, 2, :], rest))
                then(v.memset(H[:, :, :], 0.0))
            Dense(work2)

        def sb_small(n, heads):
            return small[n][:, :, :].rearrange("p b k -> p (b k)")[:, 0:NBP * heads]

        def flat3(n, heads):
            return sb_small(n, heads).rearrange("p (b k) -> p b k", k=heads)

        def gat_finish(v, then, heads, bias, o):
            c = D // heads
            both_sums(v, then, D + heads)
            then(v.tensor_copy(flat3("p_self", heads), ACC[:, :, D:D + heads]))
            if heads == 8:
                then(v.tensor_scalar(flat3("p_self", heads), flat3("p_self", heads), 1e-16, None, ALU.add))
            then(v.reciprocal(flat3("p_self", heads), flat3("p_self", heads)))
            then(v.tensor_tensor(o.rearrange("p b (k c) -> p b k c", c=c), ACC[:, :, 0:D].rearrange("p b (k c) -> p b k c", c=c),
                                 flat3("p_self", heads).unsqueeze(3).to_broadcast([P, NBP, heads, c]), ALU.mult))
            then(v.tensor_tensor(o, o, per_col(bias), ALU.add))

        def relu(v, then, t):
            then(v.tensor_scalar(t, t, 0.0, None, ALU.max))

        Xa, Ha, Ya = X[:, :, :], H[:, :, 0:D], Y[:, :, :]
        XIa = XI[:, :, :]

        def start0(d, v, then):
            then(v.memset(one1[:, :], 1.0))
            d.norm(v, then, Ha, Xa)
            relu(v, then, Ha)
            then(v.memset(ACC[:, :, :], 0.0))
        with stage_of_work():
            Dense(start0)
            layer0_dst_pass()
            Dense(lambda d, v, then: then(v.memset(H[:, :, :], 0.0)))
            layer0_src_pass()
            Dense(lambda d, v, then: both_sums(v, then, D))
            node_product(Y, [ACC], [mat["Wi1"][0]], mat["Wi2"][0], "softplus", bi1_col)

            def end0(d, v, then):
                then(v.tensor_tensor(Ya, Ya, per_col(bn_scale), ALU.mult))
                then(v.tensor_tensor(Ya, Ya, per_col(bn_shift), ALU.add))
                then(v.tensor_tensor(Xa, Xa, Ya, ALU.add))
                if stop > 0:
                    d.norm(v, then, XIa, Xa)
                    relu(v, then, XIa)
            Dense(end0)

        if stop > 0:
            for l in range(2):
                with stage_of_work():
                    node_product(H, [XI], [mat[f"W1_{l}"][0]])
                    gat_prepare(vec["L1_gnn_att_src", l][0], vec["L1_gnn_att_dst", l][0], 1, tab_d[l])
                    gat_pass(tab_d[l], 1)

                    def end1(d, v, then):
                        gat_finish(v, then, 1, vec["L1_gnn_bias", l][0], Ya)
                        then(v.tensor_tensor(Ya, Ya, XIa, ALU.add))
                        d.norm(v, then, XIa, Ya)
                        then(v.tensor_tensor(XIa, XIa, per_col(vec["L1_gnn_gamma", l][0]), ALU.mult))
                        then(v.tensor_tensor(XIa, XIa, per_col(vec["L1_gnn_beta", l][0]), ALU.add))
                        if l == 1:
                            then(v.tensor_tensor(Xa, Xa, XIa, ALU.add))
                            d.norm(v, then, XIa, Xa)
                            relu(v, then, XIa)
                    Dense(end1)

        if stop > 1:
            with stage_of_work():
                node_product(H, [XI], [wmaT])

                def start2(d, v, then):
                    then(v.tensor_tensor(Ha, Ha, per_col(cm_row), ALU.add))
                    then(v.memset(ACC[:, :, :], 0.0))
                Dense(start2)
                store_table(tab_d[2], H, D)
                Dense(lambda d, v, then: then(v.memset(H[:, :, :], 0.0)))
                mlp_pass(tab_d[2])

                def mean2(d, v, then):
                    both_sums(v, then, D + 1)
                    deg = ACC[:, :, D:D + 1]
                    then(v.tensor_scalar(mean[:, :].unsqueeze(2), deg, 1.0, None, ALU.max))
                    then(v.reciprocal(mean[:, :], mean[:, :]))
                    then(v.tensor_tensor(ACC[:, :, 0:D], ACC[:, :, 0:D], per_tile(mean[:, :]), ALU.mult))
                    then(v.tensor_tensor(var[:, :].unsqueeze(2), deg, mean[:, :].unsqueeze(2), ALU.mult))
                Dense(mean2)
                node_product(Y, [ACC], [wm2T])

                def bias2(d, v, then):
                    then(v.tensor_tensor(Ha, per_col(vec["L2_gnn_bm2"][0]), per_tile(var[:, :]), ALU.mult))
                    then(v.tensor_tensor(Ya, Ya, Ha, ALU.add))
                Dense(bias2)
                node_product(H, [XI, Y], [wuaT, wubT], wu2T, "relu", cu_col)

                def end2(d, v, then):
                    then(v.tensor_tensor(Ha, Ha, per_col(vec["L2_gnn_bu2"][0]), ALU.add))
                    then(v.tensor_tensor(Ha, Ha, XIa, ALU.add))
                    d.norm(v, then, Ya, Ha)
                    then(v.tensor_tensor(Ya, Ya, per_col(vec["L2_gnn_ln_g"][0]), ALU.mult))
                    then(v.tensor_tensor(Ya, Ya, per_col(vec["L2_gnn_ln_b"][0]), ALU.add))
                    then(v.tensor_tensor(Xa, Xa, Ya, ALU.add))
                    d.norm(v, then, XIa, Xa)
                    relu(v, then, XIa)
                Dense(end2)

        if stop > 2:
            with stage_of_work():
                node_product(H, [XI], [mat["W3"][0]])
                gat_prepare(vec["L3_gnn_att_src"][0], vec["L3_gnn_att_dst"][0], 8, tab_d[3])
                gat_pass(tab_d[3], 8)

                def end3(d, v, then):
                    gat_finish(v, then, 8, vec["L3_gnn_bias"][0], Ya)
                    then(v.tensor_tensor(Xa, Xa, Ya, ALU.add))
                Dense(end3)

        written = sem("written")
        with nc.Block() as block:
            @block.sync
            def _(sp):
                sp.dma_start(out[0:FULL * P, :].rearrange("(b p) f -> p b f", p=P), X[:, 0:FULL, :]).then_inc(written, 16)
                sp.dma_start(out[FULL * P:N, :], X[0:REST, FULL, :]).then_inc(written, 16)
                sp.wait_ge(written, 32)


STOP = 4


def kernel(**inputs):
    import numpy as _np
    import concourse.bacc as _bacc
    from concourse import mybir as _mybir
    from concourse.bass_utils import run_bass_kernel_spmd as _run

    nc = _bacc.Bacc("TRN2", target_bir_lowering=False, num_devices=1)
    arrays, args = {}, {}
    for name, value in inputs.items():
        if name == "edge_weight1":
            continue
        v = _np.ascontiguousarray(value)
        arrays[f"in_{name}_dram"] = v
        args[name] = nc.dram_tensor(f"in_{name}_dram", v.shape, _mybir.dt.from_np(v.dtype), kind="ExternalInput").ap()
    out = nc.dram_tensor("out_0_dram", (N, D), F32, kind="ExternalOutput").ap()
    gnn(nc, args, out, STOP)
    r = _run(nc, [arrays], core_ids=[0])
    return r.results[0]["out_0_dram"]
```

```python
from contextlib import ExitStack, contextmanager

import concourse.bass as bass
from concourse import mybir

F32 = mybir.dt.float32
I32 = mybir.dt.int32
BF16 = mybir.dt.bfloat16
ALU = mybir.AluOpType
ACT = mybir.ActivationFunctionType
AX = mybir.AxisListType

P = 128
N = 6250
E = 100000
D = 128
EA = 64
NF = 64
NODE_TILES = -(-N // P)
NB2 = NODE_TILES + NODE_TILES % 2
GN = 4
NG = -(-NODE_TILES // GN)
NBP = GN * NG
FULL = N // P
REST = N - FULL * P
EP, EC = 125, 800
G = 8
MAX_TILES = (E + NODE_TILES * (P - 1)) // P
NT = -(-MAX_TILES // (2 * G)) * 2 * G
ITERS = NT // (2 * G)
SLOTS = NT * P
NTP = NT + G
SC = 16
CHUNKS = 5
CH = EC // CHUNKS
CR = CH // (2 * SC)
RW = 72
R_DLOC, R_SRC, R_POS, R_W, R_SLOC = 64, 65, 66, 67, 68
AW = D + 8
MW = 132
SKIP = 1 << 20
LN_EPS = 1e-5
BN_EPS = 1e-3
CUTOFF = 8.0
SLOPE = 0.2
PI = 3.141592653589793


class Steps:

    def __init__(self, eng, sem, start=0):
        self.eng, self.sem, self.start, self.n = eng, sem, start, 0

    def then(self, ins):
        ins.then_inc(self.sem, 1)
        self.n += 1
        self.eng.wait_ge(self.sem, self.start + self.n)


def later(i):
    return not (isinstance(i, int) and i == 0)


def looped(eng, n, body):
    body(0, True)
    with eng.Fori(1, n) as i:
        body(i, False)


def gnn(nc, a, out):
    ctx = ExitStack()
    names = [0]

    def sem(name):
        names[0] += 1
        return nc.alloc_semaphore(name=f"{name}_{names[0]}")

    @contextmanager
    def stage_of_work():
        before = nc.snapshot_sems()
        yield
        nc.clear_and_free_semaphores(nc.allocated_since(before))
        nc.all_engine_barrier()

    def dram(name, shape, dt=F32):
        return nc.dram_tensor(name, shape, dt, kind="Internal").ap()

    def sbuf(stack, name, shape, dt=F32):
        names[0] += 1
        return stack.enter_context(nc.sbuf_tensor(f"{name}_{names[0]}", shape, dt))

    rec_d = dram("edge_records", [SLOTS, RW])
    msg_d = dram("layer0_messages", [SLOTS, MW])
    tab_d = [dram(f"node_table{i}", [NBP * P, w]) for i, w in enumerate((D + 1, D + 1, D, D + 8))]

    with ctx:
        def sb(name, shape, dt=F32):
            return sbuf(ctx, name, shape, dt)

        bank = [ctx.enter_context(nc.psum_tensor(f"bank{i}", [P, 512], F32)) for i in range(8)]

        iota_row = sb("iota_row", [P, P])
        ident = sb("ident", [P, P])
        ident_b = sb("ident_b", [P, P], BF16)
        zero1 = sb("zero1", [P, 1])
        dloc = sb("dloc", [P, NTP])
        src_ix = sb("src_ix", [P, NT + 2 * G], I32)
        tile_of_d = sb("tile_of_d", [1, NTP], I32)
        acc_of_d = sb("acc_of_d", [1, NTP], I32)
        acc_of_s = sb("acc_of_s", [1, NTP], I32)
        X = sb("X", [P, NBP, D])
        ACC = sb("ACC", [P, NBP, AW])
        H = sb("H", [P, NBP, AW])
        XI = sb("XI", [P, NBP, D])
        Y = sb("Y", [P, NBP, D])
        edge_buf = sb("edge_buf", [P, 2 * G * (AW + RW)])
        rows = [edge_buf[:, h * G * AW:(h + 1) * G * AW].rearrange("p (j w) -> p j w", j=G) for h in range(2)]
        recs = [edge_buf[:, 2 * G * AW + h * G * RW:2 * G * AW + (h + 1) * G * RW].rearrange("p (j w) -> p j w", j=G)
                for h in range(2)]
        mean, var, shift = sb("mean", [P, NBP]), sb("var", [P, NBP]), sb("shift", [P, NBP])
        stats = sb("stats", [P, NBP, 6])
        vec = {}
        for v in ("L0_gnn_bi2", "L0_gnn_gamma", "L0_gnn_beta", "L0_gnn_mov_mean", "L0_gnn_mov_var",
                  "L2_gnn_bm1", "L2_gnn_bm2", "L2_gnn_bu2", "L2_gnn_ln_g", "L2_gnn_ln_b", "L3_gnn_bias"):
            vec[v] = (sb(v, [P, D]), a[v])
        for v in ("L1_gnn_bias", "L1_gnn_gamma", "L1_gnn_beta"):
            for l in range(2):
                vec[v, l] = (sb(f"{v}{l}", [P, D]), a[v][l, :])
        mat = {"Wi1": (sb("Wi1", [P, D]), a["L0_gnn_Wi1"]), "Wi2": (sb("Wi2", [P, D]), a["L0_gnn_Wi2"]),
               }
        heads_of = (1, 1, 8)
        wx = [sb(f"wx{l}", [P, D + 2 * k]) for l, k in enumerate(heads_of)]
        att_col = [[sb(f"att{l}{q}", [P, 1]) for q in range(2)] for l in range(3)]
        bi1_col = sb("bi1_col", [P, 1])
        bu1_col = sb("bu1_col", [P, 1])
        gs_col = sb("gs_col", [64, 1])
        wmaT, wmbT, wmcT = sb("wmaT", [P, D]), sb("wmbT", [64, D]), sb("wmcT", [64, D])
        wm2T, wuaT, wubT, wucT = sb("wm2T", [P, D]), sb("wuaT", [P, D]), sb("wubT", [P, D]), sb("wucT", [64, D])
        wu2T = sb("wu2T", [P, D])
        cm_row = sb("cm_row", [P, D])
        cu_col = sb("cu_col", [P, 1])
        bn_scale = sb("bn_scale", [P, D])
        bn_shift = sb("bn_shift", [P, D])

        def count_stats(v, b, t):
            return v.bn_stats(stats[:, b, :], t[:, b, :])

        def finish_stats(v, then, root):
            mean_e, mean_o = stats[:, :, 1], stats[:, :, 4]
            then(v.tensor_tensor(var[:, :], mean_e, mean_o, ALU.subtract))
            then(v.tensor_tensor(var[:, :], var[:, :], var[:, :], ALU.mult))
            then(v.scalar_tensor_tensor(var[:, :], var[:, :], D / 4.0, stats[:, :, 2], ALU.mult, ALU.add))
            then(v.tensor_tensor(var[:, :], var[:, :], stats[:, :, 5], ALU.add))
            then(v.tensor_scalar(var[:, :], var[:, :], 1.0 / D, LN_EPS, ALU.mult, ALU.add))
            then(v.tensor_tensor(mean[:, :], mean_e, mean_o, ALU.add))
            then(v.tensor_scalar(mean[:, :], mean[:, :], 0.5, None, ALU.mult))
            root(var[:, :], var[:, :], ACT.Sqrt)
            then(v.reciprocal(var[:, :], var[:, :]))
            then(v.scalar_tensor_tensor(shift[:, :], mean[:, :], -1.0, var[:, :], ALU.mult, ALU.mult))

        def apply_norm(v, then, tiles, o, i):
            for b in tiles:
                ins = v.tensor_scalar(o[:, b, :], i[:, b, :], mean[:, b:b + 1], var[:, b:b + 1], ALU.subtract, ALU.mult)
            then(ins)

        def norm(v, then, root, o, i):
            for b in range(NBP):
                ins = count_stats(v, b, i)
            then(ins)
            finish_stats(v, then, root)
            apply_norm(v, then, range(NBP), o, i)

        def relu(v, then, t):
            then(v.tensor_scalar(t, t, 0.0, None, ALU.max))

        def setup():
            arenas = [[t[:, :, :].rearrange("p b f -> p (b f)"), 0] for t in (Y, XI, H)]

            def carve(arena, shape, dt=F32):
                n = 1
                for d in shape[1:]:
                    n *= d
                words = n if dt != BF16 else n // 2
                view = arena[0][0:shape[0], arena[1]:arena[1] + words]
                arena[1] += words
                assert arena[1] <= arena[0].shape[1]
                view = view if dt == F32 else view.bitcast(dt)
                return view if len(shape) == 2 else view.rearrange("p (b f) -> p b f", f=shape[2])

            def tb(shape, dt=F32):
                n = shape[1] * (shape[2] if len(shape) > 2 else 1) // (1 if dt != BF16 else 2)
                for arena in arenas:
                    if arena[1] + n <= arena[0].shape[1]:
                        return carve(arena, shape, dt)
                raise ValueError("setup's scratch is full")

            acc_arena = [ACC[:, :, :].rearrange("p b f -> p (b f)"), 0]
            meta = carve(acc_arena, [EP, EC, 5])
            row = [carve(acc_arena, [EP, EC], I32) for q in range(2)]
            pad_msg = carve(acc_arena, [P, G * MW])
            arenas.append(acc_arena)
            wf2 = tb([P, NF, NF])
            node = [tb([EP, EC], I32) for q in range(2)]
            keys, slots = tb([EP, 2, EC], BF16), tb([EP, 2, EC])
            key, pos = ([t[:, q, :] for q in range(2)] for t in (keys, slots))
            equal = [slots[:, q, :].bitcast(BF16)[:, h * EC:(h + 1) * EC] for q in range(2) for h in range(2)]
            eqs, cums = [tb([EP, 2, CH], BF16) for h in range(2)], [tb([EP, 2, CH]) for h in range(2)]
            wt, cosine = tb([EP, EC]), tb([EP, EC])
            th = [tb([EP, EC]) for h in range(2)]
            diag = [tb([P, P]) for h in range(2)]
            tri, ones = tb([P, P]), tb([P, P])
            iota_t = tb([64, NTP])
            reached = tb([64, NTP])
            pad_rec = tb([P, G * RW])
            count = [tb([EP, NB2]) for q in range(2)]
            ntile = [tb([P, NB2]) for q in range(2)]
            ntile_i = [tb([P, NB2], I32) for q in range(2)]
            upto = [tb([P, NB2]) for q in range(2)]
            upto_col = [tb([64, 1]) for q in range(2)]
            offs = tb([P, 2, NB2])
            off = [offs[:, q, :] for q in range(2)]
            acc_i = [acc_of_d, acc_of_s]
            wf1, bf1 = tb([P, NF]), tb([P, NF])
            fscale, fbias = tb([P, NF]), tb([P, NF])
            bf2, wf2_sum, bf2_sum = tb([P, NF]), tb([P, NF]), tb([P, 1])
            wm1, wm2, wu1, wu2 = tb([P, 256]), tb([P, D]), tb([P, 320]), tb([P, D])
            half_pi = tb([P, 1])
            gs_b = tb([64, D])
            head_of = tb([P, 8])
            att = [tb([P, 2 * k]) for k in heads_of]
            wT = [tb([P, D]) for l in range(3)]

            rec = [edge_buf[0:EP, h * SC * RW:(h + 1) * SC * RW].rearrange("p (c w) -> p c w", w=RW) for h in range(2)]
            ixs = [edge_buf[0:EP, 2 * SC * RW + h * SC:2 * SC * RW + (h + 1) * SC].bitcast(I32) for h in range(2)]
            with stage_of_work():
                attr_in, meta_in, scattered = ([sem(f"{n}{h}") for h in range(2)] for n in ("attr_in", "meta_in", "scattered"))
                tick, cleared, root_asked, root_done, chunk_ready, chunk_steps, x_in, msgs_padded = (
                    sem(n) for n in ("tick", "cleared", "root_asked", "root_done", "chunk_ready", "chunk_steps", "x_in",
                                     "msgs_padded"))
                attr_v = a["edge_attr_64"].rearrange("(p c) w -> p c w", c=EC)
                nodes_in = sem("nodes_in")
                consts, pads, edges_in, weights_in, filled, steps_v, steps_p = (
                    sem("consts"), sem("pads"), sem("edges_in"), sem("weights_in"), sem("filled"),
                    sem("steps_v"), sem("steps_p"))
                loop_a, loop_b, loop_c, counts_ready, offs_in_psum = (
                    sem(n) for n in ("loop_a", "loop_b", "loop_c", "counts_ready", "offs_in_psum"))
                filt_ready, cos_ready, upto_ready, upto_turned, reached_ready, tiles_counted = (
                    sem(n) for n in ("filt_ready", "cos_ready", "upto_ready", "upto_turned", "reached_ready", "tiles_counted"))
                tanh_ready, tanh_used = ([sem(f"{n}{h}") for h in range(2)] for n in ("tanh_ready", "tanh_used"))
                masked_s, slots_s, heads_in, att_ready, filter_taken = (
                    sem(n) for n in ("masked_s", "slots_s", "heads_in", "att_ready", "filter_taken"))
                wT_ready, wT_copied, cvec_ready, steps_a = sem("wT_ready"), sem("wT_copied"), sem("cvec_ready"), sem("steps_a")
                x_zero, bnv, bns = sem("x_zero"), sem("bnv"), sem("bns")
                NW = len(vec) + len(mat) + 7 + 9
                with nc.Block() as block:
                    @block.sync
                    def _(sp):
                        sp.dma_start(node[0][:, :], a["dst"].rearrange("(p c) -> p c", c=EC)).then_inc(nodes_in, 16)
                        sp.dma_start(node[1][:, :], a["src"].rearrange("(p c) -> p c", c=EC)).then_inc(nodes_in, 16)
                        sp.dma_start(wt, a["edge_weight"].rearrange("(p c) -> p c", c=EC)).then_inc(edges_in, 16)
                        sp.dma_start(wf1, a["L0_gnn_Wf1"].to_broadcast([P, NF])).then_inc(edges_in, 16)
                        sp.dma_start(bf1, a["L0_gnn_bf1"].unsqueeze(0).to_broadcast([P, NF])).then_inc(edges_in, 16)
                        sp.dma_start(bf2, a["L0_gnn_bf2"].unsqueeze(0).to_broadcast([P, NF])).then_inc(edges_in, 16)
                        sp.dma_start(wf2, a["L0_gnn_Wf2"].unsqueeze(0).to_broadcast([P, NF, NF])).then_inc(edges_in, 16)
                        for t, v in vec.values():
                            sp.dma_start(t[:, :], v.unsqueeze(0).to_broadcast([P, D])).then_inc(weights_in, 16)
                        for t, v in mat.values():
                            sp.dma_start(t[:, :], v).then_inc(weights_in, 16)
                        for l in range(3):
                            sp.dma_start(wx[l][:, 0:D], a["L1_gnn_W"][l] if l < 2 else a["L3_gnn_W"]).then_inc(weights_in, 16)
                            for q, v in enumerate(("att_src", "att_dst")):
                                v = a["L1_gnn_" + v][l, :] if l < 2 else a["L3_gnn_" + v].rearrange("h c -> (h c)")
                                sp.dma_start(att_col[l][q][:, :], v.rearrange("(p a) -> p a", a=1)).then_inc(weights_in, 16)
                        for t, v in ((bi1_col, a["L0_gnn_bi1"]), (bu1_col, a["L2_gnn_bu1"]), (gs_col, a["L2_gnn_global_state"])):
                            sp.dma_start(t[:, :], v.rearrange("(p a) -> p a", a=1)).then_inc(weights_in, 16)
                        for t, v in ((wm1, "L2_gnn_Wm1"), (wm2, "L2_gnn_Wm2"), (wu1, "L2_gnn_Wu1"), (wu2, "L2_gnn_Wu2")):
                            sp.dma_start(t[:, :], a[v]).then_inc(weights_in, 16)
                        sp.wait_ge(x_zero, 1)
                        sp.dma_start(X[:, 0:FULL, :], a["x"][0:FULL * P, :].rearrange("(b p) f -> p b f", p=P)).then_inc(x_in, 16)
                        sp.dma_start(X[0:REST, FULL, :], a["x"][FULL * P:N, :]).then_inc(x_in, 16)
                        sp.wait_ge(pads, 1)
                        sp.dma_start(rec_d.rearrange("(k p j) w -> p k (j w)", p=P, j=G),
                                     pad_rec[:, :].unsqueeze(1).to_broadcast([P, NT // G, G * RW])).then_inc(filled, 16)

                        msg_v = msg_d.rearrange("(k p j) w -> p k (j w)", p=P, j=G)
                        scatter_rounds = EC // (2 * SC)
                        part = NT // G // scatter_rounds
                        left = NT // G - part * scatter_rounds

                        def pad_messages(k, n):
                            sp.dma_start(msg_v[:, bass.ds(k, n), :],
                                         pad_msg.unsqueeze(1).to_broadcast([P, n, G * MW])).then_inc(msgs_padded, 16)

                        def body(i, first):
                            if not first:
                                pad_messages(i * part, part)
                            for h in range(2):
                                if not first:
                                    sp.wait_ge(scattered[h], i * (16 * SC))
                                sp.dma_start(rec[h][:, :, 0:EA],
                                             attr_v[:, bass.ds((2 * i + h) * SC, SC), :]).then_inc(attr_in[h], 16)
                        looped(sp, scatter_rounds, body)
                        pad_messages(0, part)
                        if left:
                            pad_messages(scatter_rounds * part, left)
                        sp.wait_ge(msgs_padded, 16 * (scatter_rounds + (1 if left else 0)))

                    @block.gpsimd
                    def _(pool):
                        st = Steps(pool, steps_p)
                        st.then(pool.memset(ident[:, :], 0.0))
                        st.then(pool.affine_select(out=ident[:, :], in_=ident[:, :], compare_op=ALU.not_equal, fill=1.0,
                                                   base=0, pattern=[[-1, P]], channel_multiplier=1))
                        st.then(pool.tensor_copy(ident_b[:, :], ident[:, :]))
                        st.then(pool.memset(tri[:, :], 1.0))
                        st.then(pool.affine_select(out=tri[:, :], in_=tri[:, :], compare_op=ALU.is_gt, fill=0.0,
                                                   base=0, pattern=[[1, P]], channel_multiplier=-1))
                        st.then(pool.memset(ones[:, :], 1.0))
                        st.then(pool.memset(dloc[:, NT:NTP], -1.0))
                        st.then(pool.memset(src_ix[:, NT:NT + 2 * G], 0))
                        st.then(pool.iota(iota_row[:, :], [[1, P]], base=0, channel_multiplier=0,
                                          allow_small_or_imprecise_dtypes=True))
                        st.then(pool.iota(iota_t[:, :], [[1, NTP]], base=0, channel_multiplier=0,
                                          allow_small_or_imprecise_dtypes=True))
                        st.then(pool.memset(zero1[:, :], 0.0))
                        pool.sem_inc(consts, 1)
                        pr = pad_rec[:, :].rearrange("p (j w) -> p j w", w=RW)
                        pm = pad_msg[:, :].rearrange("p (j w) -> p j w", w=MW)
                        st.then(pool.memset(pad_rec[:, :], 0.0))
                        st.then(pool.memset(pad_msg[:, :], 0.0))
                        st.then(pool.memset(pr[:, :, R_DLOC:R_DLOC + 1], -1.0))
                        st.then(pool.memset(pr[:, :, R_SLOC:R_SLOC + 1], -1.0))
                        st.then(pool.memset(pr[:, :, R_POS:R_POS + 1], float(SKIP)))
                        st.then(pool.memset(pm[:, :, D:D + 1], -1.0))
                        pool.sem_inc(pads, 1)
                        st.then(pool.memset(X[:, :, :], 0.0))
                        pool.sem_inc(x_zero, 1)
                        c = D // 8
                        st.then(pool.memset(head_of[:, :], 1.0))
                        st.then(pool.affine_select(out=head_of[:, :], in_=head_of[:, :], compare_op=ALU.is_ge, fill=0.0,
                                                   base=0, pattern=[[-c, 8]], channel_multiplier=1))
                        st.then(pool.affine_select(out=head_of[:, :], in_=head_of[:, :], compare_op=ALU.is_ge, fill=0.0,
                                                   base=c - 1, pattern=[[c, 8]], channel_multiplier=-1))
                        pool.sem_inc(heads_in, 1)

                        def body(i, first):
                            for h in range(2):
                                pool.wait_ge(loop_b, i * 12 + 8)
                                nc.gpsimd.tensor_tensor(cums[h][:, 1, :], cums[h][:, 1, :], eqs[h][:, 1, :], ALU.mult).then_inc(masked_s, 1)
                                pool.wait_ge(masked_s, i * 2 + h + 1)
                                if not (first and h == 0):
                                    pool.wait_ge(slots_s, i * 2 + h)
                                nc.gpsimd.tensor_tensor(pos[1][:, 0:CH], pos[1][:, 0:CH], cums[h][:, 1, :], ALU.add) \
                                    .then_inc(slots_s, 1)
                        looped(pool, NB2 // 2, body)

                        pool.wait_ge(filled, 16)
                        with pool.Fori(0, EC // (2 * SC)) as i:
                            for h in range(2):
                                pool.wait_ge(attr_in[h], i * 16 + 16)
                                pool.sem_inc(tick, 1)
                                pool.wait_ge(meta_in[h], i * 2 + 2)
                                pool.sem_inc(tick, 1)
                                for j in range(SC):
                                    pool.indirect_dma_start(rec_d, bass.IndirectOffsetOnAxis(ap=ixs[h][:, j:j + 1], axis=0),
                                                            rec[h][:, j, :], None).then_inc(scattered[h], 16)
                        for h in range(2):
                            pool.wait_ge(scattered[h], 16 * SC * (EC // (2 * SC)))

                    @block.tensor
                    def _(pe):
                        pe.wait_ge(consts, 1)

                        def body(i, first, last=False):
                            for h in range(2):
                                pe.wait_ge(tanh_ready[h], i * 2 + 2)
                                for q in range(2):
                                    ins = nc.tensor.matmul(bank[6 + q][0:EP, 0:EC // 2], diag[h][0:EP, 0:EP],
                                                           th[h][:, q * (EC // 2):(q + 1) * (EC // 2)],
                                                           start=first and h == 0, stop=last and h == 1)
                                ins.then_inc(tanh_used[h], 1)
                        pe.wait_ge(counts_ready, 1)
                        for q in range(2):
                            nc.tensor.matmul(bank[q][:, 0:NB2], tri[0:EP, :], count[q], start=True, stop=True)
                            nc.tensor.matmul(bank[2 + q][:, 0:NB2], ones[0:EP, :], count[q], start=True,
                                             stop=True).then_inc(offs_in_psum, 1)
                        body(0, True)
                        with pe.Fori(1, NF // 2 - 1) as i:
                            body(i, False)
                        body(NF // 2 - 1, False, True)
                        pe.wait_ge(weights_in, 16 * NW)
                        for n, (w, lo, hi) in enumerate(((wm1, 0, 128), (wm1, 128, 192), (wm1, 192, 256), (wm2, 0, 128))):
                            nc.tensor.transpose(bank[4][0:hi - lo, n * P:n * P + P], w[:, lo:hi], ident[:, :]).then_inc(wT_ready, 1)
                        for n, (w, lo, hi) in enumerate(((wu1, 0, 128), (wu1, 128, 256), (wu1, 256, 320), (wu2, 0, 128))):
                            nc.tensor.transpose(bank[5][0:hi - lo, n * P:n * P + P], w[:, lo:hi], ident[:, :]).then_inc(wT_ready, 1)
                        pe.wait_ge(wT_copied, 1)
                        for l in range(3):
                            nc.tensor.transpose(bank[4][:, l * P:l * P + P], wx[l][:, 0:D], ident[:, :]).then_inc(wT_ready, 1)
                        pe.wait_ge(wT_copied, 2)
                        pe.wait_ge(att_ready, 1)
                        for l in range(3):
                            nc.tensor.matmul(bank[5][:, 16 * l:16 * l + 2 * heads_of[l]], wT[l], att[l], start=True,
                                             stop=True).then_inc(wT_ready, 1)
                        pe.wait_ge(filter_taken, 1)
                        pe.wait_ge(wT_copied, 1)
                        nc.tensor.matmul(bank[6][:, 0:P], gs_b, wmcT[:, :], start=True, stop=True)
                        nc.tensor.matmul(bank[7][:, 0:1], wucT[:, :], gs_col[:, :], start=True, stop=True).then_inc(cvec_ready, 1)
                        pe.wait_ge(upto_ready, 1)
                        for q in range(2):
                            nc.tensor.transpose(bank[q][0:NB2, 0:P], upto[q], ident[:, :]).then_inc(upto_turned, 1)
                        for q in range(2):
                            pe.wait_ge(reached_ready, q + 1)
                            for n in range(2):
                                nc.tensor.matmul(bank[2 + n][0:1, 0:NTP // 2], ones[0:NODE_TILES, 0:1],
                                                 reached[0:NODE_TILES, n * (NTP // 2):(n + 1) * (NTP // 2)],
                                                 start=True, stop=True).then_inc(tiles_counted, 1)

                    @block.scalar
                    def _(act):
                        st = Steps(act, steps_a)
                        act.wait_ge(filt_ready, 1)
                        def body(i, first):
                            for h in range(2):
                                if not first:
                                    act.wait_ge(tanh_used[h], i)
                                f = i * 2 + h
                                nc.scalar.activation(diag[h], ident[:, :], ACT.Copy, scale=wf2_sum[:, bass.ds(f, 1)]) \
                                    .then_inc(tanh_ready[h], 1)
                                nc.scalar.activation(th[h], wt, ACT.Tanh, bias=fbias[0:EP, bass.ds(f, 1)],
                                                     scale=fscale[0:EP, bass.ds(f, 1)]).then_inc(tanh_ready[h], 1)
                        looped(act, NF // 2, body)
                        st.then(nc.scalar.activation(cosine, cosine, ACT.Sin, bias=half_pi[0:EP, :], scale=-PI / CUTOFF))
                        act.sem_inc(cos_ready, 1)
                        act.wait_ge(wT_ready, 8)
                        for n, (t, r) in enumerate(((wmaT, P), (wmbT, 64), (wmcT, 64), (wm2T, P))):
                            st.then(nc.scalar.copy(t[:, :], bank[4][0:r, n * P:n * P + P]))
                        for n, (t, r) in enumerate(((wuaT, P), (wubT, P), (wucT, 64), (wu2T, P))):
                            st.then(nc.scalar.copy(t[:, :], bank[5][0:r, n * P:n * P + P]))
                        st.then(nc.scalar.copy(gs_b, gs_col[:, 0:1].to_broadcast([64, D])))
                        act.sem_inc(wT_copied, 1)
                        act.wait_ge(wT_ready, 11)
                        for l in range(3):
                            st.then(nc.scalar.copy(wT[l], bank[4][:, l * P:l * P + P]))
                        act.sem_inc(wT_copied, 1)

                        def rounds(lo, hi):
                            def body(i, first):
                                for h in range(2):
                                    if first:
                                        act.wait_ge(cleared, 2)
                                    else:
                                        act.wait_ge(scattered[h], i * (16 * SC))
                                    nc.scalar.copy(rec[h][:, :, EA:EA + 5], meta[:, bass.ds((2 * i + h) * SC, SC), :]) \
                                        .then_inc(meta_in[h], 1)
                                    nc.scalar.copy(ixs[h], row[0][:, bass.ds((2 * i + h) * SC, SC)]).then_inc(meta_in[h], 1)
                            if lo == 0:
                                body(0, True)
                            with act.Fori(max(lo, 1), hi) as i:
                                body(i, False)

                        for c in range(CHUNKS - 1):
                            act.wait_ge(chunk_ready, c + 1)
                            rounds(c * CR, (c + 1) * CR)
                        act.wait_ge(wT_ready, 14)
                        for l in range(3):
                            st.then(nc.scalar.copy(wx[l][:, D:D + 2 * heads_of[l]], bank[5][:, 16 * l:16 * l + 2 * heads_of[l]]))
                        act.wait_ge(bnv, 1)
                        st.then(nc.scalar.activation(bn_scale[:, :], bn_scale[:, :], ACT.Sqrt, bias=zero1[:, :]))
                        act.sem_inc(bns, 1)
                        act.wait_ge(chunk_ready, CHUNKS)
                        rounds((CHUNKS - 1) * CR, CHUNKS * CR - 2)
                        act.wait_ge(root_asked, 1)
                        nc.scalar.activation(var[:, :], var[:, :], ACT.Sqrt, bias=zero1[:, :]).then_inc(root_done, 1)
                        rounds(CHUNKS * CR - 2, CHUNKS * CR)

                    @block.vector
                    def _(dve):
                        v = nc.vector
                        st = Steps(dve, steps_v)
                        for h in range(2):
                            v.memset(rec[h][:, :, EA:RW], 0.0).then_inc(cleared, 1)
                        dve.wait_ge(nodes_in, 32)
                        dve.wait_ge(consts, 1)
                        for q in range(2):
                            st.then(v.tensor_single_scalar(row[q][:, :], node[q][:, :], 7, ALU.logical_shift_right))
                            st.then(v.tensor_copy(key[q][:, :], row[q][:, :]))
                            st.then(v.tensor_single_scalar(row[q][:, :], node[q][:, :], P - 1, ALU.bitwise_and))
                            st.then(v.tensor_copy(meta[:, :, 4 * q:4 * q + 1], row[q][:, :].unsqueeze(2)))
                        st.then(v.tensor_copy(meta[:, :, 1:2], node[1].unsqueeze(2)))

                        def count_round(i, first):
                            for h in range(2):
                                for q in range(2):
                                    if not first:
                                        dve.wait_ge(loop_a, i * 4 + 2 * h + q - 3)
                                    b = i * 2 + h
                                    v.tensor_scalar(equal[2 * h + q], key[q], iota_row[0:EP, bass.ds(b, 1)], 0.0,
                                                    ALU.is_equal, ALU.add, accum_out=count[q][:, bass.ds(b, 1)]).then_inc(loop_a, 1)
                        looped(dve, NB2 // 2, count_round)
                        dve.wait_ge(loop_a, NB2 * 2)
                        dve.sem_inc(counts_ready, 1)
                        st.then(v.memset(slots, 0.0))
                        dve.wait_ge(edges_in, 16 * 5)
                        st.then(v.tensor_scalar(fscale, wf1, 2.0 / CUTOFF, None, ALU.mult))
                        st.then(v.tensor_tensor(fbias, bf1, wf1, ALU.subtract))
                        st.then(v.tensor_reduce(wf2_sum, wf2, AX.X, ALU.add))
                        st.then(v.tensor_reduce(bf2_sum, bf2, AX.X, ALU.add))
                        st.then(v.memset(half_pi, PI / 2))
                        st.then(v.tensor_scalar(cosine, wt, CUTOFF, None, ALU.min))
                        dve.sem_inc(filt_ready, 1)
                        dve.wait_ge(offs_in_psum, 2)
                        for q in range(2):
                            st.then(v.tensor_scalar(ntile_i[q], bank[2 + q][:, 0:NB2], float(P - 1), None, ALU.add))
                            st.then(v.tensor_single_scalar(ntile_i[q], ntile_i[q], 7, ALU.logical_shift_right))
                            st.then(v.tensor_copy(ntile[q], ntile_i[q]))
                            st.then(v.tensor_tensor_scan(upto[q], ntile[q], ntile[q], 0.0, ALU.add, ALU.bypass))
                            st.then(v.tensor_tensor(ntile[q], upto[q], ntile[q], ALU.subtract))
                            st.then(v.tensor_scalar(ntile[q], ntile[q], float(P), -1.0, ALU.mult, ALU.add))
                            st.then(v.tensor_tensor(off[q], ntile[q], bank[q][:, 0:NB2], ALU.add))
                        dve.sem_inc(upto_ready, 1)

                        def slot_round(i, c, count, base, helped):
                            at = bass.ds(c * CH, CH)
                            mine = slice(0, 1 if helped else 2)

                            def step(n, work):
                                for h in range(2):
                                    work(h, eqs[h], cums[h], bass.ds(i * 2 + h, 1))
                                dve.wait_ge(count, base + n)

                            def equal_to(h, eq, cum, b):
                                if helped and later(i):
                                    dve.wait_ge(slots_s, i * 2 + h - 1)
                                v.tensor_scalar(eq, keys[:, :, at], iota_row[0:EP, b], None, ALU.is_equal).then_inc(count, 1)

                            def running_count(h, eq, cum, b):
                                for q in range(2):
                                    v.tensor_tensor_scan(cum[:, q, :], eq[:, q, :], eq[:, q, :], offs[0:EP, q, b],
                                                         ALU.add, ALU.bypass).then_inc(count, 1)

                            def carry_on(h, eq, cum, b):
                                v.tensor_scalar(offs[0:EP, :, b], cum[:, :, CH - 1:CH], 0.0, None, ALU.add).then_inc(count, 1)

                            def mask(h, eq, cum, b):
                                v.tensor_tensor(cum[:, mine, :], cum[:, mine, :], eq[:, mine, :], ALU.mult).then_inc(count, 1)

                            def gather_slots(h, eq, cum, b):
                                v.tensor_tensor(slots[:, mine, at], slots[:, mine, at], cum[:, mine, :], ALU.add) \
                                    .then_inc(count, 1)
                                dve.wait_ge(count, base + 11 + h)

                            step(2, equal_to)
                            step(6, running_count)
                            step(8, carry_on)
                            step(10, mask)
                            step(12, gather_slots)

                        def slot_rows(c, then):
                            at = bass.ds(c * CH, CH)
                            for q in range(2):
                                ci, ei, r = cums[0][:, q, :].bitcast(I32), cums[1][:, q, :].bitcast(I32), row[q][:, at]
                                then(v.tensor_scalar(ci, pos[q][:, at], 0.0, None, ALU.add))
                                then(v.tensor_scalar(r, ci, -P * G, None, ALU.bitwise_and))
                                then(v.tensor_scalar(ei, ci, P - 1, 3, ALU.bitwise_and, ALU.logical_shift_left))
                                then(v.tensor_tensor(r, r, ei, ALU.bitwise_or))
                                then(v.tensor_scalar(ei, ci, 7, G - 1, ALU.logical_shift_right, ALU.bitwise_and))
                                then(v.tensor_tensor(r, r, ei, ALU.bitwise_or))
                            then(v.tensor_scalar(meta[:, at, 2:3], row[1][:, at].unsqueeze(2), 0.0, None, ALU.add))
                            dve.sem_inc(chunk_ready, 1)

                        unroll = 5
                        assert NB2 // 2 % unroll == 0
                        looped(dve, NB2 // 2 // unroll,
                               lambda i, first: [slot_round(i * unroll + k, 0, loop_b, (i * unroll + k) * 12, True)
                                                 for k in range(unroll)])
                        dve.wait_ge(slots_s, NB2)
                        dve.wait_ge(cos_ready, 1)
                        st.then(v.tensor_scalar(cosine, cosine, 0.5, 0.5, ALU.mult, ALU.add))
                        st.then(v.scalar_tensor_tensor(cosine, wt, CUTOFF, cosine, ALU.is_le, ALU.mult))
                        for h in range(2):
                            dve.wait_ge(tanh_used[h], NF // 2)
                        for q in range(2):
                            at = slice(q * (EC // 2), (q + 1) * (EC // 2))
                            st.then(v.scalar_tensor_tensor(meta[:, at, 3:4], bank[6 + q][0:EP, 0:EC // 2].unsqueeze(2),
                                                           bf2_sum[0:EP, 0:1], cosine[:, at].unsqueeze(2), ALU.add, ALU.mult))
                        slot_rows(0, st.then)
                        with dve.Fori(1, CHUNKS) as c:
                            with dve.Fori(0, NB2 // 2) as i:
                                slot_round(i, c, loop_c, c * (NB2 * 6) + i * 12 - NB2 * 6, False)
                            slot_rows(c, Steps(dve, chunk_steps, c * 13 - 13).then)
                        dve.sem_inc(filter_taken, 1)
                        dve.wait_ge(weights_in, 16 * NW)
                        dve.wait_ge(heads_in, 1)
                        for l in range(3):
                            for q in range(2):
                                k = heads_of[l]
                                if k == 1:
                                    st.then(v.tensor_copy(att[l][:, q:q + 1], att_col[l][q][:, :]))
                                else:
                                    st.then(v.tensor_scalar(att[l][:, q * k:(q + 1) * k], head_of, att_col[l][q][:, 0:1],
                                                            None, ALU.mult))
                        dve.sem_inc(att_ready, 1)
                        st.then(v.tensor_scalar(bn_scale[:, :], vec["L0_gnn_mov_var"][0][:, :], BN_EPS, None, ALU.add))
                        dve.sem_inc(bnv, 1)
                        dve.wait_ge(bns, 1)
                        st.then(v.reciprocal(bn_scale[:, :], bn_scale[:, :]))
                        st.then(v.tensor_tensor(bn_scale[:, :], bn_scale[:, :], vec["L0_gnn_gamma"][0][:, :], ALU.mult))
                        st.then(v.tensor_tensor(bn_shift[:, :], vec["L0_gnn_bi2"][0][:, :], vec["L0_gnn_mov_mean"][0][:, :], ALU.subtract))
                        st.then(v.tensor_tensor(bn_shift[:, :], bn_shift[:, :], bn_scale[:, :], ALU.mult))
                        st.then(v.tensor_tensor(bn_shift[:, :], bn_shift[:, :], vec["L0_gnn_beta"][0][:, :], ALU.add))
                        dve.wait_ge(cvec_ready, 1)
                        st.then(v.tensor_tensor(cm_row[:, :], bank[6][:, 0:P], vec["L2_gnn_bm1"][0][:, :], ALU.add))
                        st.then(v.tensor_tensor(cu_col[:, :], bank[7][:, 0:1], bu1_col[:, :], ALU.add))
                        dve.wait_ge(upto_turned, 2)
                        for q in range(2):
                            st.then(v.tensor_copy(upto_col[q][0:NB2, :], bank[q][0:NB2, 0:1]))
                            st.then(v.tensor_scalar(reached[0:NB2, :], iota_t[0:NB2, :], upto_col[q][0:NB2, :], None, ALU.is_ge))
                            dve.sem_inc(reached_ready, 1)
                            dve.wait_ge(tiles_counted, 2 * q + 2)
                            for n in range(2):
                                at = slice(n * (NTP // 2), (n + 1) * (NTP // 2))
                                counted = bank[2 + n][0:1, 0:NTP // 2]
                                if q == 0:
                                    st.then(v.tensor_scalar(tile_of_d[:, at], counted, float(NODE_TILES - 1), None, ALU.min))
                                st.then(v.tensor_scalar(acc_i[q][:, at], counted, float(NODE_TILES - 1), float(AW),
                                                        ALU.min, ALU.mult))
                        dve.wait_ge(x_in, 32)
                        dve.wait_ge(filled, 16)

                        def root(o, i, f):
                            dve.sem_inc(root_asked, 1)
                            dve.wait_ge(root_done, 1)
                        norm(v, st.then, root, H[:, :, 0:D], X[:, :, :])
                        relu(v, st.then, H[:, :, 0:D])

        setup()

        def per_col(t):
            return t[:, :].unsqueeze(1).to_broadcast([P, NBP, D])


        def columns(t, n):
            return t[:, :].unsqueeze(1).to_broadcast([P, n, D])

        class Dense:

            def __init__(self, work, roots=0, on_pool=None):
                steps, pool_steps, pool_done, asked, done = (
                    sem(n) for n in ("dense_steps", "pool_steps", "pool_done", "asked", "done"))
                self.pool_done, self.asked, self.done, self.n = pool_done, asked, done, 0
                with nc.Block() as block:
                    @block.vector
                    def _(dve):
                        self.dve = dve
                        work(self, nc.vector, Steps(dve, steps).then)

                    if on_pool:
                        @block.gpsimd
                        def _(pool):
                            on_pool(pool, nc.gpsimd, Steps(pool, pool_steps).then)
                            pool.sem_inc(pool_done, 1)

                    @block.scalar
                    def _(act):
                        for n in range(roots):
                            act.wait_ge(asked, n + 1)
                            nc.scalar.activation(var[:, :], var[:, :], ACT.Sqrt, bias=zero1[:, :]).then_inc(done, 1)

            def root(self, o, i, f):
                self.n += 1
                self.dve.sem_inc(self.asked, 1)
                self.dve.wait_ge(self.done, self.n)

            def wait_pool(self):
                self.dve.wait_ge(self.pool_done, 1)

        rows_w = [t[:, :, :].rearrange("p j w -> p (j w)") for t in rows]
        hid = rows_w[1][:, 0:GN * P]
        stT = [t[:, :, :].rearrange("p j w -> p (j w)")[:, 0:GN * P] for t in recs]

        def group(g):
            return slice(g * GN, (g + 1) * GN)

        def product_psum(g, pair, cols):
            return bank[4 + 2 * (g % 2) + pair][:, 0:2 * cols].rearrange("p (j f) -> p j f", f=cols)

        def take_product(dve, v, then, g, prod, taken, cols, after):
            for q in range(2):
                dve.wait_ge(prod, 2 * g + q + 1)
                after(v, then, g * GN + 2 * q, product_psum(g, q, cols))
            dve.sem_inc(taken, 1)

        def node_product(srcs, ws, after, before=None, normed=None, cols=D, w2=None, bias=None, store=None,
                         behind=None):
            k = len(srcs)
            norm_done, ready, turned, turned_sb, in_hid, hid_ready, prod, taken, steps, stored = (
                sem(n) for n in ("norm_done", "ready", "turned", "turned_sb", "in_hid", "hid_ready", "prod", "taken", "steps", "stored"))
            turns = 2 if k == 1 else 1

            with nc.Block() as block:
                @block.vector
                def _(dve):
                    v, then = nc.vector, Steps(dve, steps).then

                    def prepare(g):
                        if before:
                            if normed:
                                dve.wait_ge(norm_done, g + 1)
                            before(v, then, g)
                            dve.sem_inc(ready, 1)
                    prepare(0)
                    prepare(1)
                    for g in range(NG):
                        if g + 2 < NG:
                            prepare(g + 2)
                        take_product(dve, v, then, g, prod, taken, cols, after)

                if store:
                    @block.sync
                    def _(sp):
                        table, rows_out, words = store
                        for g in range(NG):
                            sp.wait_ge(taken, g + 1)
                            sp.dma_start(table[g * GN * P:(g + 1) * GN * P, :].rearrange("(b p) w -> p b w", p=P),
                                         rows_out[:, group(g), 0:words]).then_inc(stored, 16)
                        sp.wait_ge(stored, 16 * NG)

                if behind:
                    @block.gpsimd
                    def _(pool):
                        for g in range(NG):
                            pool.wait_ge(taken, g + 1)
                            behind(g)

                @block.tensor
                def _(pe):
                    def turn(g):
                        if before:
                            pe.wait_ge(ready, g + 1)
                        elif normed:
                            pe.wait_ge(norm_done, g + 1)
                        for n in range(k):
                            if g >= turns:
                                pe.wait_ge(turned_sb, (g - turns) * k + n + 1)
                            buf = n if k > 1 else g % 2
                            for j in range(GN):
                                ins = nc.tensor.transpose(bank[buf][:, j * P:j * P + P], srcs[n][:, g * GN + j, 0:D], ident[:, :])
                            ins.then_inc(turned, 1)

                    def first(g):
                        pe.wait_ge(turned_sb, g * k + k)
                        if g:
                            pe.wait_ge(hid_ready, g)
                        for n in range(k):
                            ins = nc.tensor.matmul(bank[2][:, :], ws[n][:, :], stT[n if k > 1 else g % 2],
                                                   start=(n == 0), stop=(n == k - 1))
                        ins.then_inc(in_hid, 1)

                    def last(g):
                        if w2 is None:
                            pe.wait_ge(turned_sb, g * k + k)
                        else:
                            pe.wait_ge(hid_ready, g + 1)
                        if g >= 2:
                            pe.wait_ge(taken, g - 1)
                        for j in range(GN):
                            o = product_psum(g, j // 2, cols)[:, j % 2, :]
                            if w2 is not None:
                                ins = nc.tensor.matmul(o, hid[:, j * P:j * P + P], w2[:, :], start=True, stop=True)
                            for n in range(k if w2 is None else 0):
                                ins = nc.tensor.matmul(o, stT[n if k > 1 else g % 2][:, j * P:j * P + P], ws[n][:, 0:cols],
                                                       start=(n == 0), stop=(n == k - 1))
                            if j % 2:
                                ins.then_inc(prod, 1)

                    turn(0)
                    for g in range(NG):
                        if w2 is not None:
                            first(g)
                        if g + 1 < NG:
                            turn(g + 1)
                        last(g)

                @block.scalar
                def _(act):
                    def copy(g):
                        for n in range(k):
                            act.wait_ge(turned, g * k + n + 1)
                            if g >= turns:
                                if w2 is None:
                                    act.wait_ge(prod, 2 * (g - turns) + 2)
                                else:
                                    act.wait_ge(in_hid, g - turns + 1)
                            buf = n if k > 1 else g % 2
                            nc.scalar.copy(stT[buf][:, :], bank[buf][:, :]).then_inc(turned_sb, 1)

                    if normed:
                        for g in range(2):
                            normed(g).then_inc(norm_done, 1)
                    copy(0)
                    for g in range(NG):
                        if normed and g + 2 < NG:
                            normed(g + 2).then_inc(norm_done, 1)
                        if w2 is not None:
                            act.wait_ge(in_hid, g + 1)
                            if g:
                                act.wait_ge(prod, 2 * g)
                            nc.scalar.activation(hid[:, :], bank[2][:, :], ACT.Relu, bias=bias[:, 0:1]).then_inc(hid_ready, 1)
                        if g + 1 < NG:
                            copy(g + 1)

        def softplus_product(src, w1, bias, w2, before, after):
            flat = [t[:, :, :].rearrange("p b f -> p (b f)") for t in (XI, Y)]
            words = GN * P
            ready, turned, turned_sb, in_hid, z_out, absolute, exps, logs, halves, prod, taken, steps = (
                sem(n) for n in ("ready", "turned", "turned_sb", "in_hid", "z_out", "absolute", "exps", "logs", "halves",
                                 "prod", "taken", "steps"))
            half_groups = (0, NG // 2, NG)
            half = [slice(half_groups[n] * words, half_groups[n + 1] * words) for n in range(2)]
            with nc.Block() as block:
                @block.vector
                def _(dve):
                    v, then = nc.vector, Steps(dve, steps).then

                    def prepare(g):
                        before(v, then, g)
                        dve.sem_inc(ready, 1)
                    prepare(0)
                    prepare(1)
                    for g in range(NG):
                        if g + 2 < NG:
                            prepare(g + 2)
                        dve.wait_ge(in_hid, g + 1)
                        v.tensor_scalar(flat[0][:, g * words:(g + 1) * words], bank[2 + g % 2][:, :], bias[:, 0:1], None,
                                        ALU.add).then_inc(z_out, 1)
                    dve.wait_ge(z_out, NG)
                    for n in range(2):
                        dve.wait_ge(logs, n + 1)
                        v.scalar_tensor_tensor(flat[0][:, half[n]], flat[0][:, half[n]], 0.0, flat[1][:, half[n]],
                                               ALU.max, ALU.add).then_inc(halves, 1)
                    dve.wait_ge(halves, 2)
                    for g in range(NG):
                        take_product(dve, v, then, g, prod, taken, D, after)

                @block.tensor
                def _(pe):
                    def turn(g):
                        pe.wait_ge(ready, g + 1)
                        if g >= 2:
                            pe.wait_ge(turned_sb, g - 1)
                        for j in range(GN):
                            ins = nc.tensor.transpose(bank[g % 2][:, j * P:j * P + P], src[:, g * GN + j, 0:D], ident[:, :])
                        ins.then_inc(turned, 1)
                    turn(0)
                    for g in range(NG):
                        if g + 1 < NG:
                            turn(g + 1)
                        pe.wait_ge(turned_sb, g + 1)
                        if g >= 2:
                            pe.wait_ge(z_out, g - 1)
                            pe.wait_ge(absolute, g - 1)
                        nc.tensor.matmul(bank[2 + g % 2][:, :], w1[:, :], stT[g % 2], start=True, stop=True).then_inc(in_hid, 1)
                    for g in range(NG):
                        pe.wait_ge(halves, 1 if g < half_groups[1] else 2)
                        if g >= 2:
                            pe.wait_ge(taken, g - 1)
                        for j in range(GN):
                            at = g * words + j * P
                            ins = nc.tensor.matmul(product_psum(g, j // 2, D)[:, j % 2, :], flat[0][:, at:at + P], w2[:, :],
                                                   start=True, stop=True)
                            if j % 2:
                                ins.then_inc(prod, 1)

                @block.scalar
                def _(act):
                    def copy(g):
                        act.wait_ge(turned, g + 1)
                        if g >= 2:
                            act.wait_ge(in_hid, g - 1)
                        nc.scalar.copy(stT[g % 2][:, :], bank[g % 2][:, :]).then_inc(turned_sb, 1)
                    copy(0)
                    for g in range(NG):
                        if g + 1 < NG:
                            copy(g + 1)
                        act.wait_ge(in_hid, g + 1)
                        act.wait_ge(z_out, g + 1)
                        nc.scalar.activation(flat[1][:, g * words:(g + 1) * words], bank[2 + g % 2][:, :], ACT.Abs,
                                             bias=bias[:, 0:1]).then_inc(absolute, 1)
                    act.wait_ge(absolute, NG)
                    for n in range(2):
                        nc.scalar.activation(flat[1][:, half[n]], flat[1][:, half[n]], ACT.Exp, bias=zero1[:, :], scale=-1.0) \
                            .then_inc(exps, 1)
                    for n in range(2):
                        act.wait_ge(exps, n + 1)
                        nc.scalar.activation(flat[1][:, half[n]], flat[1][:, half[n]], ACT.Ln, bias=one1[:, :]).then_inc(logs, 1)

        one1 = sb("one1", [P, 1])

        Yflat = Y[:, :, :].rearrange("p b f -> p (b f)")
        oh = [Yflat[:, h * G * P:(h + 1) * G * P].rearrange("p (j n) -> p j n", j=G) for h in range(2)]
        ohT = [Yflat[:, (2 + h) * G * P:(3 + h) * G * P] for h in range(2)]
        msgs = [Yflat[:, 4 * G * P + h * G * AW:4 * G * P + (h + 1) * G * AW].rearrange("p (j w) -> p j w", j=G)
                for h in range(2)]
        ixr = [sb(f"ixr{h}", [P, G], I32) for h in range(2)]
        z = [sb(f"z{h}", [P, G, 8]) for h in range(2)]
        adc = sb("adc", [P, NBP * 48], BF16)
        ohb = [ohT[h].bitcast(BF16)[:, 0:G * P] for h in range(2)]
        ohbT = [ohT[h].bitcast(BF16)[:, G * P:2 * G * P] for h in range(2)]
        pk = sb("pk", [P, G, 16])

        def onehot(h, loc):
            return nc.vector.tensor_tensor(oh[h][:, :, :], iota_row[:, :].unsqueeze(1).to_broadcast([P, G, P]),
                                           loc.to_broadcast([P, G, P]), ALU.is_equal)

        sums = [ACC[:, :, :].rearrange("p b w -> p (b w)"), H[:, :, :].rearrange("p b w -> p (b w)")]

        def node_tiles(engine, tiles, i, h):
            return nc.values_load_multi_w_load_instructions(
                tiles[0:1, bass.ds(i * 2 * G + h * G, G)], engines=[engine], min_val=0,
                max_val=(NODE_TILES - 1) * (AW if tiles is not tile_of_d else 1),
                skip_runtime_bounds_check_because="setup cuts them at NODE_TILES - 1")[1]

        def sum_slot(j):
            return bank[4 + j // 2][:, (j % 2) * AW:(j % 2) * AW + AW]

        def sum_tiles(pe, i, h, onehots, messages, w, summed, added, used, midway=None):
            for j in range(G):
                if j == G // 2 and midway:
                    midway()
                if j % 2 == 0 and (later(i) or h):
                    pe.wait_ge(added, i * 2 * G + h * G - G + j + 2)
                ins = nc.tensor.matmul(sum_slot(j)[:, 0:w], onehots[:, j, :], messages[:, j, 0:w], start=True, stop=True)
                if j % 2:
                    ins.then_inc(summed, 1)
            pe.wait_ge(summed, (i * 2 + h + 1) * (G // 2))
            pe.sem_inc(used[h], 1)

        def before(i, h):
            return (i, 0) if h else (i - 1, 1)

        def add_sums(dve, i, h, tiles, w, summed, added):
            at = node_tiles(mybir.EngineType.DVE, tiles, i, h)
            for j in range(G):
                if j % 2 == 0:
                    dve.wait_ge(summed, (i * 2 + h) * (G // 2) + j // 2 + 1)
                t = i * 2 * G + h * G + j
                acc = sums[j % 2][:, bass.ds(at[j], w)]
                if j >= 2 or h or later(i):
                    dve.wait_ge(added, t - 1)
                nc.vector.tensor_tensor(acc, acc, sum_slot(j)[:, 0:w], ALU.add).then_inc(added, 1)

        def ahead(h):
            return (1, 0) if h == 0 else (0, 1)

        def turn_onehot(pe, i, h, oh_ready, turned, ohT_ready):
            pe.wait_ge(oh_ready[h], i + 1)
            if later(i) or h:
                pe.wait_ge(ohT_ready, i * 4 + 2 * h)
            for j in range(G):
                ins = nc.tensor.transpose(bank[j // 4][:, (j % 4) * P:(j % 4) * P + P], oh[h][:, j, :], ident[:, :])
                if j % 4 == 3:
                    ins.then_inc(turned, 1)

        def copy_turned(act, i, h, turned, ohT_ready, ohT_used):
            if later(i):
                act.wait_ge(ohT_used[h], i)
            for n in range(2):
                act.wait_ge(turned, i * 4 + 2 * h + n + 1)
                nc.scalar.copy(ohT[h][:, n * 512:n * 512 + 512], bank[n][:, :]).then_inc(ohT_ready, 1)

        def layer0_dst_pass():
            rec_in, oh_ready, ohT_used, scaled, sent, kept = ([sem(f"{n}{h}") for h in range(2)] for n in
                                                              ("rec_in", "oh_ready", "ohT_used", "scaled", "sent", "kept"))
            turned, ohT_ready, picked, psum_free = sem("turned"), sem("ohT_ready"), sem("picked"), sem("psum_free")
            cleared = sem("cleared")
            fields = XI[:, :, :].rearrange("p b f -> p (b f)")[:, 0:NT * 5].rearrange("p (t k) -> p t k", k=5)
            rec_v = rec_d.rearrange("(k p j) w -> k p (j w)", p=P, j=G)
            with nc.Block() as block:
                @block.sync
                def _(sp):
                    def body(i, first):
                        for h in range(2):
                            if not first:
                                sp.wait_ge(kept[h], i)
                            sp.dma_start(recs[h][:, :, :].rearrange("p j w -> p (j w)"),
                                         rec_v[bass.ds(2 * i + h, 1)].rearrange("k p w -> (k p) w")).then_inc(rec_in[h], 16)
                    looped(sp, ITERS, body)

                @block.vector
                def _(dve):
                    def prepare(i, h):
                        t = i * 2 * G + h * G
                        dve.wait_ge(rec_in[h], i * 16 + 16)
                        nc.vector.tensor_copy(fields[:, bass.ds(t, G), :], recs[h][:, :, EA:EA + 5]).then_inc(kept[h], 1)
                        dve.wait_ge(kept[h], i + 1)
                        if later(i):
                            dve.wait_ge(ohT_used[h], i)
                        onehot(h, fields[:, bass.ds(t, G), 0:1]).then_inc(oh_ready[h], 1)

                    def finish(i, h):
                        t = i * 2 * G + h * G
                        if later(i):
                            dve.wait_ge(sent[h], i * (16 * G))
                        nc.vector.tensor_copy(rows[h][:, :, D:D + 1], fields[:, bass.ds(t, G), R_SLOC - EA:R_SLOC - EA + 1]) \
                            .then_inc(scaled[h], 1)
                        nc.vector.tensor_copy(ixr[h][:, :].unsqueeze(2),
                                              fields[:, bass.ds(t, G), R_POS - EA:R_POS - EA + 1]) \
                            .then_inc(scaled[h], 1)
                        for n in range(2):
                            dve.wait_ge(picked, i * 4 + 2 * h + n + 1)
                            nc.vector.tensor_tensor(rows[h][:, 4 * n:4 * n + 4, 0:D],
                                                    bank[2 + n][:, :].rearrange("p (j f) -> p j f", f=D),
                                                    fields[:, bass.ds(t + 4 * n, 4), R_W - EA:R_W - EA + 1].to_broadcast([P, 4, D]),
                                                    ALU.mult).then_inc(scaled[h], 1)
                        dve.wait_ge(scaled[h], i * 4 + 4)
                        dve.sem_inc(psum_free, 1)

                    for h in range(2):
                        nc.vector.memset(rows[h][:, :, D:D + 8], 0.0).then_inc(cleared, 1)
                    nc.vector.memset(one1[:, :], 1.0)
                    dve.wait_ge(cleared, 2)
                    prepare(0, 0)

                    def body(i, last):
                        for h in range(2):
                            nh, step = ahead(h)
                            if not (last and h == 1):
                                prepare(i + step, nh)
                            finish(i, h)
                    body(0, False)
                    with dve.Fori(1, ITERS - 1) as i:
                        body(i, False)
                    body(ITERS - 1, True)
                    for n in range(2):
                        dve.wait_ge(kept[n], ITERS)
                    nc.vector.tensor_copy(dloc[:, 0:NT].unsqueeze(2), fields[:, :, 0:1])
                    nc.vector.tensor_copy(src_ix[:, 0:NT].unsqueeze(2), fields[:, :, 1:2])
                    nc.vector.tensor_tensor(X[:, :, :], X[:, :, :], per_col(bn_shift), ALU.add)

                @block.tensor
                def _(pe):
                    def pick(i, h):
                        at = node_tiles(mybir.EngineType.PE, tile_of_d, i, h)
                        if later(i) or h:
                            pe.wait_ge(psum_free, i * 2 + h)
                        for j in range(G):
                            if j % 4 == 0:
                                pe.wait_ge(ohT_ready, i * 4 + 2 * h + j // 4 + 1)
                            ins = nc.tensor.matmul(bank[2 + j // 4][:, (j % 4) * P:(j % 4) * P + P],
                                                   ohT[h][:, j * P:j * P + P], Hflat[:, bass.ds(at[j] * AW, D)],
                                                   start=True, stop=True)
                            if j % 4 == 3:
                                ins.then_inc(picked, 1)
                        pe.wait_ge(picked, i * 4 + 2 * h + 2)
                        pe.sem_inc(ohT_used[h], 1)

                    turn_onehot(pe, 0, 0, oh_ready, turned, ohT_ready)

                    def body(i, last):
                        for h in range(2):
                            nh, step = ahead(h)
                            if not (last and h == 1):
                                turn_onehot(pe, i + step, nh, oh_ready, turned, ohT_ready)
                            pick(i, h)
                    body(0, False)
                    with pe.Fori(1, ITERS - 1) as i:
                        body(i, False)
                    body(ITERS - 1, True)

                @block.scalar
                def _(act):
                    nc.scalar.copy(ACC[:, :, :], zero1[:, :].unsqueeze(2).to_broadcast([P, NBP, AW]))
                    looped(act, ITERS, lambda i, first: [copy_turned(act, i, h, turned, ohT_ready, ohT_used)
                                                         for h in range(2)])

                @block.gpsimd
                def _(pool):
                    with pool.Fori(0, ITERS) as i:
                        for h in range(2):
                            pool.wait_ge(scaled[h], i * 4 + 4)
                            pool.sem_inc(poolt, 1)
                            for j in range(G):
                                pool.indirect_dma_start(
                                    msg_d, bass.IndirectOffsetOnAxis(ap=ixr[h][:, j:j + 1], axis=0),
                                    rows[h][:, j, 0:MW], None, bounds_check=SLOTS - 1, oob_is_err=False).then_inc(sent[h], 16)
                    for h in range(2):
                        pool.wait_ge(sent[h], 16 * G * ITERS)

        poolt = sem("pool_tick")
        Hflat = sums[1]

        def layer0_src_pass():
            deep, oh_deep = 8, 4
            msg_in, apart, distance, oh_ready, used = ([sem(f"{n}{q}") for q in range(deep)] for n in
                                                       ("msg_in", "apart", "distance", "oh_ready", "used"))
            summed, added, odd_cleared = sem("summed"), sem("added"), sem("odd_cleared")
            msg_v = msg_d.rearrange("(k p j) w -> k p (j w)", p=P, j=G)
            places = [XI[:, :, :].rearrange("p b f -> p (b f)"), edge_buf[:, :]]
            sent_msgs = [t[:, q * G * MW:(q + 1) * G * MW] for t in places for q in range(t.shape[1] // (G * MW))][0:deep]
            by_tile = [m.rearrange("p (j w) -> p j w", w=MW) for m in sent_msgs]
            onehots = [Yflat[:, q % oh_deep * G * P:(q % oh_deep + 1) * G * P].rearrange("p (j n) -> p j n", j=G)
                       for q in range(deep)]
            rounds = ITERS * 2 // deep

            def half_of(i, q):
                return i * (deep // 2) + q // 2, q % 2

            with nc.Block() as block:
                @block.sync
                def _(sp):
                    def body(i, first):
                        for q in range(deep):
                            if not first:
                                sp.wait_ge(used[q], i)
                            sp.dma_start(sent_msgs[q], msg_v[bass.ds(deep * i + q, 1)].rearrange("k p w -> (k p) w")) \
                                .then_inc(msg_in[q], 16)
                    looped(sp, rounds, body)

                @block.gpsimd
                def _(pool):
                    def body(i, first):
                        for q in range(deep):
                            if q >= oh_deep:
                                pool.wait_ge(used[q - oh_deep], i + 1)
                                pool.sem_inc(poolt, 1)
                            elif not first:
                                pool.wait_ge(used[q + deep - oh_deep], i)
                                pool.sem_inc(poolt, 1)
                            pool.wait_ge(msg_in[q], i * 16 + 16)
                            pool.sem_inc(poolt, 1)
                            nc.gpsimd.tensor_tensor(onehots[q], iota_row[:, :].unsqueeze(1).to_broadcast([P, G, P]),
                                                    by_tile[q][:, :, D:D + 1].to_broadcast([P, G, P]), ALU.subtract) \
                                .then_inc(apart[q], 1)
                    looped(pool, rounds, body)

                @block.scalar
                def _(act):
                    def body(i, first):
                        for q in range(deep):
                            act.wait_ge(apart[q], i + 1)
                            nc.scalar.activation(onehots[q], onehots[q], ACT.Abs, bias=zero1[:, :]).then_inc(distance[q], 1)
                            act.wait_ge(distance[q], i + 1)
                            nc.scalar.activation(onehots[q], onehots[q], ACT.Relu, bias=one1[:, :], scale=-1.0) \
                                .then_inc(oh_ready[q], 1)
                    looped(act, rounds, body)

                @block.vector
                def _(dve):
                    nc.vector.memset(H[:, :, :], 0.0).then_inc(odd_cleared, 1)
                    dve.wait_ge(odd_cleared, 1)
                    looped(dve, rounds, lambda i, first: [add_sums(dve, *half_of(i, q), acc_of_s, D, summed, added)
                                                          for q in range(deep)])

                @block.tensor
                def _(pe):
                    def body(i, first):
                        for q in range(deep):
                            pe.wait_ge(oh_ready[q], i + 1)
                            sum_tiles(pe, *half_of(i, q), onehots[q], by_tile[q], D, summed, added, [used[q], used[q]])
                    looped(pe, rounds, body)

        def copy_index(i, h, ix_ready):
            nc.scalar.copy(ixr[h][:, :], src_ix[:, bass.ds(i * 2 * G + h * G, G)]).then_inc(ix_ready[h], 1)

        def gather_rows(pool, i, h, first, table, w, msg_ready, ix_ready, rows_in):
            if not first:
                pool.wait_ge(msg_ready[h], i)
                pool.sem_inc(poolt, 1)
            pool.wait_ge(ix_ready[h], i + 1)
            pool.sem_inc(poolt, 1)
            for j in range(G):
                pool.indirect_dma_start(rows[h][:, j, 0:w], None, table,
                                        bass.IndirectOffsetOnAxis(ap=ixr[h][:, j:j + 1], axis=0)).then_inc(rows_in[h], 16)

        a_dst, den = sb("a_dst", [P, NBP * 8]), sb("den", [P, NBP * 8])
        gmax, gmax_all = sb("gmax", [P, 8]), sb("gmax_all", [P, 8])

        def by_head(t, heads):
            return t[:, 0:NBP * heads].rearrange("p (b k) -> p b k", k=heads)

        def gat_pass(table, heads, meanwhile):
            w, c = D + heads, D // heads
            ad, ps_self, as3 = by_head(a_dst, heads), by_head(den, heads), H[:, :, D:D + heads]
            adc3, rest = (Yflat[:, n * NBP * 16:n * NBP * 16 + NBP * 2 * heads].rearrange("p (b k) -> p b k", k=2 * heads)
                          for n in range(2))
            bound = adc3[:, :, heads:2 * heads]
            parts = adc[:, 0:NBP * 6 * heads].rearrange("p (b t k) -> p b t k", t=3, k=2 * heads)
            maxed, reduced, asked, exped, parts_ready, sums_cleared = (
                sem(n) for n in ("maxed", "reduced", "asked", "exped", "parts_ready", "sums_cleared"))

            def bounds_and_parts(dve, v, then):
                then(v.tensor_reduce(gmax[:, 0:heads], as3.rearrange("p b k -> p k b"), AX.X, ALU.max))
                dve.sem_inc(maxed, 1)
                then(v.tensor_copy(adc3[:, :, 0:heads], ad))
                then(v.tensor_tensor(ps_self, as3, ad, ALU.add))
                then(v.scalar_tensor_tensor(ps_self, ps_self, SLOPE, ps_self, ALU.mult, ALU.max))
                dve.wait_ge(reduced, 1)
                then(v.tensor_tensor(bound, ad, gmax_all[:, 0:heads].unsqueeze(1).to_broadcast([P, NBP, heads]), ALU.add))
                then(v.scalar_tensor_tensor(bound, bound, SLOPE, bound, ALU.mult, ALU.max))
                then(v.tensor_tensor(ps_self, ps_self, bound, ALU.subtract))
                dve.sem_inc(asked, 1)
                then(v.tensor_copy(parts[:, :, 0, :], adc3))
                then(v.tensor_tensor(rest, adc3, parts[:, :, 0, :], ALU.subtract))
                then(v.tensor_copy(parts[:, :, 1, :], rest))
                then(v.tensor_tensor(rest, rest, parts[:, :, 1, :], ALU.subtract))
                then(v.tensor_copy(parts[:, :, 2, :], rest))
                dve.sem_inc(parts_ready, 1)


            def picks(h):
                return bank[2 + h][:, 0:G * 6 * heads]

            rows_in, ix_ready, oh_ready, used, msg_ready, ohb_ready, turned, ohbT_ready, picked = (
                [sem(f"{n}{h}") for h in range(2)] for n in
                ("rows_in", "ix_ready", "oh_ready", "used", "msg_ready", "ohb_ready", "turned", "ohbT_ready", "picked"))
            logits, probs, zst, summed, added, node_steps = (
                sem(n) for n in ("logits", "probs", "zst", "summed", "added", "node_steps"))
            with nc.Block() as block:
                @block.gpsimd
                def _(pool):
                    pool.wait_ge(maxed, 1)
                    pool.partition_all_reduce(gmax_all[:, 0:heads], gmax[:, 0:heads], P, bass.bass_isa.ReduceOp.max) \
                        .then_inc(reduced, 1)
                    looped(pool, ITERS, lambda i, first: [gather_rows(pool, i, h, first, table, w, msg_ready, ix_ready, rows_in)
                                                          for h in range(2)])

                @block.vector
                def _(dve):
                    def prepare(i, h):
                        if later(i):
                            dve.wait_ge(used[h], i)
                        onehot(h, dloc[:, bass.ds(i * 2 * G + h * G, G)].unsqueeze(2)).then_inc(oh_ready[h], 1)

                    then = Steps(dve, node_steps).then
                    bounds_and_parts(dve, nc.vector, then)
                    prepare(0, 0)
                    dve.wait_ge(exped, 1)
                    meanwhile(nc.vector, then)
                    dve.wait_ge(sums_cleared, 1)

                    def body(i, first):
                        for h in range(2):
                            nh, step = ahead(h)
                            dve.wait_ge(rows_in[h], i * (16 * G) + 16 * G)
                            dve.wait_ge(picked[h], i + 1)
                            zz = z[h][:, :, 0:heads]
                            ps = pk[:, :, 0:2 * heads]
                            st = Steps(dve, zst, i * 8 + h * 4)
                            st.then(nc.vector.tensor_reduce(ps, picks(h).rearrange("p (j t k) -> p j k t", j=G, t=3),
                                                            AX.X, ALU.add))
                            st.then(nc.vector.tensor_tensor(zz, rows[h][:, :, D:w], ps[:, :, 0:heads], ALU.add))
                            st.then(nc.vector.scalar_tensor_tensor(zz, zz, SLOPE, zz, ALU.mult, ALU.max))
                            st.then(nc.vector.tensor_tensor(zz, zz, ps[:, :, heads:2 * heads], ALU.subtract))
                            nc.vector.tensor_scalar(zz, zz, 0.0, None, ALU.min).then_inc(logits, 1)
                            prepare(i + step, nh)
                            dve.wait_ge(probs, i * 2 + h + 1)
                            split = "p j (k c) -> p j k c"
                            nc.vector.tensor_tensor(msgs[h][:, :, 0:D].rearrange(split, c=c),
                                                    rows[h][:, :, 0:D].rearrange(split, c=c),
                                                    msgs[h][:, :, D:w].unsqueeze(3).to_broadcast([P, G, heads, c]),
                                                    ALU.mult).then_inc(msg_ready[h], 1)
                            if h or not first:
                                add_sums(dve, *before(i, h), acc_of_d, w, summed, added)
                    looped(dve, ITERS, body)
                    add_sums(dve, ITERS - 1, 1, acc_of_d, w, summed, added)

                @block.scalar
                def _(act):
                    def narrow(i, h):
                        act.wait_ge(oh_ready[h], i + 1)
                        if later(i):
                            act.wait_ge(turned[h], i)
                        nc.scalar.copy(ohb[h], oh[h].rearrange("p j n -> p (j n)")).then_inc(ohb_ready[h], 1)

                    def copy_turned_b(i, h):
                        act.wait_ge(turned[h], i + 1)
                        if later(i):
                            act.wait_ge(picked[h], i)
                        nc.scalar.copy(ohbT[h], bank[h][:, :].bitcast(BF16)).then_inc(ohbT_ready[h], 1)

                    for h in range(2):
                        copy_index(0, h, ix_ready)
                    nc.scalar.copy(ACC[:, :, :], zero1[:, :].unsqueeze(2).to_broadcast([P, NBP, AW])).then_inc(sums_cleared, 1)
                    act.wait_ge(asked, 1)
                    nc.scalar.activation(ps_self, ps_self, ACT.Exp, bias=zero1[:, :]).then_inc(exped, 1)
                    narrow(0, 0)
                    copy_turned_b(0, 0)

                    def body(i, first):
                        for h in range(2):
                            nh, step = ahead(h)
                            act.wait_ge(logits, i * 2 + h + 1)
                            if not first:
                                act.wait_ge(used[h], i)
                            nc.scalar.activation(msgs[h][:, :, D:w], z[h][:, :, 0:heads], ACT.Exp, bias=zero1[:, :]) \
                                .then_inc(probs, 1)
                            copy_index(i + 1, h, ix_ready)
                            narrow(i + step, nh)
                            copy_turned_b(i + step, nh)
                    looped(act, ITERS, body)

                @block.tensor
                def _(pe):
                    def turn(i, h):
                        pe.wait_ge(ohb_ready[h], i + 1)
                        if later(i):
                            pe.wait_ge(ohbT_ready[h], i)
                        tb_ = bank[h][:, :].bitcast(BF16)
                        for j in range(G):
                            ins = nc.tensor.transpose(tb_[:, j * P:(j + 1) * P], ohb[h][:, j * P:(j + 1) * P], ident_b[:, :])
                        ins.then_inc(turned[h], 1)

                    def tiles_of(i, h):
                        return node_tiles(mybir.EngineType.PE, tile_of_d, i, h)

                    def pick(i, h, at):
                        if later(i):
                            pe.wait_ge(msg_ready[h], i)
                        pe.wait_ge(ohbT_ready[h], i + 1)
                        for j in range(G):
                            ins = nc.tensor.matmul(picks(h)[:, j * 6 * heads:(j + 1) * 6 * heads],
                                                   ohbT[h][:, j * P:j * P + P], adc[:, bass.ds(at[j] * (6 * heads), 6 * heads)],
                                                   start=True, stop=True)
                        ins.then_inc(picked[h], 1)

                    turn(0, 0)
                    pe.wait_ge(parts_ready, 1)
                    pick(0, 0, tiles_of(0, 0))

                    def body(i, first):
                        for h in range(2):
                            nh, step = ahead(h)
                            turn(i + step, nh)
                            at = tiles_of(i + step, nh)
                            pe.wait_ge(msg_ready[h], i + 1)
                            sum_tiles(pe, i, h, oh[h], msgs[h], w, summed, added, used,
                                      midway=lambda: pick(i + step, nh, at))
                    looped(pe, ITERS, body)

        def mlp_pass(table, meanwhile):
            w = D + 1
            rec_in, rows_in, ix_ready, oh_ready, used, ones_in, hid_ready = (
                [sem(f"{n}{h}") for h in range(2)] for n in
                ("rec_in", "rows_in", "ix_ready", "oh_ready", "used", "ones_in", "hid_ready"))
            pe_tick, node_steps = sem("pe_tick"), sem("node_steps")
            turned, at_ready, prod, added_rows, summed, added = (
                sem(n) for n in ("turned", "at_ready", "prod", "added_rows", "summed", "added"))
            rec_v = rec_d.rearrange("(k p j) w -> k p (j w)", p=P, j=G)
            with nc.Block() as block:
                @block.gpsimd
                def _(pool):
                    looped(pool, ITERS, lambda i, first: [gather_rows(pool, i, h, first, table, D, hid_ready, ix_ready, rows_in)
                                                          for h in range(2)])

                @block.sync
                def _(sp):
                    def body(i, first):
                        for h in range(2):
                            if not first:
                                sp.wait_ge(turned, i * 4 + 2 * h - 2)
                            sp.dma_start(recs[h][:, :, :].rearrange("p j w -> p (j w)"),
                                         rec_v[bass.ds(2 * i + h, 1)].rearrange("k p w -> (k p) w")).then_inc(rec_in[h], 16)
                    looped(sp, ITERS, body)

                @block.vector
                def _(dve):
                    def prepare(i, h):
                        if later(i):
                            dve.wait_ge(used[h], i)
                        onehot(h, dloc[:, bass.ds(i * 2 * G + h * G, G)].unsqueeze(2)).then_inc(oh_ready[h], 1)

                    def body(i, first):
                        for h in range(2):
                            dve.wait_ge(rows_in[h], i * (16 * G) + 16 * G)
                            for n in range(2):
                                dve.wait_ge(prod, i * 4 + 2 * h + n + 1)
                                hv = rows[h][:, 4 * n:4 * n + 4, 0:D]
                                nc.vector.tensor_tensor(hv, hv, bank[2 + n][:, :].rearrange("p (j f) -> p j f", f=D),
                                                        ALU.add).then_inc(added_rows, 1)
                            if h or not first:
                                add_sums(dve, *before(i, h), acc_of_d, w, summed, added)
                            nh, step = ahead(h)
                            prepare(i + step, nh)
                    for h in range(2):
                        nc.vector.memset(msgs[h][:, :, D:D + 8], 1.0).then_inc(ones_in[h], 1)
                        dve.wait_ge(ones_in[h], 1)
                    prepare(0, 0)
                    meanwhile(nc.vector, Steps(dve, node_steps).then)
                    looped(dve, ITERS, body)
                    add_sums(dve, ITERS - 1, 1, acc_of_d, w, summed, added)

                @block.scalar
                def _(act):
                    def copy_attr(i, h):
                        if later(i) or h:
                            act.wait_ge(prod, i * 4 + 2 * h)
                        for n in range(2):
                            act.wait_ge(turned, i * 4 + 2 * h + n + 1)
                            nc.scalar.copy(ohT[0][0:EA, n * 512:n * 512 + 512], bank[n][0:EA, :]).then_inc(at_ready, 1)

                    for h in range(2):
                        copy_index(0, h, ix_ready)
                    copy_attr(0, 0)

                    def body(i, last):
                        for h in range(2):
                            nh, step = ahead(h)
                            if not (last and h == 1):
                                copy_attr(i + step, nh)
                            act.wait_ge(added_rows, i * 4 + 2 * h + 2)
                            copy_index(i + 1, h, ix_ready)
                            if later(i):
                                act.wait_ge(used[h], i)
                            nc.scalar.activation(msgs[h][:, :, 0:D], rows[h][:, :, 0:D], ACT.Relu, bias=zero1[:, :]) \
                                .then_inc(hid_ready[h], 1)
                    body(0, False)
                    with act.Fori(1, ITERS - 1) as i:
                        body(i, False)
                    body(ITERS - 1, True)

                @block.tensor
                def _(pe):
                    for h in range(2):
                        pe.wait_ge(ones_in[h], 1)

                    def edge_part(i, h):
                        pe.wait_ge(rec_in[h], i * 16 + 16)
                        if later(i) or h:
                            pe.wait_ge(at_ready, i * 4 + 2 * h)
                        pe.sem_inc(pe_tick, 1)
                        for j in range(G):
                            ins = nc.tensor.transpose(bank[j // 4][0:EA, (j % 4) * P:(j % 4) * P + P],
                                                      recs[h][:, j, 0:EA], ident[:, :])
                            if j % 4 == 3:
                                ins.then_inc(turned, 1)
                        if later(i) or h:
                            pe.wait_ge(added_rows, i * 4 + 2 * h)
                        for j in range(G):
                            if j % 4 == 0:
                                pe.wait_ge(at_ready, i * 4 + 2 * h + j // 4 + 1)
                            ins = nc.tensor.matmul(bank[2 + j // 4][:, (j % 4) * P:(j % 4) * P + P],
                                                   ohT[0][0:EA, j * P:j * P + P], wmbT[:, :], start=True, stop=True)
                            if j % 4 == 3:
                                ins.then_inc(prod, 1)

                    edge_part(0, 0)

                    def body(i, last):
                        for h in range(2):
                            nh, step = ahead(h)
                            if not (last and h == 1):
                                edge_part(i + step, nh)
                            pe.wait_ge(oh_ready[h], i + 1)
                            pe.wait_ge(hid_ready[h], i + 1)
                            sum_tiles(pe, i, h, oh[h], msgs[h], w, summed, added, used)
                    body(0, False)
                    with pe.Fori(1, ITERS - 1) as i:
                        body(i, False)
                    body(ITERS - 1, True)

        def gat_product(l, heads, table, addends, normed, before=None):
            ad = by_head(a_dst, heads)
            cols = D + 2 * heads

            def after(v, then, b, rows_psum):
                at = slice(b, b + 2)
                v.tensor_copy(H[:, at, 0:D + heads], rows_psum[:, :, 0:D + heads])
                then(v.tensor_copy(ad[:, at, :], rows_psum[:, :, D + heads:cols]))

            def behind(g):
                for t, row_vec in addends:
                    nc.gpsimd.tensor_tensor(t[:, group(g), :], t[:, group(g), :], columns(row_vec, GN), ALU.add)
            node_product([XI], [wx[l]], after, before, normed, cols=cols, store=(table, H, D + heads), behind=behind)

        def self_loops(v, then, heads):
            ps, h4 = by_head(den, heads), H[:, :, 0:D].rearrange("p b (k c) -> p b k c", k=heads)
            then(v.tensor_tensor(h4, h4, ps.unsqueeze(3).to_broadcast([P, NBP, heads, D // heads]), ALU.mult))
            then(v.tensor_copy(H[:, :, D:D + heads], ps))

        def weights_of_nodes(v, then, heads):
            at = slice(D, D + heads)
            then(v.tensor_tensor(by_head(den, heads), ACC[:, :, at], H[:, :, at], ALU.add))
            if heads == 8:
                then(v.tensor_scalar(by_head(den, heads), by_head(den, heads), 1e-16, None, ALU.add))
            then(v.reciprocal(by_head(den, heads), by_head(den, heads)))

        def rows_of_nodes(v, then, tiles, heads):
            n = tiles.stop - tiles.start
            acc4 = ACC[:, tiles, 0:D].rearrange("p b (k c) -> p b k c", k=heads)
            then(v.tensor_tensor(ACC[:, tiles, 0:D], ACC[:, tiles, 0:D], H[:, tiles, 0:D], ALU.add))
            then(v.tensor_tensor(acc4, acc4, by_head(den, heads)[:, tiles, :].unsqueeze(3)
                                 .to_broadcast([P, n, heads, D // heads]), ALU.mult))

        def scaled(g, f, i):
            for b in range(g * GN, (g + 1) * GN):
                ins = nc.scalar.activation(XI[:, b, :], i[:, b, 0:D], f, bias=shift[:, b:b + 1], scale=var[:, b:b + 1])
            return ins

        def relu_norm_x(g):
            return scaled(g, ACT.Relu, X)

        def norm_into_x(t, gamma):
            norm_done, steps, asked, done = (sem(n) for n in ("norm_done", "steps", "asked", "done"))
            with nc.Block() as block:
                @block.scalar
                def _(act):
                    for g in range(NG):
                        scaled(g, ACT.Identity, t).then_inc(norm_done, 1)
                    act.wait_ge(asked, 1)
                    nc.scalar.activation(var[:, :], var[:, :], ACT.Sqrt, bias=zero1[:, :]).then_inc(done, 1)

                @block.vector
                def _(dve):
                    v, then = nc.vector, Steps(dve, steps).then
                    for g in range(NG):
                        at = group(g)
                        dve.wait_ge(norm_done, g + 1)
                        then(v.tensor_tensor(XI[:, at, :], XI[:, at, :], columns(gamma, GN), ALU.mult))
                        then(v.tensor_tensor(X[:, at, :], X[:, at, :], XI[:, at, :], ALU.add))
                        for b in range(g * GN, (g + 1) * GN):
                            ins = count_stats(v, b, X)
                    then(ins)
                    dve.wait_ge(norm_done, NG)

                    def root(o, i, f):
                        dve.sem_inc(asked, 1)
                        dve.wait_ge(done, 1)
                    finish_stats(v, then, root)

        with stage_of_work():
            layer0_dst_pass()
            layer0_src_pass()

            def sums0(v, then, g):
                then(v.tensor_tensor(ACC[:, group(g), 0:D], ACC[:, group(g), 0:D], H[:, group(g), 0:D], ALU.add))

            def after0(v, then, b, rows_psum):
                at = slice(b, b + 2)
                then(v.tensor_tensor(ACC[:, at, 0:D], rows_psum, columns(bn_scale, 2), ALU.mult))
                then(v.tensor_tensor(X[:, at, :], X[:, at, :], ACC[:, at, 0:D], ALU.add))
                for n in range(2):
                    ins = count_stats(v, b + n, X)
                then(ins)
            softplus_product(ACC, mat["Wi1"][0], bi1_col, mat["Wi2"][0], sums0, after0)
            Dense(lambda d, v, then: finish_stats(v, then, d.root), roots=1)

        def norm_l1(v, then, g):
            at = group(g)
            then(v.tensor_tensor(XI[:, at, :], XI[:, at, :], columns(vec["L1_gnn_gamma", 0][0], GN), ALU.mult))
            then(v.tensor_tensor(XI[:, at, :], XI[:, at, :], columns(vec["L1_gnn_beta", 0][0], GN), ALU.add))

        for l in range(2):
            with stage_of_work():
                addends = [(XI, vec["L1_gnn_bias", l][0])]
                if l == 0:
                    gat_product(0, 1, tab_d[0], addends, relu_norm_x)
                else:
                    addends.append((X, vec["L1_gnn_beta", 1][0]))
                    gat_product(1, 1, tab_d[1], addends, lambda g: scaled(g, ACT.Identity, Y), norm_l1)
                gat_pass(tab_d[l], 1, lambda v, then: self_loops(v, then, 1))
                weights_in_den = sem("weights_in_den")
                cut = NBP - 20
                assert cut % 2 == 0

                def pool1(pool, v, then):
                    tiles = slice(cut, NBP)
                    then(v.tensor_tensor(ACC[:, tiles, 0:D], ACC[:, tiles, 0:D], H[:, tiles, 0:D], ALU.add))
                    pool.wait_ge(weights_in_den, 1)
                    then(v.tensor_tensor(ACC[:, tiles, 0:D], ACC[:, tiles, 0:D],
                                         by_head(den, 1)[:, tiles, :].to_broadcast([P, NBP - cut, D]), ALU.mult))
                    then(v.tensor_tensor(Y[:, tiles, :], ACC[:, tiles, 0:D], XI[:, tiles, :], ALU.add))

                def end1(d, v, then):
                    weights_of_nodes(v, then, 1)
                    d.dve.sem_inc(weights_in_den, 1)
                    then(v.tensor_tensor(ACC[:, 0:cut, 0:D], ACC[:, 0:cut, 0:D], H[:, 0:cut, 0:D], ALU.add))
                    for b in range(cut):
                        ins = v.scalar_tensor_tensor(Y[:, b, :], ACC[:, b, 0:D], den[:, b:b + 1], XI[:, b, :], ALU.mult, ALU.add)
                    then(ins)
                    for b in range(cut):
                        ins = count_stats(v, b, Y)
                    d.wait_pool()
                    for b in range(cut, NBP):
                        ins = count_stats(v, b, Y)
                    then(ins)
                    finish_stats(v, then, d.root)
                Dense(end1, roots=1, on_pool=pool1)
                if l == 1:
                    norm_into_x(Y, vec["L1_gnn_gamma", 1][0])

        with stage_of_work():
            def after_h(v, then, b, rows_psum):
                then(v.tensor_tensor(H[:, b:b + 2, 0:D], rows_psum, columns(cm_row, 2), ALU.add))
                v.memset(ACC[:, b:b + 2, :], 0.0)
                v.tensor_tensor(X[:, b:b + 2, :], X[:, b:b + 2, :], columns(vec["L2_gnn_ln_b"][0], 2), ALU.add)
            node_product([XI], [wmaT], after_h, normed=relu_norm_x, store=(tab_d[2], H, D))

            mlp_pass(tab_d[2], lambda v, then: then(v.memset(H[:, :, :], 0.0)))

            def degree2(d, v, then):
                deg = ACC[:, :, D:D + 1]
                then(v.tensor_tensor(deg, deg, H[:, :, D:D + 1], ALU.add))
                then(v.tensor_scalar(mean[:, :].unsqueeze(2), deg, 1.0, None, ALU.max))
                then(v.reciprocal(mean[:, :], mean[:, :]))
                then(v.tensor_tensor(var[:, :].unsqueeze(2), deg, mean[:, :].unsqueeze(2), ALU.mult))
            Dense(degree2)

            def mean2(v, then, g):
                at = group(g)
                then(v.tensor_tensor(ACC[:, at, 0:D], ACC[:, at, 0:D], H[:, at, 0:D], ALU.add))
                then(v.tensor_tensor(ACC[:, at, 0:D], ACC[:, at, 0:D],
                                     mean[:, at].unsqueeze(2).to_broadcast([P, GN, D]), ALU.mult))

            def after_m(v, then, b, rows_psum):
                for n in range(2):
                    ins = v.scalar_tensor_tensor(Y[:, b + n, :], vec["L2_gnn_bm2"][0][:, :], var[:, b + n:b + n + 1],
                                                 rows_psum[:, n, :], ALU.mult, ALU.add)
                then(ins)
            node_product([ACC], [wm2T], after_m, mean2)

            def after_u(v, then, b, rows_psum):
                at = slice(b, b + 2)
                then(v.tensor_tensor(ACC[:, at, 0:D], rows_psum, columns(vec["L2_gnn_bu2"][0], 2), ALU.add))
                then(v.tensor_tensor(H[:, at, 0:D], ACC[:, at, 0:D], XI[:, at, :], ALU.add))
                for n in range(2):
                    ins = v.bn_stats(stats[:, b + n, :], H[:, b + n, 0:D])
                then(ins)
            node_product([XI, Y], [wuaT, wubT], after_u, w2=wu2T, bias=cu_col)

            Dense(lambda d, v, then: finish_stats(v, then, d.root), roots=1)
            norm_into_x(H, vec["L2_gnn_ln_g"][0])

        with stage_of_work():
            gat_product(2, 8, tab_d[3], [(X, vec["L3_gnn_bias"][0])], relu_norm_x)
            gat_pass(tab_d[3], 8, lambda v, then: self_loops(v, then, 8))

            den_ready, written, steps, pool_steps = (sem(n) for n in ("den_ready", "written", "steps", "pool_steps"))
            parts = [slice(n * GN * 3, (n + 1) * GN * 3) for n in range(3)] + [slice(GN * 9, NBP)]
            part_ready = [sem(f"part_ready{n}") for n in range(4)]

            def finish(engine, v, then, n):
                rows_of_nodes(v, then, parts[n], 8)
                then(v.tensor_tensor(X[:, parts[n], :], X[:, parts[n], :], ACC[:, parts[n], 0:D], ALU.add))
                engine.sem_inc(part_ready[n], 1)

            with nc.Block() as block:
                @block.vector
                def _(dve):
                    then = Steps(dve, steps).then
                    weights_of_nodes(nc.vector, then, 8)
                    dve.sem_inc(den_ready, 1)
                    for n in range(3):
                        finish(dve, nc.vector, then, n)

                @block.gpsimd
                def _(pool):
                    pool.wait_ge(den_ready, 1)
                    finish(pool, nc.gpsimd, Steps(pool, pool_steps).then, 3)

                @block.sync
                def _(sp):
                    for n, tiles in enumerate(parts):
                        whole = min(tiles.stop, FULL)
                        sp.wait_ge(part_ready[n], 1)
                        sp.dma_start(out[tiles.start * P:whole * P, :].rearrange("(b p) f -> p b f", p=P),
                                     X[:, tiles.start:whole, :]).then_inc(written, 16)
                    sp.dma_start(out[FULL * P:N, :], X[0:REST, FULL, :]).then_inc(written, 16)
                    sp.wait_ge(written, 16 * (len(parts) + 1))


def kernel(**inputs):
    import numpy as _np
    import concourse.bacc as _bacc
    from concourse import mybir as _mybir
    from concourse.bass_utils import run_bass_kernel_spmd as _run

    nc = _bacc.Bacc("TRN2", target_bir_lowering=False, num_devices=1)
    arrays, args = {}, {}
    for name, value in inputs.items():
        if name == "edge_weight1":
            continue
        v = _np.ascontiguousarray(value)
        arrays[f"in_{name}_dram"] = v
        args[name] = nc.dram_tensor(f"in_{name}_dram", v.shape, _mybir.dt.from_np(v.dtype), kind="ExternalInput").ap()
    out = nc.dram_tensor("out_0_dram", (N, D), F32, kind="ExternalOutput").ap()
    gnn(nc, args, out)
    r = _run(nc, [arrays], core_ids=[0])
    return r.results[0]["out_0_dram"]
```
